# Optimizing a Trainium2 kernel written in Bass

```python
import numpy as np
import jax
import jax.numpy as jnp

def _softmax(x, axis=-1):
    return jax.nn.softmax(x, axis=axis)

def _gelu(x):
    return jax.nn.gelu(x, approximate=True)

def _silu(x):
    return jax.nn.silu(x)

def _sigmoid(x):
    return jax.nn.sigmoid(x)

def _layernorm(x, axis=-1, eps=1e-05):
    m = jnp.mean(x, axis=axis, keepdims=True)
    v = jnp.var(x, axis=axis, keepdims=True)
    return (x - m) / jnp.sqrt(v + eps)

def _scatter_add(tgt, idx, src, axis=0):
    return tgt.at[idx].add(src)

def _segment_sum(src, seg, n):
    return jax.ops.segment_sum(src, seg, n)
kernel_name = 'mk_adaln_d1_jaxref_r8_41a9a2'

def setup_inputs(seed: int=0):
    np.random.seed(seed)
    _w = jnp.asarray

    def _L0_attn_setup():
        import jax, jax.numpy as jnp
        import numpy as np
        NUM_HEADS = 16
        key = jax.random.key(seed)
        k1, k2, k3 = jax.random.split(key, 3)
        B, S, H = (2, 256, 256)
        x = jax.random.normal(k1, (B, S, H), dtype=jnp.float32)
        lim_qkv = (6.0 / (H + 3 * H)) ** 0.5
        lim_out = (6.0 / (H + H)) ** 0.5
        Wqkv = jax.random.uniform(k2, (3 * H, H), jnp.float32, -lim_qkv, lim_qkv)
        bqkv = jnp.zeros((3 * H,), jnp.float32)
        Wout = jax.random.uniform(k3, (H, H), jnp.float32, -lim_out, lim_out)
        bout = jnp.zeros((H,), jnp.float32)
        return {'x': x, 'Wqkv': Wqkv, 'bqkv': bqkv, 'Wout': Wout, 'bout': bout}
    _L0_attn_in = _L0_attn_setup()

    def _L0_ffn_setup():
        import jax, jax.numpy as jnp
        import numpy as np
        E, H, I = (8, 256, 512)
        TOP_K = 1
        B, S = (1, 256)
        key = jax.random.key(seed)
        ks = jax.random.split(key, 7)
        std = 0.02
        return {'hidden_states': jax.random.normal(ks[0], (B, S, H), dtype=jnp.float32), 'router_w': jax.random.normal(ks[1], (E, H), dtype=jnp.float32) * std, 'gate_up_proj': jax.random.normal(ks[2], (E, H, 2 * I), dtype=jnp.float32) * std, 'down_proj': jax.random.normal(ks[3], (E, I, H), dtype=jnp.float32) * std, 'shared_gate_w': jax.random.normal(ks[4], (H, I), dtype=jnp.float32) * std, 'shared_up_w': jax.random.normal(ks[5], (H, I), dtype=jnp.float32) * std, 'shared_down_w': jax.random.normal(ks[6], (I, H), dtype=jnp.float32) * std}
    _L0_ffn_in = _L0_ffn_setup()
    _L0_c = _w((lambda *s: np.random.randn(*s).astype(np.float32) * 0.05)(4, 256))
    _L0_wmod = _w((lambda *s: np.random.randn(*s).astype(np.float32) * 0.05)(256, 6 * 256) * 256 ** (-0.5))
    _d = {'L0_attn_x': _L0_attn_in['x'], 'L0_attn_Wqkv': _L0_attn_in['Wqkv'], 'L0_attn_bqkv': _L0_attn_in['bqkv'], 'L0_attn_Wout': _L0_attn_in['Wout'], 'L0_attn_bout': _L0_attn_in['bout'], 'L0_ffn_router_w': _L0_ffn_in['router_w'], 'L0_ffn_gate_up_proj': _L0_ffn_in['gate_up_proj'], 'L0_ffn_down_proj': _L0_ffn_in['down_proj'], 'L0_ffn_shared_gate_w': _L0_ffn_in['shared_gate_w'], 'L0_ffn_shared_up_w': _L0_ffn_in['shared_up_w'], 'L0_ffn_shared_down_w': _L0_ffn_in['shared_down_w'], 'L0_c': _L0_c, 'L0_wmod': _L0_wmod}
    _x0 = _d['L0_attn_x']
    _d['L0_attn_x'] = jax.random.normal(jax.random.fold_in(jax.random.key(seed), 1), (4, 512, 256), dtype=_x0.dtype)
    del _x0
    return _d

def reference(L0_attn_x, L0_attn_Wqkv, L0_attn_bqkv, L0_attn_Wout, L0_attn_bout, L0_ffn_router_w, L0_ffn_gate_up_proj, L0_ffn_down_proj, L0_ffn_shared_gate_w, L0_ffn_shared_up_w, L0_ffn_shared_down_w, L0_c, L0_wmod):

    def _L0_attn_ref(x, Wqkv, bqkv, Wout, bout):
        import jax, jax.numpy as jnp
        import numpy as np
        NUM_HEADS = 16
        B, S, H = x.shape
        nh = NUM_HEADS
        hd = H // nh
        qkv = jnp.einsum('bsh,oh->bso', x, Wqkv) + bqkv
        q, k, v = jnp.split(qkv, 3, axis=-1)
        q = q.reshape(B, S, nh, hd).transpose(0, 2, 1, 3)
        k = k.reshape(B, S, nh, hd).transpose(0, 2, 1, 3)
        v = v.reshape(B, S, nh, hd).transpose(0, 2, 1, 3)
        scale = hd ** (-0.5)
        scores = jnp.einsum('bhqd,bhkd->bhqk', q, k) * scale
        causal = jnp.triu(jnp.ones((S, S), dtype=bool), k=1)
        scores = jnp.where(causal, -jnp.inf, scores)
        attn = jax.nn.softmax(scores, axis=-1)
        out = jnp.einsum('bhqk,bhkd->bhqd', attn, v)
        out = out.transpose(0, 2, 1, 3).reshape(B, S, H)
        return jnp.einsum('bsh,oh->bso', out, Wout) + bout

    def _L0_ffn_ref(hidden_states, router_w, gate_up_proj, down_proj, shared_gate_w, shared_up_w, shared_down_w):
        import jax, jax.numpy as jnp
        import numpy as np
        E, H, I = (8, 256, 512)
        TOP_K = 1
        B, S = (1, 256)
        orig_shape = hidden_states.shape
        x = hidden_states.reshape(-1, H)
        T = x.shape[0]
        logits = x @ router_w.T
        top_vals, top_idx = jax.lax.top_k(logits, TOP_K)
        scores = jnp.full_like(logits, -jnp.inf)
        scores = scores.at[jnp.arange(T)[:, None], top_idx].set(top_vals)
        scores = jax.nn.sigmoid(scores.astype(jnp.float32)).astype(logits.dtype)
        xr = x[None, :, :] * scores.T[:, :, None]
        gate_up = jnp.einsum('eth,ehf->etf', xr, gate_up_proj)
        gate, up = jnp.split(gate_up, 2, axis=-1)
        routed = jnp.einsum('etf,efh->eth', up * jax.nn.silu(gate), down_proj)
        routed_sum = routed.sum(axis=0)
        shared = jax.nn.silu(x @ shared_gate_w) * (x @ shared_up_w) @ shared_down_w
        return (shared + routed_sum).reshape(orig_shape)
    x = L0_attn_x
    mod = (_silu(L0_c) @ L0_wmod).reshape(L0_c.shape[0], 6, 1, -1)
    sa, ca, ga, sb, cb, gb = (mod[:, 0], mod[:, 1], mod[:, 2], mod[:, 3], mod[:, 4], mod[:, 5])
    ga = (2 * (ga >= 0) - 1) * jnp.maximum(jnp.abs(ga), 0.25)
    gb = (2 * (gb >= 0) - 1) * jnp.maximum(jnp.abs(gb), 0.25)
    h = _layernorm(x, axis=-1) * (1 + ca) + sa
    x = x + ga * _L0_attn_ref(h, L0_attn_Wqkv, L0_attn_bqkv, L0_attn_Wout, L0_attn_bout)
    h = _layernorm(x, axis=-1) * (1 + cb) + sb
    x = x + gb * _L0_ffn_ref(h, L0_ffn_router_w, L0_ffn_gate_up_proj, L0_ffn_down_proj, L0_ffn_shared_gate_w, L0_ffn_shared_up_w, L0_ffn_shared_down_w)
    return x

_drawn_inputs = setup_inputs


def setup_inputs(seed=0):
    import zlib

    import numpy as np

    out = dict(_drawn_inputs(seed))
    spreads = {'L0_attn_bqkv': (0.0, 0.309), 'L0_attn_bout': (0.0, 0.332)}
    factors = {'L0_ffn_router_w': 8.0,
     'L0_ffn_gate_up_proj': 8.0,
     'L0_ffn_down_proj': 8.0,
     'L0_ffn_shared_gate_w': 8.0,
     'L0_ffn_shared_up_w': 8.0,
     'L0_ffn_shared_down_w': 8.0}
    for name, (base, spread) in spreads.items():
        noise = np.random.default_rng([zlib.crc32(name.encode()), seed]).standard_normal(out[name].shape)
        drawn = base * np.exp(spread * noise) if base else spread * noise
        out[name] = jnp.asarray(drawn.astype(out[name].dtype))
    for name, factor in factors.items():
        out[name] = (out[name] * factor).astype(out[name].dtype)
    return out
```

```python
import numpy as np
import concourse.bass as bass
from concourse import mybir
from contextlib import ExitStack

F32, F16, BF16, I32 = mybir.dt.float32, mybir.dt.float16, mybir.dt.bfloat16, mybir.dt.int32
U32 = mybir.dt.uint32
ALU = mybir.AluOpType
ACT = mybir.ActivationFunctionType
AX = mybir.AxisListType

P = 128
B, S, H = 4, 512, 256
NH, HD = 16, 16
E, I = 8, 512
TT = S // P
NT = B * TT
KC = H // P
FC = I // P
RT = NT + E - 1
WS = 64.0
EPS = 1e-5
WE = KC * 2 * I + FC * H
WX = 2 * WE
ROW = 520
OOB = 1 << 20
NEG = -1e30
UNITS = 11
CUM = [4, 8, 10, 11]
STEP = 1024
NG = 4


def group_heads(g):
    return 64 * (g // 2), 4 * (g % 2)


def query_units():
    return [(0, 0, 4), (1, 0, 2), (1, 2, 2)] + [(t, i, 1) for t in (2, 3) for i in range(4)]


def key_units():
    return [(0, i, 1) for i in range(4)] + [(1, i, 1) for i in range(4)] + [(2, 0, 2), (2, 2, 2), (3, 0, 4)]


def build(nc, x, wqkvT, bqkv, bqkc, woutT, bout, rwT, gup, down, sgw, suw, sdw, cT, wmod, out):
    ctx = ExitStack()
    with ctx:
        def sb(name, shape, dt=F32):
            return ctx.enter_context(nc.sbuf_tensor(name, shape, dt))

        def sem(name):
            return ctx.enter_context(nc.semaphore(name))

        qk_d = nc.dram_tensor("qk_d", [2, 4, H, S], F16).ap()
        ng_d = nc.dram_tensor("ng_d", [2, 64, 2, P], F16).ap()
        mod_d = nc.dram_tensor("mod_d", [B, 4 * H], F32).ap()
        gb_d = nc.dram_tensor("gb_d", [B, H], F32).ap()
        xs_d = nc.dram_tensor("xs_d", [RT * P, ROW // 2], U32).ap()

        W = sb("W", [P, (E + 1) * WX], F16)
        x_sb = sb("x_sb", [P, NT, H])
        row = sb("row", [P, NT, ROW], F16)
        row32 = row[:, :, :].bitcast(F32)
        h2T = sb("h2T", [P, 2, KC, B * S], F16)
        stage = sb("stage", [P, 3, STEP])
        ffn = sb("ffn", [P, 5120])
        gbb = sb("gbb", [P, B, H])
        ident = sb("ident", [P, P])
        ident16 = sb("ident16", [P, P], F16)
        identb = sb("identb", [P, P], BF16)
        maskb = sb("maskb", [P, P], BF16)
        tri16 = sb("tri16", [P, P], F16)
        ones16 = sb("ones16", [P, P], F16)
        neghalf = sb("neghalf", [P, TT])
        iw_i = sb("iw_i", [P, E], I32)
        ij_i = sb("ij_i", [P, NT], I32)
        it_i = sb("it_i", [P, RT], I32)
        iw = sb("iw", [P, E])
        ij = sb("ij", [P, NT])
        it = sb("it", [P, RT])
        cs = sb("cs", [P, 2, KC, B])
        sac = sb("sac", [P, KC, B])
        cac = sb("cac", [P, KC, B])
        bqk = sb("bqk", [P, 4])
        st1 = sb("st1", [P, NT, 6])
        mv1 = sb("mv1", [P, NT, 2])
        ve1 = sb("ve1", [P, NT])
        rs1 = sb("rs1", [P, NT])
        st2 = sb("st2", [P, NT, 6])
        mv2 = sb("mv2", [P, NT, 2])
        ve2 = sb("ve2", [P, NT])
        rs2 = sb("rs2", [P, NT])
        rw_s = sb("rw_s", [P, KC, E])
        rw16 = sb("rw16", [P, 2, KC, E], F16)
        lg = sb("lg", [P, NT, E])
        mx = sb("mx", [P, 2, 64])
        negm = sb("negm", [64, 2, P], F16)
        rec = sb("rec", [P, 2, NH])
        top = sb("top", [P, NT])
        oh = sb("oh", [P, NT, E])
        ohw = sb("ohw", [P, NT, E])
        wtop = sb("wtop", [P, NT])
        oh16 = sb("oh16", [P, NT, E], F16)
        cmpc = sb("cmpc", [P, E, NT])
        ntile = sb("ntile", [P, E])
        onesE = sb("onesE", [P, E])
        ends = sb("ends", [P, E])
        base = sb("base", [P, E])
        posf = sb("posf", [P, NT, E])
        posr = sb("posr", [P, NT])
        pos_i = sb("pos_i", [P, NT], I32)
        tec = sb("tec", [P, RT, E])
        tef = sb("tef", [P, RT])
        te_i = sb("te_i", [P, RT], I32)
        srow = sb("srow", [P, NT])
        rb = sb("rb", [P, 3, ROW], F16)
        rb32 = rb[:, :, :].bitcast(F32)
        gbr = sb("gbr", [P, 2, H])
        fill = gbr[:, :, :].rearrange("p r n -> p (r n)").bitcast(F16)[:, 0:ROW]

        at = [0]

        def early(cols, dt=F32):
            n = cols * (2 if dt == F32 else 1)
            v = W[:, at[0]:at[0] + n]
            at[0] += n
            return v.bitcast(F32) if dt == F32 else v

        wq16 = early(2 * KC * 3 * H, F16).rearrange("p (s k n) -> p s k n", s=2, k=KC)
        wo16 = early(2 * KC * H, F16).rearrange("p (s k n) -> p s k n", s=2, k=KC)
        xn = early(TT * H).rearrange("p (t n) -> p t n", t=TT)
        h1 = early(2 * KC * S, F16).rearrange("p (s k n) -> p s k n", s=2, k=KC)
        h32 = early(KC * S).rearrange("p (k n) -> p k n", k=KC)
        q32 = h32
        bvb = early(H)
        boutb = early(H)
        qk16 = early(4 * 2 * S, F16).rearrange("p (a c n) -> p a c n", a=4, c=2)
        stk = early(2 * 2 * 8 * S, F16).rearrange("p (r a h n) -> p r a h n", r=2, a=2, h=8)
        v1 = early(2 * (TT * NH * 17 + 16)).rearrange("p (r n) -> p r n", r=2)
        OTs = early(2 * S).rearrange("p (r n) -> p r n", r=2)
        an = early(TT * H).rearrange("p (t n) -> p t n", t=TT)
        aT = early(2 * KC * S, F16).rearrange("p (s k n) -> p s k n", s=2, k=KC)
        bc = early(2 * 3 * H).rearrange("p (r n) -> p r n", r=2)
        bga = early(H)
        o1 = early(TT * H).rearrange("p (t n) -> p t n", t=TT)
        h2f = o1
        assert at[0] <= E * WX, (at[0], E*WX)
        pt_at = [0, 4 * 512, 4 * 896, 4 * 1152]
        PT = [ffn[:, pt_at[j]:pt_at[j] + 4 * (S - P * j)].rearrange("p (i n) -> p i n", i=4)
              for j in range(TT)]
        wm = stage[:, :, :].rearrange("p a b -> p (a b)").rearrange("p (k n) -> p k n", k=KC)
        hs = h2T[:, :, :, :].rearrange("p a b c -> p (a b c)").bitcast(F32)
        wq_s = hs[:, 0:KC * 3 * H].rearrange("p (k n) -> p k n", k=KC)
        wo_s = hs[:, KC * 3 * H:KC * 4 * H].rearrange("p (k n) -> p k n", k=KC)
        m4 = hs[0:B, KC * 4 * H:KC * 4 * H + 4 * H]
        m4t = hs[0:B, KC * 6 * H:KC * 6 * H + 4 * H]
        g32 = ffn[:, 0:2 * I].rearrange("p (r n) -> p r n", r=2)
        hid = ffn[:, 2 * I:4 * I].rearrange("p (r n) -> p r n", r=2)
        hT = ffn[:, 4 * I:8 * I].bitcast(F16).rearrange("p (s f n) -> p s f n", s=2, f=FC)
        xT = ffn[:, 8 * I:9 * I].bitcast(F16).rearrange("p (r n) -> p r n", r=2)
        yo = ffn[:, 9 * I:10 * I].rearrange("p (r n) -> p r n", r=2)
        rhT = hT.rearrange("p s f n -> p (s f n)").rearrange("p (r s f n) -> p r s f n", r=4, s=2, f=FC)[:, 0:2]

        bank = [ctx.enter_context(nc.psum_tensor(f"bank{i}", [P, 512], F32)) for i in range(8)]
        S0, S1, T0, T1, T2, OTb, M0, M1 = bank
        SB, TB, MB = [S0, S1], [T0, T1, T2], [M0, M1]

        s_const = sem("s_const")
        s_c = sem("s_c")
        s_wm = sem("s_wm")
        s_wq = sem("s_wq")
        s_wo = sem("s_wo")
        s_bias = sem("s_bias")
        s_x = [sem(f"s_xin{b}") for b in range(B)]
        s_sc = sem("s_sc")
        s_mp = sem("s_mp")
        s_m4 = sem("s_m4")
        s_md = sem("s_md")
        s_bc = [sem(f"s_bc{r}") for r in range(2)]
        s_gbb = sem("s_gbb")
        s_wh = sem("s_wh")
        s_wl = sem("s_wl")
        s_mv = sem("s_mv")
        s_rstd = sem("s_rstd")
        s_xn = sem("s_xn")
        s_xt = sem("s_xt")
        s_h1h = sem("s_h1h")
        s_h32 = sem("s_h32")
        s_h1l = sem("s_h1l")
        s_qkv = sem("s_qkv")
        s_qh = sem("s_qh")
        s_q32 = sem("s_q32")
        s_ql = sem("s_ql")
        s_v = sem("s_v")
        s_xb = sem("s_xb")
        s_qkw = [sem(f"s_qkw{r}") for r in range(2)]
        s_stk = [sem(f"s_stk{r}") for r in range(2)]
        s_s1 = sem("s_s1")
        s_mx = sem("s_mx")
        s_mt = sem("s_mt")
        s_neg = sem("s_neg")
        s_ngw = sem("s_ngw")
        s_ng = [sem(f"s_ng{r}") for r in range(2)]
        s_st = sem("s_st")
        s_exp = sem("s_exp")
        s_msk = sem("s_msk")
        s_pv = sem("s_pv")
        s_ote = sem("s_ote")
        s_rt = sem("s_rt")
        s_nrm = sem("s_nrm")
        s_at = sem("s_at")
        s_ath = sem("s_ath")
        s_atl = sem("s_atl")
        s_o = sem("s_o")
        s_x2 = sem("s_x2")
        s_mv2 = sem("s_mv2")
        s_rstd2 = sem("s_rstd2")
        s_hm = sem("s_hm")
        s_h2 = sem("s_h2")
        s_rh = sem("s_rh")
        s_rl = sem("s_rl")
        s_ht = sem("s_ht")
        s_hta = sem("s_hta")
        s_htd = sem("s_htd")
        s_r = sem("s_r")
        s_lg = sem("s_lg")
        s_dv = sem("s_dv")
        s_po = sem("s_po")
        s_eld = [sem(f"s_eld{r}") for r in range(3)]
        s_eh = sem("s_eh")
        s_el = sem("s_el")
        s_g = sem("s_g")
        s_u = sem("s_u")
        s_silu = sem("s_silu")
        s_hid = sem("s_hid")
        s_hh = sem("s_hh")
        s_hl = sem("s_hl")
        s_y = sem("s_y")
        s_ye = sem("s_ye")
        s_x3 = sem("s_x3")
        s_out = sem("s_out")
        s_fill = sem("s_fill")
        s_oh = sem("s_oh")
        s_rank = sem("s_rank")
        s_pos = sem("s_pos")
        s_te = sem("s_te")
        s_top = sem("s_top")
        s_sg = sem("s_sg")
        s_srow = sem("s_srow")
        s_sct = sem("s_sct")
        s_ld = [sem(f"s_ld{r}") for r in range(3)]
        s_gbr = [sem(f"s_gbr{r}") for r in range(2)]
        s_rxt = sem("s_rxt")
        s_rxe = sem("s_rxe")
        s_rg = sem("s_rg")
        s_ru = sem("s_ru")
        s_rsilu = sem("s_rsilu")
        s_rhid = sem("s_rhid")
        s_rht = sem("s_rht")
        s_rhh = sem("s_rhh")
        s_rhl = sem("s_rhl")
        s_ry = sem("s_ry")
        s_rye = sem("s_rye")
        s_add = sem("s_add")

        QU, KU = query_units(), key_units()

        def last_p(b):
            return min(b + 1, B - 1)

        unit_list = [(E, u) for u in range(3)] + [(e, u) for e in range(E) for u in range(3)]
        NU = len(unit_list)
        gu_v = gup.rearrange("e (k p) n -> e k p n", p=P)
        dn_v = down.rearrange("e (f p) n -> e p f n", p=P)

        block = ctx.enter_context(nc.Block())

        @block.sync
        def _(sp):
            sp.dma_start(cs[:, 0], cT.rearrange("(k p) b -> p k b", p=P)).then_inc(s_c, 16)
            sp.dma_start(x_sb[:, 0:TT, :], x[0].rearrange("(t p) n -> p t n", p=P)).then_inc(s_x[0], 16)
            sp.dma_start(wm, wmod.rearrange("(k p) n -> p k n", p=P)).then_inc(s_wm, 16)
            sp.dma_start(wq_s, wqkvT.rearrange("(k p) n -> p k n", p=P)).then_inc(s_wq, 16)
            sp.dma_start(bqk[:, :], bqkc).then_inc(s_bias, 16)
            sp.dma_start(bvb, bqkv[2 * H:3 * H].partition_broadcast(P)).then_inc(s_bias, 16)
            sp.dma_start(boutb, bout.partition_broadcast(P)).then_inc(s_bias, 16)
            sp.dma_start(wo_s, woutT.rearrange("(k p) n -> p k n", p=P)).then_inc(s_wo, 16)
            sp.dma_start(rw_s[:, :, :], rwT.rearrange("(k p) n -> p k n", p=P)).then_inc(s_wo, 16)
            for b in range(1, B):
                sp.dma_start(x_sb[:, TT * b:TT * (b + 1), :],
                             x[b].rearrange("(t p) n -> p t n", p=P)).then_inc(s_x[b], 16)
            sp.wait_ge(s_const, 2)
            sp.dma_start(xs_d.rearrange("(n p) w -> p n w", p=P),
                         fill.bitcast(U32).unsqueeze(1).to_broadcast([P, RT, ROW // 2])).then_inc(s_fill, 16)

            def stacks(b):
                r = b % 2
                sp.wait_ge(s_ql, 4 * (b + 1))
                if b >= 2:
                    sp.wait_ge(s_pv, 16 * (b - 1))
                sp.dma_start(qk_d[r].rearrange("a (c p) n -> p (a c) n", p=P),
                             qk16.rearrange("p a c n -> p (a c) n")).then_inc(s_qkw[r], 16)
                sp.wait_ge(s_qkw[r], 16 * (b // 2 + 1))
                for par in range(2):
                    for a, parts in enumerate(((0, 0, 1), (2, 3, 2))):
                        for j, part in enumerate(parts):
                            src = qk_d[r, part].rearrange("(h two d) n -> two d h n", two=2, d=HD)
                            q0 = 64 * par + HD * j
                            sp.dma_start(stk[q0:q0 + HD, r, a], src[par]).then_inc(s_stk[r], 16)

            def mod_rows(b):
                r = b % 2
                if b >= 2:
                    sp.wait_ge(s_h2, TT * (b - 1))
                sp.dma_start(bc[:, r, :], mod_d[b, 0:3 * H].partition_broadcast(P)).then_inc(s_bc[r], 16)

            def maxima(b):
                r = b % 2
                sp.wait_ge(s_neg, b + 1)
                sp.dma_start(ng_d[r], negm[:, :, :]).then_inc(s_ngw, 16)
                sp.wait_ge(s_ngw, 16 * (b + 1))
                src = ng_d[r].rearrange("(t two h) s q -> two s t h q", t=TT, two=2)
                for par in range(2):
                    for t in range(TT):
                        sp.dma_start(stk[64 * par + 48:64 * par + 50, r, 0, :, P * t:P * (t + 1)],
                                     src[par, :, t]).then_inc(s_ng[r], 16)

            def expert_load(n):
                e, u = unit_list[n]
                if n == 0:
                    sp.wait_ge(s_mp, 1)
                if n >= 3:
                    sp.wait_ge(s_el, n - 2)
                dst = stage[:, n % 3, :]
                s = s_eld[n % 3]
                if e == E:
                    if u < 2:
                        sp.dma_start(dst[:, 0:I], sgw[u * P:(u + 1) * P, :]).then_inc(s, 16)
                        sp.dma_start(dst[:, I:2 * I], suw[u * P:(u + 1) * P, :]).then_inc(s, 16)
                    else:
                        sp.dma_start(dst.rearrange("p (f n) -> p f n", f=FC),
                                     sdw.rearrange("(f p) n -> p f n", p=P)).then_inc(s, 32)
                elif u < 2:
                    sp.dma_start(dst, gu_v[e, u]).then_inc(s, 32)
                else:
                    sp.dma_start(dst.rearrange("p (f n) -> p f n", f=FC), dn_v[e]).then_inc(s, 32)

            sp.wait_ge(s_m4, 1)
            sp.dma_start(mod_d[:, :], m4[:, :]).then_inc(s_md, 16)
            sp.dma_start(gb_d[:, :], m4[:, 3 * H:4 * H]).then_inc(s_md, 16)
            sp.wait_ge(s_md, 32)
            mod_rows(0)
            mod_rows(1)
            sp.dma_start(gbb[:, :, :], mod_d[:, 3 * H:4 * H].partition_broadcast(P)).then_inc(s_gbb, 16)
            stacks(0)
            for n in range(3):
                expert_load(n)
            stacks(1)
            maxima(0)
            for b in range(B):
                if b + 1 < B:
                    maxima(b + 1)
                if b + 2 < B:
                    stacks(b + 2)
                    mod_rows(b + 2)
            for n in range(3, 6):
                expert_load(n)
            loaded = 6
            for b in range(B):
                while loaded < min(NU, 3 + 8 * (b + 1) + 3):
                    expert_load(loaded)
                    loaded += 1
                sp.wait_ge(s_x3, TT * (b + 1))
                sp.dma_start(out[b].rearrange("(t p) n -> p t n", p=P),
                             x_sb[:, TT * b:TT * (b + 1), :]).then_inc(s_out, 16)
            for r in range(RT):
                if r == 0:
                    sp.wait_ge(s_sct, 16 * NT)
                if r >= 3:
                    sp.wait_ge(s_rsilu, r - 2)
                    sp.wait_ge(s_rxt, r - 2)
                    sp.wait_ge(s_add, 16 * (r - 2))
                sp.dma_start(rb[:, r % 3, :].bitcast(U32), xs_d[P * r:P * (r + 1), :]).then_inc(s_ld[r % 3], 16)

        @block.gpsimd
        def _(po):
            g = nc.gpsimd
            n_po = [0]

            def link(ins):
                n_po[0] += 1
                ins.then_inc(s_po, 1)
                po.wait_ge(s_po, n_po[0])

            link(g.memset(fill, 0.0))
            g.memset(fill[:, 514:516].bitcast(I32), OOB).then_inc(s_const, 1)
            link(g.memset(ident[:, :], 0.0))
            link(g.affine_select(out=ident[:, :], in_=ident[:, :], compare_op=ALU.not_equal, fill=1.0,
                                 base=0, pattern=[[-1, P]], channel_multiplier=1))
            g.tensor_copy(ident16[:, :], ident[:, :])
            g.memset(neghalf[:, :], -0.5).then_inc(s_const, 1)
            link(g.tensor_copy(identb[:, :], ident[:, :]))
            link(g.memset(maskb[:, :], 0.0))
            link(g.affine_select(out=maskb[:, :], in_=maskb[:, :], compare_op=ALU.is_ge, fill=NEG,
                                 base=0, pattern=[[-1, P]], channel_multiplier=1))
            link(g.memset(stk[32:64, :, 1], 1.0))
            link(g.memset(stk[96:128, :, 1], 1.0))
            g.memset(v1[:, :, :], 1.0).then_inc(s_const, 1)
            g.memset(ones16[:, :], 1.0)
            g.memset(onesE[:, :], 1.0)
            link(g.memset(tri16[:, :], 1.0))
            g.affine_select(out=tri16[:, :], in_=tri16[:, :], compare_op=ALU.is_ge, fill=0.0,
                            base=-1, pattern=[[1, P]], channel_multiplier=-1)
            g.iota(iw_i[:, :], pattern=[[-1, E]], base=E, channel_multiplier=0)
            g.iota(ij_i[:, :], pattern=[[P, NT]], base=0, channel_multiplier=0)
            link(g.iota(it_i[:, :], pattern=[[1, RT]], base=0, channel_multiplier=0))
            g.tensor_copy(iw[:, :], iw_i[:, :])
            g.tensor_copy(ij[:, :], ij_i[:, :])
            g.tensor_copy(it[:, :], it_i[:, :])
            g.iota(row32[:, :, 257].bitcast(I32), pattern=[[P, NT]], base=0, channel_multiplier=1)
            g.iota(row32[:, :, 258].bitcast(I32), pattern=[[1, B], [0, TT]], base=0, channel_multiplier=0)
            g.memset(row32[:, :, 259], 0.0).then_inc(s_const, 1)

            def rstd(ve, mv, rs, b, ready, done):
                c = slice(TT * b, TT * (b + 1))
                po.wait_ge(ready, b + 1)
                link(g.tensor_scalar(ve[:, c], mv[:, c, 1], EPS, 0.0, ALU.add, ALU.add))
                g.tensor_tensor(rs[:, c], ve[:, c], neghalf[:, :], ALU.pow).then_inc(done, 1)

            def project(b):
                rstd(ve1, mv1, rs1, b, s_mv, s_rstd)
                for k in range(KC):
                    po.wait_ge(s_h32, KC * b + k + 1)
                    if b and k == 0:
                        po.wait_ge(s_qkv, 6 * b)
                    g.tensor_tensor(h1[:, 1, k], h32[:, k], h1[:, 0, k], ALU.subtract).then_inc(s_h1l, 1)
                for u in range(4):
                    po.wait_ge(s_q32, 4 * b + u + 1)
                    if b and u == 0:
                        po.wait_ge(s_qkw[(b - 1) % 2], 16 * ((b - 1) // 2 + 1))
                    g.tensor_tensor(qk16[:, 2 * (u % 2) + 1, u // 2], q32[:, u % 2],
                                    qk16[:, 2 * (u % 2), u // 2], ALU.subtract).then_inc(s_ql, 1)

            def bias_x(b):
                po.wait_ge(s_bc[b % 2], 16 * (b // 2 + 1))
                po.wait_ge(s_xn, TT * (b + 1))
                if b == 0:
                    po.wait_ge(s_bias, 48)
                link(g.tensor_tensor(bga, boutb, bc[:, b % 2, 0:H], ALU.mult))
                for t in range(TT):
                    i = g.tensor_tensor(x_sb[:, TT * b + t], x_sb[:, TT * b + t], bga, ALU.add)
                link(i)
                g.tensor_copy(ve1[0:1, 0:1], ve1[0:1, 0:1]).then_inc(s_xb, 1)

            def masks(b, gr):
                for j in range(TT):
                    po.wait_ge(s_exp, 44 * b + UNITS * gr + CUM[j])
                    d = PT[j][:, :, 0:P]
                    g.affine_select(out=d, in_=d, compare_op=ALU.is_ge, fill=0.0, base=0,
                                    pattern=[[0, 4], [1, P]], channel_multiplier=-1).then_inc(s_msk, 1)

            def norm2(b):
                rstd(ve2, mv2, rs2, b, s_mv2, s_rstd2)
                for t in range(TT):
                    n = TT * b + t
                    po.wait_ge(s_hm, n + 1)
                    link(g.tensor_tensor(h2f[:, t], h2f[:, t], bc[:, b % 2, H:2 * H], ALU.add))
                    i = g.tensor_copy(row[:, n, 0:H], h2f[:, t])
                    i.then_inc(s_h2, 1)
                    po.wait_ge(s_h2, n + 1)
                    g.tensor_tensor(row[:, n, H:2 * H], h2f[:, t], row[:, n, 0:H],
                                    ALU.subtract).then_inc(s_rl, 1)

            for b in range(2):
                project(b)
                bias_x(b)
            for b in range(B):
                for gr in range(NG):
                    masks(b, gr)
                if b + 2 < B:
                    project(b + 2)
                norm2(b)
                if b + 2 < B:
                    bias_x(b + 2)
            done = 0
            for b in range(B):
                for t in range(TT):
                    n = TT * b + t
                    po.wait_ge(s_ye, n + 1)
                    g.tensor_tensor(x_sb[:, n], x_sb[:, n], yo[:, n % 2], ALU.add).then_inc(s_x3, 1)
                if b == 2:
                    po.wait_ge(s_pos, 1)
                    po.wait_ge(s_srow, 1)
                    po.wait_ge(s_fill, 16)
                    for n in range(NT):
                        g.indirect_dma_start(xs_d, bass.IndirectOffsetOnAxis(ap=pos_i[:, n:n + 1].bitcast(U32), axis=0),
                                             row[:, n, :].bitcast(U32), None).then_inc(s_sct, 16)
            po.wait_ge(s_out, 16 * B)
            for r in range(RT + 1):
                if r < RT:
                    po.wait_ge(s_ld[r % 3], 16 * (r // 3 + 1))
                    if r >= 2:
                        po.wait_ge(s_rye, r - 1)
                    g.indirect_dma_start(gbr[:, r % 2, :], None, gb_d,
                                         bass.IndirectOffsetOnAxis(ap=rb32[:, r % 3, 258:259].bitcast(U32), axis=0)
                                         ).then_inc(s_gbr[r % 2], 16)
                if r:
                    q = r - 1
                    po.wait_ge(s_rye, q + 1)
                    g.indirect_dma_start(out.rearrange("b s n -> (b s) n"),
                                         bass.IndirectOffsetOnAxis(ap=rb32[:, q % 3, 257:258].bitcast(U32), axis=0),
                                         yo[:, q % 2], None, bounds_check=B * S - 1, oob_is_err=False,
                                         compute_op=ALU.add).then_inc(s_add, 16)
                    po.wait_ge(s_add, 16 * (q + 1))

        @block.scalar
        def _(ac):
            a = nc.scalar
            ac.wait_ge(s_c, 16)
            a.activation(cs[:, 1], cs[:, 0], ACT.Silu).then_inc(s_sc, 1)
            ac.wait_ge(s_wq, 16)
            a.activation(wq16[:, 0], wq_s, ACT.Copy, scale=WS).then_inc(s_wh, 1)
            ac.wait_ge(s_wo, 32)
            a.activation(wo16[:, 0], wo_s, ACT.Copy, scale=WS).then_inc(s_wh, 1)
            a.activation(rw16[:, 0], rw_s[:, :, :], ACT.Copy, scale=WS).then_inc(s_wh, 1)

            def project(b):
                for k in range(KC):
                    if k == 0:
                        ac.wait_ge(s_xt, b + 1)
                        if b == 0:
                            ac.wait_ge(s_m4, 1)
                        if b:
                            ac.wait_ge(s_qkv, 6 * b)
                    a.activation(h1[:, 0, k], MB[k][:, :], ACT.Identity, bias=sac[:, k, b:b + 1],
                                 scale=cac[:, k, b:b + 1]).then_inc(s_h1h, 1)
                for u in range(4):
                    ac.wait_ge(s_qkv, 6 * b + u + 1)
                    if b and u == 0:
                        ac.wait_ge(s_qkw[(b - 1) % 2], 16 * ((b - 1) // 2 + 1))
                    isk = u % 2
                    a.activation(qk16[:, 2 * isk, u // 2], SB[u % 2][:, :], ACT.Identity,
                                 bias=bqk[:, 2 * isk + u // 2:2 * isk + u // 2 + 1],
                                 scale=1.0 / WS if isk else 0.25 / WS).then_inc(s_qh, 1)

            def exps(b, gr):
                G = NG * b + gr
                for n, (j, i, m) in enumerate(KU):
                    N = 44 * b + UNITS * gr + n
                    w = S - P * j
                    ac.wait_ge(s_st, N + 1)
                    if i == 0 and G:
                        ac.wait_ge(s_pv, 4 * (G - 1) + j + 1)
                    a.activation(PT[j][:, i:i + m, :],
                                 TB[N % 3][:, 0:m * w].rearrange("p (i n) -> p i n", i=m),
                                 ACT.Exp).then_inc(s_exp, 1)
                    if n == 4 and gr:
                        outs(G - 1)

            def outs(G):
                ac.wait_ge(s_pv, 4 * G + 4)
                if G >= 2:
                    ac.wait_ge(s_rt, G - 1)
                a.activation(OTs[:, G % 2], OTb[:, :], ACT.Copy).then_inc(s_ote, 1)

            def attn_high(b):
                for k in range(KC):
                    ac.wait_ge(s_at, b + 1)
                    if b:
                        ac.wait_ge(s_o, TT * b)
                    a.activation(aT[:, 0, k], TB[k][:, :], ACT.Copy).then_inc(s_ath, 1)

            def h2_high(b):
                ac.wait_ge(s_ht, b + 1)
                a.activation(h2T[:, 0, :, S * b:S * (b + 1)],
                             T0[:, :].bitcast(F16).rearrange("p (k n) -> p k n", k=KC),
                             ACT.Copy).then_inc(s_hta, 1)

            def split_high(n):
                e, u = unit_list[n]
                ac.wait_ge(s_eld[n % 3], 32 * (n // 3 + 1))
                a.activation(W[:, e * WX + STEP * u:e * WX + STEP * (u + 1)], stage[:, n % 3, :],
                             ACT.Copy, scale=WS).then_inc(s_eh, 1)

            project(0)
            for n in range(3):
                split_high(n)
            project(1)
            for b in range(B):
                for gr in range(NG):
                    exps(b, gr)
                outs(NG * b + NG - 1)
                if b:
                    h2_high(b - 1)
                attn_high(b)
                if b + 2 < B:
                    project(b + 2)

            split = 3
            for b in range(B):
                for f in range(FC):
                    n = FC * b + f
                    ac.wait_ge(s_g, n + 1)
                    if n >= 2:
                        ac.wait_ge(s_hid, n - 1)
                    a.activation(g32[:, n % 2], [S0, M0][n % 2][:, :], ACT.Silu,
                                 scale=1.0 / WS).then_inc(s_silu, 1)
                    for _ in range(2):
                        if split < NU:
                            split_high(split)
                            split += 1
                    ac.wait_ge(s_hid, n + 1)
                    if b and f == 0:
                        ac.wait_ge(s_y, TT * b)
                    a.activation(hT[:, 0, f], hid[:, n % 2], ACT.Copy).then_inc(s_hh, 1)
                if b == 0:
                    h2_high(B - 1)
                if b == 1:
                    ac.wait_ge(s_top, 1)
                    a.activation(srow[:, :], top[:, :], ACT.Sigmoid).then_inc(s_sg, 1)

            def hidden_high(r):
                ac.wait_ge(s_rht, r + 1)
                if r >= 2:
                    ac.wait_ge(s_ry, r - 1)
                a.activation(rhT[:, r % 2, 0].rearrange("p f n -> p (f n)"), T1[:, :],
                             ACT.Copy).then_inc(s_rhh, 1)

            for r in range(RT + 1):
                if r < RT:
                    ac.wait_ge(s_rg, r + 1)
                    if r >= 2:
                        ac.wait_ge(s_rhid, r - 1)
                    a.activation(g32[:, r % 2], [S0, M0][r % 2][:, :], ACT.Silu,
                                 scale=rb32[:, r % 3, 256:257]).then_inc(s_rsilu, 1)
                if r:
                    hidden_high(r - 1)

        @block.vector
        def _(ve):
            v = nc.vector
            n_dv = [0]

            def link(ins):
                n_dv[0] += 1
                ins.then_inc(s_dv, 1)
                ve.wait_ge(s_dv, n_dv[0])

            def stats1(b):
                ve.wait_ge(s_x[b], 16)
                for t in range(TT):
                    i = v.bn_stats(st1[:, TT * b + t], x_sb[:, TT * b + t])
                link(i)
                for t in range(TT):
                    i = v.bn_aggr(mv1[:, TT * b + t], st1[:, TT * b + t])
                i.then_inc(s_mv, 1)

            def norm1(b):
                ve.wait_ge(s_rstd, b + 1)
                if b == 0:
                    ve.wait_ge(s_mv, 1)
                if b:
                    ve.wait_ge(s_xt, b)
                for t in range(TT):
                    n = TT * b + t
                    v.tensor_scalar(xn[:, t], x_sb[:, n], mv1[:, n, 0:1], rs1[:, n:n + 1],
                                    ALU.subtract, ALU.mult).then_inc(s_xn, 1)

            def project(b):
                stats1(b)
                norm1(b)
                if b == 0:
                    modulation()
                    low_parts()
                for k in range(KC):
                    ve.wait_ge(s_h1h, KC * b + k + 1)
                    if b and k == 0:
                        ve.wait_ge(s_ql, 4 * b)
                    v.tensor_scalar(h32[:, k], MB[k][:, :], cac[:, k, b:b + 1], sac[:, k, b:b + 1],
                                    ALU.mult, ALU.add).then_inc(s_h32, 1)
                for u in range(4):
                    ve.wait_ge(s_qh, 4 * b + u + 1)
                    if 4 * b + u >= 2:
                        ve.wait_ge(s_ql, 4 * b + u - 1)
                    isk = u % 2
                    v.tensor_scalar(q32[:, u % 2], SB[u % 2][:, :], 1.0 / WS if isk else 0.25 / WS,
                                    bqk[:, 2 * isk + u // 2:2 * isk + u // 2 + 1],
                                    ALU.mult, ALU.add).then_inc(s_q32, 1)
                for t in range(TT):
                    if t % 2 == 0:
                        ve.wait_ge(s_qkv, 6 * b + 5 + t // 2)
                    if t == 0 and b >= 2:
                        ve.wait_ge(s_pv, 16 * (b - 1))
                    dst = v1[:, b % 2, NH * 17 * t:NH * 17 * (t + 1)].rearrange("p (h d) -> p h d", d=17)
                    src = MB[t // 2][:, H * (t % 2):H * (t % 2 + 1)].rearrange("p (h d) -> p h d", d=HD)
                    v.scalar_tensor_tensor(dst[:, :, 0:HD], src, 1.0 / WS,
                                           bvb.rearrange("p (h d) -> p h d", d=HD),
                                           ALU.mult, ALU.add).then_inc(s_v, 1)

            def modulation():
                ve.wait_ge(s_mp, 1)
                v.tensor_copy(sac[:, :, :], T2[:, 0:8].rearrange("p (k b) -> p k b", k=KC))
                v.tensor_scalar(cac[:, :, :], T2[:, 8:16].rearrange("p (k b) -> p k b", k=KC),
                                1.0, None, ALU.add)
                v.tensor_copy(m4[:, H:2 * H], T0[0:B, H:2 * H])
                v.tensor_scalar(m4[:, 2 * H:3 * H], T1[0:B, 0:H], 1.0, None, ALU.add)
                for src, at_ in ((T0[0:B, 0:H], 0), (T1[0:B, H:2 * H], 3 * H)):
                    link(v.tensor_scalar(m4t[:, 0:H], src, 0.0, 2.0, ALU.is_ge, ALU.mult))
                    link(v.tensor_scalar(m4t[:, H:2 * H], src, -1.0, None, ALU.mult))
                    link(v.tensor_tensor(m4t[:, 2 * H:3 * H], src, m4t[:, H:2 * H], ALU.max))
                    link(v.tensor_scalar(m4t[:, 3 * H:4 * H], m4t[:, 2 * H:3 * H], 0.25, None, ALU.max))
                    link(v.scalar_tensor_tensor(m4[:, at_:at_ + H], m4t[:, 0:H], -1.0,
                                                m4t[:, 3 * H:4 * H], ALU.add, ALU.mult))
                ve.wait_ge(s_bias, 48)
                v.tensor_scalar(bqk[:, 0:2], bqk[:, 0:2], 0.25, None, ALU.mult).then_inc(s_m4, 1)
                ve.wait_ge(s_m4, 1)

            def low_parts():
                ve.wait_ge(s_wh, 1)
                v.scalar_tensor_tensor(wq16[:, 1], wq_s, WS, wq16[:, 0], ALU.mult,
                                       ALU.subtract).then_inc(s_wl, 1)
                ve.wait_ge(s_wh, 3)
                v.scalar_tensor_tensor(wo16[:, 1], wo_s, WS, wo16[:, 0], ALU.mult, ALU.subtract)
                v.scalar_tensor_tensor(rw16[:, 1], rw_s[:, :, :], WS, rw16[:, 0], ALU.mult,
                                       ALU.subtract).then_inc(s_wl, 1)

            def maxima(b, gr):
                for n, (t, i, m) in enumerate(QU):
                    N = 44 * b + UNITS * gr + n
                    w = P * (t + 1)
                    ve.wait_ge(s_s1, N + 1)
                    if gr == 0 and n == 0 and b >= 2:
                        ve.wait_ge(s_mt, b - 1)
                    c = NH * t + 4 * gr + i
                    v.tensor_reduce(mx[:, b % 2, c:c + m],
                                    SB[N % 2][:, 0:m * w].rearrange("p (i n) -> p i n", i=m),
                                    AX.X, ALU.max).then_inc(s_mx, 1)

            def negate(b):
                ve.wait_ge(s_mt, b + 1)
                if b:
                    ve.wait_ge(s_ngw, 16 * b)
                link(v.tensor_scalar(negm[:, 0], T2[0:64, 0:P], -1.0, None, ALU.mult))
                v.scalar_tensor_tensor(negm[:, 1], T2[0:64, 0:P], -1.0, negm[:, 0], ALU.mult,
                                       ALU.subtract).then_inc(s_neg, 1)

            def normalise(G):
                b, gr = G // NG, G % NG
                ve.wait_ge(s_rt, G + 1)
                if b and gr == 0:
                    ve.wait_ge(s_at, b)
                src = MB[G % 2][:, :].rearrange("p (t i d) -> p t i d", t=TT, i=4)
                r = rec[:, G % 2, :].rearrange("p (t i) -> p t i", t=TT)
                link(v.reciprocal(r, src[:, :, :, HD]))
                dst = an.rearrange("p t (h two d) -> p two t h d", two=2, d=HD)[:, gr // 2, :, 4 * (gr % 2):4 * (gr % 2) + 4]
                v.tensor_tensor(dst, src[:, :, :, 0:HD], r.unsqueeze(3).to_broadcast([P, TT, 4, HD]),
                                ALU.mult).then_inc(s_nrm, 1)

            def attn_low(b):
                for k in range(KC):
                    ve.wait_ge(s_ath, KC * b + k + 1)
                    if b and k == 0:
                        ve.wait_ge(s_o, TT * b)
                    v.tensor_tensor(aT[:, 1, k], TB[k][:, :], aT[:, 0, k], ALU.subtract).then_inc(s_atl, 1)

            def residual(b):
                ob = [T0, T1, S0, S1]
                for t in range(TT):
                    n = TT * b + t
                    ve.wait_ge(s_o, n + 1)
                    if t == 0:
                        ve.wait_ge(s_xb, b + 1)
                        if b:
                            ve.wait_ge(s_rl, TT * b)
                    link(v.scalar_tensor_tensor(o1[:, t], ob[t][:, 0:H], 1.0 / WS, bc[:, b % 2, 0:H],
                                                ALU.mult, ALU.mult))
                    v.tensor_tensor(x_sb[:, n], x_sb[:, n], o1[:, t], ALU.add).then_inc(s_x2, 1)
                ve.wait_ge(s_x2, TT * (b + 1))
                for t in range(TT):
                    i = v.bn_stats(st2[:, TT * b + t], x_sb[:, TT * b + t])
                link(i)
                for t in range(TT):
                    i = v.bn_aggr(mv2[:, TT * b + t], st2[:, TT * b + t])
                i.then_inc(s_mv2, 1)
                ve.wait_ge(s_mv2, b + 1)
                ve.wait_ge(s_rstd2, b + 1)
                for t in range(TT):
                    n = TT * b + t
                    link(v.tensor_scalar(h2f[:, t], x_sb[:, n], mv2[:, n, 0:1], rs2[:, n:n + 1],
                                         ALU.subtract, ALU.mult))
                    v.tensor_tensor(h2f[:, t], h2f[:, t], bc[:, b % 2, 2 * H:3 * H],
                                    ALU.mult).then_inc(s_hm, 1)

            def h2_low(b):
                ve.wait_ge(s_ht, b + 1)
                v.tensor_copy(h2T[:, 1, :, S * b:S * (b + 1)],
                              T1[:, :].bitcast(F16).rearrange("p (k n) -> p k n", k=KC)).then_inc(s_htd, 1)

            def logits(b):
                ve.wait_ge(s_r, b + 1)
                v.tensor_scalar(lg[:, TT * b:TT * (b + 1), :],
                                T2[:, 0:TT * E].rearrange("p (t e) -> p t e", t=TT), 1.0 / WS, None,
                                ALU.mult).then_inc(s_lg, 1)

            def split_low(n):
                e, u = unit_list[n]
                ve.wait_ge(s_eh, n + 1)
                c = e * WX + STEP * u
                v.scalar_tensor_tensor(W[:, c + WE:c + WE + STEP], stage[:, n % 3, :], WS,
                                       W[:, c:c + STEP], ALU.mult, ALU.subtract).then_inc(s_el, 1)

            project(0)
            for n in range(3):
                split_low(n)
            project(1)
            for gr in range(NG):
                maxima(0, gr)
            negate(0)
            for b in range(B):
                for gr in range(NG):
                    if b + 1 < B:
                        maxima(b + 1, gr)
                    if gr:
                        normalise(NG * b + gr - 1)
                if b:
                    h2_low(b - 1)
                    logits(b - 1)
                normalise(NG * b + NG - 1)
                attn_low(b)
                if b + 1 < B:
                    negate(b + 1)
                if b + 2 < B:
                    project(b + 2)
                residual(b)

            split = [3]

            def hidden(n):
                ve.wait_ge(s_silu, n + 1)
                ve.wait_ge(s_u, n + 1)
                if n >= 2:
                    ve.wait_ge(s_hh, n - 1)
                v.scalar_tensor_tensor(hid[:, n % 2], [S1, M1][n % 2][:, :], 1.0 / WS, g32[:, n % 2],
                                       ALU.mult, ALU.mult).then_inc(s_hid, 1)
                ve.wait_ge(s_hh, n + 1)
                b, f = n // FC, n % FC
                if b and f == 0:
                    ve.wait_ge(s_y, TT * b)
                v.tensor_tensor(hT[:, 1, f], hid[:, n % 2], hT[:, 0, f], ALU.subtract).then_inc(s_hl, 1)

            def route():
                ve.wait_ge(s_lg, B)
                ve.wait_ge(s_const, 4)
                v.tensor_reduce(top[:, :], lg[:, :, :], AX.X, ALU.max).then_inc(s_top, 1)
                ve.wait_ge(s_top, 1)
                link(v.tensor_tensor(oh[:, :, :], lg[:, :, :], top[:, :].unsqueeze(2).to_broadcast([P, NT, E]),
                                     ALU.is_equal))
                link(v.tensor_tensor(ohw[:, :, :], oh[:, :, :], iw[:, :].unsqueeze(1).to_broadcast([P, NT, E]),
                                     ALU.mult))
                link(v.tensor_reduce(wtop[:, :], ohw[:, :, :], AX.X, ALU.max))
                link(v.tensor_tensor(oh[:, :, :], ohw[:, :, :], wtop[:, :].unsqueeze(2).to_broadcast([P, NT, E]),
                                     ALU.is_equal))
                v.tensor_copy(oh16[:, :, :], oh[:, :, :]).then_inc(s_oh, 1)

            def slots():
                ve.wait_ge(s_rank, 1)
                count = OTb[:, 0:E]
                rank = T2[:, 0:NT * E].rearrange("p (t e) -> p t e", t=NT)
                link(v.tensor_tensor(cmpc[:, :, :], count.unsqueeze(2).to_broadcast([P, E, NT]),
                                     ij[:, :].unsqueeze(1).to_broadcast([P, E, NT]), ALU.is_gt))
                link(v.tensor_reduce(ntile[:, :], cmpc[:, :, :], AX.X, ALU.add))
                link(v.tensor_tensor_scan(ends[:, :], onesE[:, :], ntile[:, :], 0.0, ALU.mult, ALU.add))
                link(v.tensor_tensor(base[:, :], ends[:, :], ntile[:, :], ALU.subtract))
                link(v.tensor_scalar(base[:, :], base[:, :], float(P), None, ALU.mult))
                link(v.tensor_tensor(posf[:, :, :], rank, base[:, :].unsqueeze(1).to_broadcast([P, NT, E]),
                                     ALU.add))
                link(v.tensor_tensor(posf[:, :, :], posf[:, :, :], oh[:, :, :], ALU.mult))
                link(v.tensor_reduce(posr[:, :], posf[:, :, :], AX.X, ALU.add))
                v.tensor_copy(pos_i[:, :], posr[:, :]).then_inc(s_pos, 1)
                link(v.tensor_tensor(tec[:, :, :], it[:, :].unsqueeze(2).to_broadcast([P, RT, E]),
                                     ends[:, :].unsqueeze(1).to_broadcast([P, RT, E]), ALU.is_ge))
                link(v.tensor_reduce(tef[:, :], tec[:, :, :], AX.X, ALU.add))
                link(v.tensor_scalar(tef[:, :], tef[:, :], float(WX), None, ALU.mult))
                v.tensor_copy(te_i[:, :], tef[:, :]).then_inc(s_te, 1)
                ve.wait_ge(s_sg, 1)
                v.tensor_scalar(row32[:, :, 256], srow[:, :], 1.0 / WS, None, ALU.mult).then_inc(s_srow, 1)

            for b in range(B):
                for f in range(FC):
                    n = FC * b + f
                    hidden(n)
                    for _ in range(2):
                        if split[0] < NU:
                            split_low(split[0])
                            split[0] += 1
                if b == 0:
                    h2_low(B - 1)
                    logits(B - 1)
                    route()
                for t in range(TT):
                    n = TT * b + t
                    ve.wait_ge(s_y, n + 1)
                    if n >= 2:
                        ve.wait_ge(s_x3, n - 1)
                    if n == 0:
                        ve.wait_ge(s_gbb, 16)
                    v.scalar_tensor_tensor(yo[:, n % 2], [T0, T1, T2, OTb][t][:, 0:H], 1.0 / WS,
                                           gbb[:, b], ALU.mult, ALU.mult).then_inc(s_ye, 1)
                if b == 1:
                    slots()

            def rows_in(r):
                ve.wait_ge(s_rxt, r + 1)
                if r >= 2:
                    ve.wait_ge(s_ru, r - 1)
                v.tensor_copy(xT[:, r % 2, 0:512], T0[:, 0:256].bitcast(F16)).then_inc(s_rxe, 1)

            def hidden_low(r):
                ve.wait_ge(s_rhh, r + 1)
                v.tensor_tensor(rhT[:, r % 2, 1].rearrange("p f n -> p (f n)"), T1[:, :],
                                rhT[:, r % 2, 0].rearrange("p f n -> p (f n)"), ALU.subtract).then_inc(s_rhl, 1)

            def routed_out(r):
                ve.wait_ge(s_ry, r + 1)
                ve.wait_ge(s_gbr[r % 2], 16 * (r // 2 + 1))
                if r >= 2:
                    ve.wait_ge(s_add, 16 * (r - 1))
                if r == 0:
                    ve.wait_ge(s_x3, NT)
                v.scalar_tensor_tensor(yo[:, r % 2], [T2, OTb][r % 2][:, 0:H], 1.0 / WS, gbr[:, r % 2],
                                       ALU.mult, ALU.mult).then_inc(s_rye, 1)

            rows_in(0)
            for r in range(RT + 1):
                if r:
                    hidden_low(r - 1)
                if r < RT:
                    ve.wait_ge(s_ru, r + 1)
                    ve.wait_ge(s_rsilu, r + 1)
                    if r >= 2:
                        ve.wait_ge(s_rht, r - 1)
                    v.scalar_tensor_tensor(hid[:, r % 2], [S1, M1][r % 2][:, :], rb32[:, r % 3, 256:257],
                                           g32[:, r % 2], ALU.mult, ALU.mult).then_inc(s_rhid, 1)
                if r + 1 < RT:
                    rows_in(r + 1)
                if r:
                    routed_out(r - 1)

        @block.tensor
        def _(pe):
            t_ = nc.tensor

            def split_mm(outp, pairs, **kw):
                prods = [p for (ah, al, bh, bl) in pairs for p in ((ah, bh), (ah, bl), (al, bh))]
                for n, (l, r) in enumerate(prods):
                    i = t_.matmul(outp, l, r, start=(n == 0), stop=(n == len(prods) - 1), **kw)
                return i

            def modulation():
                pe.wait_ge(s_sc, 1)
                pe.wait_ge(s_wm, 16)
                for c in range(4):
                    for k in range(KC):
                        t_.matmul(T2[:, 4 * c:4 * c + 4], wm[:, k, P * c:P * (c + 1)], cs[:, 1, k],
                                  start=(k == 0), stop=(k == KC - 1))
                for c, bk in enumerate((T0, T1)):
                    for k in range(KC):
                        i = t_.matmul(bk[0:B, :], cs[:, 1, k], wm[:, k, 512 * (c + 1):512 * (c + 2)],
                                      start=(k == 0), stop=(k == KC - 1))
                i.then_inc(s_mp, 1)

            def project(b):
                pe.wait_ge(s_xn, TT * (b + 1))
                if b == 0:
                    pe.wait_ge(s_const, 2)
                if b:
                    pe.wait_ge(s_v, TT * b)
                if b >= 2:
                    pe.wait_ge(s_nrm, NG * (b - 1))
                for k in range(KC):
                    for t in range(TT):
                        i = t_.transpose(MB[k][:, P * t:P * (t + 1)], xn[:, t, P * k:P * (k + 1)], ident[:, :])
                i.then_inc(s_xt, 1)
                if b == 0:
                    modulation()
                    pe.wait_ge(s_wl, 1)
                pe.wait_ge(s_h1l, KC * (b + 1))
                for u in range(4):
                    n = 4 * b + u
                    if n >= 2:
                        pe.wait_ge(s_q32, n - 1)
                    if u == 0 and b >= 2:
                        pe.wait_ge(s_mx, 44 * b)
                    c = H * (u % 2) + P * (u // 2)
                    split_mm(SB[u % 2][:, :],
                             [(wq16[:, 0, k, c:c + P], wq16[:, 1, k, c:c + P], h1[:, 0, k], h1[:, 1, k])
                              for k in range(KC)]).then_inc(s_qkv, 1)
                pe.wait_ge(s_h32, KC * (b + 1))
                for t in range(TT):
                    sl = slice(P * t, P * (t + 1))
                    i = split_mm(MB[t // 2][:, H * (t % 2):H * (t % 2 + 1)],
                                 [(h1[:, 0, k, sl], h1[:, 1, k, sl], wq16[:, 0, k, 2 * H:3 * H],
                                   wq16[:, 1, k, 2 * H:3 * H]) for k in range(KC)])
                    if t % 2:
                        i.then_inc(s_qkv, 1)

            def scores(b, gr, n):
                N = 44 * b + UNITS * gr + n
                t, i0, m = QU[n]
                r = b % 2
                p0, hp0 = group_heads(gr)
                if gr == 0 and n == 0:
                    pe.wait_ge(s_stk[r], 16 * 12 * (b // 2 + 1))
                    pe.wait_ge(s_q32, 4 * (last_p(max(b - 1, 0)) + 1))
                    if b == 0:
                        pe.wait_ge(s_const, 3)
                    if b >= 2:
                        pe.wait_ge(s_x2, TT * (b - 1))
                if N >= 2:
                    pe.wait_ge(s_mx, N - 1)
                w = P * (t + 1)
                bk = SB[N % 2]
                for i in range(m):
                    hp = hp0 + i0 + i
                    t_.matmul(bk[:, w * i:w * (i + 1)], stk[p0:p0 + 48, r, 0, hp, P * t:w],
                              stk[p0:p0 + 48, r, 1, hp, 0:w], start=(i == 0), stop=False, skip_group_check=True)
                t_.matmul(bk[:, 0:m * w].rearrange("p (i n) -> p i n", i=m)[:, :, w - P:w], identb[:, :],
                          maskb[:, :].unsqueeze(1).to_broadcast([P, m, P]), start=False, stop=True,
                          skip_group_check=True).then_inc(s_s1, 1)

            def max_turn(b):
                pe.wait_ge(s_mx, 44 * (b + 1))
                if b:
                    pe.wait_ge(s_exp, 44 * b)
                if b >= 2:
                    pe.wait_ge(s_lg, b - 1)
                t_.transpose(T2[0:64, 0:P], mx[:, b % 2], ident[:, :]).then_inc(s_mt, 1)

            def scores_t(b, gr, n):
                N = 44 * b + UNITS * gr + n
                j, i0, m = KU[n]
                r = b % 2
                p0, hp0 = group_heads(gr)
                if gr == 0 and n == 0:
                    pe.wait_ge(s_ng[r], 16 * 2 * TT * (b // 2 + 1))
                    pe.wait_ge(s_neg, b + 1)
                    if b:
                        pe.wait_ge(s_x2, TT * b)
                if N >= 3:
                    pe.wait_ge(s_exp, N - 2)
                w = S - P * j
                for i in range(m):
                    hp = hp0 + i0 + i
                    q = t_.matmul(TB[N % 3][:, w * i:w * (i + 1)], stk[p0:p0 + 50, r, 1, hp, P * j:P * (j + 1)],
                                  stk[p0:p0 + 50, r, 0, hp, P * j:S], start=True, stop=True)
                q.then_inc(s_st, 1)

            def values(G, j):
                b, gr = G // NG, G % NG
                if gr == 0 and j == 0:
                    pe.wait_ge(s_v, TT * (b + 1))
                if j == 0 and G:
                    pe.wait_ge(s_ote, G)
                pe.wait_ge(s_msk, 4 * G + j + 1)
                _, hp0 = group_heads(gr)
                for i in range(4):
                    h = 2 * (hp0 + i) + gr // 2
                    c = 17 * (NH * j + h)
                    q = t_.matmul(OTb[32 * i:32 * i + 32, P * j:S], v1[:, b % 2, c:c + 32], PT[j][:, i],
                                  start=(j == 0), stop=(j == TT - 1), tile_position=(0, 32 * i),
                                  skip_group_check=True)
                q.then_inc(s_pv, 1)

            def turn_out(G):
                pe.wait_ge(s_ote, G + 1)
                if G >= 2:
                    pe.wait_ge(s_nrm, G - 1)
                if G % NG == 0:
                    pe.wait_ge(s_v, TT * (last_p(G // NG) + 1))
                for t in range(TT):
                    q = t_.transpose(MB[G % 2][:, P * t:P * (t + 1)], OTs[:, G % 2, P * t:P * (t + 1)], ident[:, :])
                q.then_inc(s_rt, 1)

            def attend(b):
                for gr in range(NG):
                    G = NG * b + gr
                    for n in range(UNITS):
                        scores_t(b, gr, n)
                        if b + 1 < B:
                            scores(b + 1, gr, n)
                        if n == 1 and gr:
                            values(G - 1, 2)
                        if n == 3 and gr:
                            values(G - 1, 3)
                        if n == 6 and gr:
                            turn_out(G - 1)
                        if n == 8:
                            values(G, 0)
                        if n == 10:
                            values(G, 1)
                values(NG * b + NG - 1, 2)
                values(NG * b + NG - 1, 3)

            def attn_turn(b):
                turn_out(NG * b + NG - 1)
                pe.wait_ge(s_nrm, NG * (b + 1))
                pe.wait_ge(s_exp, 44 * (b + 1))
                if b:
                    pe.wait_ge(s_htd, b)
                    pe.wait_ge(s_hta, b)
                for k in range(KC):
                    for t in range(TT):
                        q = t_.transpose(TB[k][:, P * t:P * (t + 1)], an[:, t, P * k:P * (k + 1)], ident[:, :])
                q.then_inc(s_at, 1)

            def output(b):
                pe.wait_ge(s_atl, KC * (b + 1))
                if b == 0:
                    pe.wait_ge(s_wl, 2)
                for t, bk in enumerate((T0, T1, S0, S1)):
                    if t == 2:
                        pe.wait_ge(s_q32, 4 * (min(b + 2, B - 1) + 1))
                        pe.wait_ge(s_mx, 44 * (min(b + 1, B - 1) + 1))
                    sl = slice(P * t, P * (t + 1))
                    split_mm(bk[:, 0:H], [(aT[:, 0, k, sl], aT[:, 1, k, sl], wo16[:, 0, k], wo16[:, 1, k])
                                          for k in range(KC)]).then_inc(s_o, 1)

            def h2_turn(b):
                pe.wait_ge(s_rl, TT * (b + 1))
                pe.wait_ge(s_exp, 44 * min(b + 2, B))
                pe.wait_ge(s_x2, TT * (b + 1))
                for part, bk in enumerate((T0, T1)):
                    o = bk[:, :].bitcast(F16)
                    for k in range(KC):
                        for t in range(TT):
                            q = t_.transpose(o[:, S * k + P * t:S * k + P * (t + 1)],
                                             row[:, TT * b + t, H * part + P * k:H * part + P * (k + 1)],
                                             ident16[:, :])
                q.then_inc(s_ht, 1)

            def router(b):
                pe.wait_ge(s_hta, b + 1)
                pe.wait_ge(s_htd, b + 1)
                for t in range(TT):
                    sl = slice(S * b + P * t, S * b + P * (t + 1))
                    q = split_mm(T2[:, E * t:E * (t + 1)],
                                 [(h2T[:, 0, k, sl], h2T[:, 1, k, sl], rw16[:, 0, k], rw16[:, 1, k])
                                  for k in range(KC)])
                q.then_inc(s_r, 1)

            project(0)
            project(1)
            for gr in range(NG):
                for n in range(UNITS):
                    scores(0, gr, n)
            max_turn(0)
            for b in range(B):
                attend(b)
                if b:
                    h2_turn(b - 1)
                    router(b - 1)
                attn_turn(b)
                if b + 1 < B:
                    max_turn(b + 1)
                if b + 2 < B:
                    project(b + 2)
                output(b)

            def we(e, part, k_or_f, lo, n, is_down=False):
                c = e * WX + part * WE + (KC * 2 * I + H * k_or_f if is_down else 2 * I * k_or_f) + lo
                return W[:, c:c + n]

            def shared(b):
                if b == 0:
                    pe.wait_ge(s_el, 3)
                tok = slice(S * b, S * (b + 1))
                for f in range(FC):
                    n = FC * b + f
                    gk, uk = (S0, S1) if n % 2 == 0 else (M0, M1)
                    if n == 0:
                        pe.wait_ge(s_x2, TT * B)
                    if n == 1:
                        pe.wait_ge(s_nrm, NG * B)
                    if n >= 2:
                        pe.wait_ge(s_hid, n - 1)
                    for half, bk, s in ((0, gk, s_g), (I, uk, s_u)):
                        split_mm(bk[:, :], [(we(E, 0, k, half + P * f, P), we(E, 1, k, half + P * f, P),
                                             h2T[:, 0, k, tok], h2T[:, 1, k, tok])
                                            for k in range(KC)]).then_inc(s, 1)

            def shared_down(b):
                pe.wait_ge(s_hl, FC * (b + 1))
                for t, bk in enumerate((T0, T1, T2, OTb)):
                    if b:
                        pe.wait_ge(s_ye, TT * (b - 1) + t + 1)
                    elif t == 0:
                        pe.wait_ge(s_lg, B)
                        pe.wait_ge(s_htd, B)
                        pe.wait_ge(s_hta, B)
                    sl = slice(P * t, P * (t + 1))
                    split_mm(bk[:, 0:H], [(hT[:, 0, f, sl], hT[:, 1, f, sl], we(E, 0, f, 0, H, True),
                                           we(E, 1, f, 0, H, True)) for f in range(FC)]).then_inc(s_y, 1)

            def ranks():
                pe.wait_ge(s_oh, 1)
                pe.wait_ge(s_ye, TT * 2)
                rank = T2[:, 0:NT * E]
                t_.matmul(rank, tri16[:, :], oh16[:, :, :].rearrange("p t e -> p (t e)"), start=True,
                          stop=False, skip_group_check=True)
                for t in range(NT - 1):
                    m = NT - 1 - t
                    t_.matmul(rank[:, E * (t + 1):].rearrange("p (t e) -> p t e", t=m), ones16[:, :],
                              oh16[:, t:t + 1, :].to_broadcast([P, m, E]), start=False, stop=(t == NT - 2),
                              skip_group_check=True)
                for t in range(NT):
                    q = t_.matmul(OTb[:, 0:E], ones16[:, :], oh16[:, t], start=(t == 0), stop=(t == NT - 1))
                q.then_inc(s_rank, 1)

            for b in range(B):
                shared(b)
                if b == 0:
                    h2_turn(B - 1)
                    router(B - 1)
                if b == 2:
                    pe.wait_ge(s_pos, 1)
                shared_down(b)
                if b == 1:
                    ranks()

            def rows_turn(r):
                pe.wait_ge(s_ld[r % 3], 16 * (r // 3 + 1))
                if r:
                    pe.wait_ge(s_rxe, r)
                else:
                    pe.wait_ge(s_ye, NT)
                o = T0[:, 0:256].bitcast(F16)
                for c in range(4):
                    q = t_.transpose(o[:, P * c:P * (c + 1)], rb[:, r % 3, P * c:P * (c + 1)], ident16[:, :])
                q.then_inc(s_rxt, 1)

            def up_half(r, off, half, bk, s):
                pairs = []
                for k in range(KC):
                    c = 2 * I * k + half
                    pairs.append((xT[:, r % 2, P * k:P * (k + 1)], xT[:, r % 2, 256 + P * k:256 + P * (k + 1)],
                                  W[:, bass.ds(off + c, I)], W[:, bass.ds(off + (c + WE), I)]))
                split_mm(bk[:, :], pairs).then_inc(s, 1)

            def hidden_turn(r):
                pe.wait_ge(s_rhid, r + 1)
                if r:
                    pe.wait_ge(s_rhl, r)
                for f in range(FC):
                    q = t_.transpose(T1[:, P * f:P * (f + 1)], hid[:, r % 2, P * f:P * (f + 1)], ident[:, :])
                q.then_inc(s_rht, 1)

            def down_rows(r, off):
                pe.wait_ge(s_rhl, r + 1)
                if r >= 2:
                    pe.wait_ge(s_rye, r - 1)
                pairs = []
                for f in range(FC):
                    c = KC * 2 * I + H * f
                    pairs.append((rhT[:, r % 2, 0, f], rhT[:, r % 2, 1, f],
                                  W[:, bass.ds(off + c, H)], W[:, bass.ds(off + (c + WE), H)]))
                split_mm([T2, OTb][r % 2][:, 0:H], pairs).then_inc(s_ry, 1)

            rows_turn(0)
            pe.wait_ge(s_te, 1)
            pe.wait_ge(s_el, NU)
            offs = {}
            for r in range(RT + 1):
                if r < RT:
                    offs[r] = t_.value_load(te_i[0:1, r:r + 1], min_val=0, max_val=E * WX)
                    pe.wait_ge(s_rxe, r + 1)
                    if r >= 2:
                        pe.wait_ge(s_rhid, r - 1)
                    elif r == 0:
                        pe.wait_ge(s_hid, NT)
                    gk, uk = (S0, S1) if r % 2 == 0 else (M0, M1)
                    up_half(r, offs[r], 0, gk, s_rg)
                if r:
                    hidden_turn(r - 1)
                if r < RT:
                    up_half(r, offs[r], I, uk, s_ru)
                if r:
                    down_rows(r - 1, offs[r - 1])
                if r + 1 < RT:
                    rows_turn(r + 1)


_INS = ["x", "wqkvT", "bqkv", "bqkc", "woutT", "bout", "rwT", "gup", "down", "sgw", "suw", "sdw", "cT", "wmod"]


def kernel(L0_attn_x, L0_attn_Wqkv, L0_attn_bqkv, L0_attn_Wout, L0_attn_bout, L0_ffn_router_w,
           L0_ffn_gate_up_proj, L0_ffn_down_proj, L0_ffn_shared_gate_w, L0_ffn_shared_up_w,
           L0_ffn_shared_down_w, L0_c, L0_wmod):
    import concourse.bacc as bacc
    from concourse.bass_utils import run_bass_kernel_spmd

    given = dict(x=L0_attn_x, wqkvT=np.asarray(L0_attn_Wqkv).T, bqkv=L0_attn_bqkv,
                 bqkc=np.asarray(L0_attn_bqkv)[:2 * H].reshape(4, P).T,
                 woutT=np.asarray(L0_attn_Wout).T, bout=L0_attn_bout,
                 rwT=np.asarray(L0_ffn_router_w).T, gup=L0_ffn_gate_up_proj, down=L0_ffn_down_proj,
                 sgw=L0_ffn_shared_gate_w, suw=L0_ffn_shared_up_w, sdw=L0_ffn_shared_down_w,
                 cT=np.asarray(L0_c).T, wmod=L0_wmod)
    nc = bacc.Bacc("TRN2", target_bir_lowering=False, num_devices=1)
    arrays, args = {}, []
    for name in _INS:
        a = np.ascontiguousarray(given[name])
        arrays["in_" + name] = a
        args.append(nc.dram_tensor("in_" + name, a.shape, mybir.dt.from_np(a.dtype), kind="ExternalInput").ap())
    args.append(nc.dram_tensor("out_0", (B, S, H), F32, kind="ExternalOutput").ap())
    build(nc, *args)
    r = run_bass_kernel_spmd(nc, [arrays], core_ids=[0])
    return r.results[0]["out_0"]
```

```python
import numpy as np
import concourse.bass as bass
from concourse import mybir
from contextlib import ExitStack

F32, F16, BF16, I32 = mybir.dt.float32, mybir.dt.float16, mybir.dt.bfloat16, mybir.dt.int32
U32 = mybir.dt.uint32
ALU = mybir.AluOpType
ACT = mybir.ActivationFunctionType
AX = mybir.AxisListType

P = 128
B, S, H = 4, 512, 256
NH, HD = 16, 16
E, I = 8, 512
TT = S // P
NT = B * TT
KC = H // P
FC = I // P
RT = NT + E - 1
WS = 64.0
EPS = 1e-5
WE = KC * 2 * I + FC * H
WX = 2 * WE
ROW = 520
OOB = 1 << 20
NEG = -1e30
UNITS = 11
CUM = [4, 8, 10, 11]
STEP = 1024
GR = 8
YR = 4
NG = 4


def group_heads(g):
    return g % 2, 4 * (g // 2)


def place(e):
    return (E - e) * WX


def query_units():
    return [(0, 0, 4), (1, 0, 2), (1, 2, 2)] + [(t, i, 1) for t in (2, 3) for i in range(4)]


def key_units():
    return [(0, i, 1) for i in range(4)] + [(1, i, 1) for i in range(4)] + [(2, 0, 2), (2, 2, 2), (3, 0, 4)]


def build(nc, x, wqkvT, bqkv, bqkc, woutT, bout, rwT, gup, down, sgw, suw, sdw, cT, wmod, out):
    ctx = ExitStack()
    with ctx:
        def sb(name, shape, dt=F32):
            return ctx.enter_context(nc.sbuf_tensor(name, shape, dt))

        def sem(name):
            return ctx.enter_context(nc.semaphore(name))

        qk_d = nc.dram_tensor("qk_d", [2, 4, H, S], F16).ap()
        ng_d = nc.dram_tensor("ng_d", [2, 64, 2, P], F16).ap()
        mod_d = nc.dram_tensor("mod_d", [B, 4 * H], F32).ap()
        gb_d = nc.dram_tensor("gb_d", [B, H], F32).ap()
        xs_d = nc.dram_tensor("xs_d", [RT * P, ROW // 2], U32).ap()

        W = sb("W", [P, (E + 1) * WX], F16)
        x_sb = sb("x_sb", [P, NT, H])
        row = sb("row", [P, NT, ROW], F16)
        row32 = row[:, :, :].bitcast(F32)
        h2T = sb("h2T", [P, 2, KC, B * S], F16)
        stage = sb("stage", [P, 3, STEP])
        ffn = sb("ffn", [P, 5120])
        gbb = sb("gbb", [P, B, H])
        ident = sb("ident", [P, P])
        ident16 = sb("ident16", [P, P], F16)
        identb = sb("identb", [P, P], BF16)
        maskb = sb("maskb", [P, P], BF16)
        tri16 = sb("tri16", [P, P], F16)
        ones16 = sb("ones16", [P, P], F16)
        neghalf = sb("neghalf", [P, TT])
        iw_i = sb("iw_i", [P, E], I32)
        ij_i = sb("ij_i", [P, NT], I32)
        it_i = sb("it_i", [P, RT], I32)
        iw = sb("iw", [P, E])
        ij = sb("ij", [P, NT])
        it = sb("it", [P, RT])
        cs = sb("cs", [P, 2, KC, B])
        sac = sb("sac", [P, KC, B])
        cac = sb("cac", [P, KC, B])
        bqk = sb("bqk", [P, 4])
        st1 = sb("st1", [P, NT, 6])
        mv1 = sb("mv1", [P, NT, 2])
        ve1 = sb("ve1", [P, NT])
        rs1 = sb("rs1", [P, NT])
        st2 = sb("st2", [P, NT, 6])
        mv2 = sb("mv2", [P, NT, 2])
        ve2 = sb("ve2", [P, NT])
        rs2 = sb("rs2", [P, NT])
        rw_s = sb("rw_s", [P, KC, E])
        rw16 = sb("rw16", [P, 2, KC, E], F16)
        lg = sb("lg", [P, NT, E])
        mx = sb("mx", [P, 2, 64])
        negm = sb("negm", [64, 2, P], F16)
        rec = sb("rec", [P, 2, NH])
        top = sb("top", [P, NT])
        oh = sb("oh", [P, NT, E])
        ohw = sb("ohw", [P, NT, E])
        wtop = sb("wtop", [P, NT])
        oh16 = sb("oh16", [P, NT, E], F16)
        cmpc = sb("cmpc", [P, E, NT])
        ntile = sb("ntile", [P, E])
        onesE = sb("onesE", [P, E])
        ends = sb("ends", [P, E])
        base = sb("base", [P, E])
        posf = sb("posf", [P, NT, E])
        posr = sb("posr", [P, NT])
        pos_i = sb("pos_i", [P, NT], I32)
        tec = sb("tec", [P, RT, E])
        tef = sb("tef", [P, RT])
        te_i = sb("te_i", [P, RT], I32)
        srow = sb("srow", [P, NT])
        fillb = sb("fillb", [P, ROW], F16)
        fill = fillb[:, :]

        at = [0]

        def early(cols, dt=F32):
            n = cols * (2 if dt == F32 else 1)
            v = W[:, at[0]:at[0] + n]
            at[0] += n
            return v.bitcast(F32) if dt == F32 else v

        wq16 = early(2 * KC * 3 * H, F16).rearrange("p (s k n) -> p s k n", s=2, k=KC)
        xn = early(TT * H).rearrange("p (t n) -> p t n", t=TT)
        h1 = early(2 * KC * S, F16).rearrange("p (s k n) -> p s k n", s=2, k=KC)
        h32 = early(KC * S).rearrange("p (k n) -> p k n", k=KC)
        q32 = h32
        bvb = early(H)
        qk16 = early(4 * 2 * S, F16).rearrange("p (a c n) -> p a c n", a=4, c=2)
        qs, ks, v1 = [], [], []
        for _ in range(2):
            qs.append(early(NH * S, F16).rearrange("p (h two n) -> p h two n", two=2, n=S))
            ks.append(early(NH // 2 * S, F16).rearrange("p (h n) -> p h n", n=S))
            v1.append(early(TT * NH * 17 + 16))
        wo16 = early(2 * KC * H, F16).rearrange("p (s k n) -> p s k n", s=2, k=KC)
        OTs = early(2 * S).rearrange("p (r n) -> p r n", r=2)
        an = early(TT * H).rearrange("p (t n) -> p t n", t=TT)
        aT = early(2 * KC * S, F16).rearrange("p (s k n) -> p s k n", s=2, k=KC)
        bc = early(2 * 3 * H).rearrange("p (r n) -> p r n", r=2)
        o1 = early(TT * H).rearrange("p (t n) -> p t n", t=TT)
        h2f = o1
        assert at[0] <= (E + 1) * WX
        boutb = gbb[:, 0]
        bga = gbb[:, 1]
        pt_at = [0, 4 * 512, 4 * 896, 4 * 1152]
        PT = [ffn[:, pt_at[j]:pt_at[j] + 4 * (S - P * j)].rearrange("p (i n) -> p i n", i=4)
              for j in range(TT)]
        wm = stage[:, :, :].rearrange("p a b -> p (a b)").rearrange("p (k n) -> p k n", k=KC)
        hs = h2T[:, :, :, :].rearrange("p a b c -> p (a b c)").bitcast(F32)
        wq_s = hs[:, 0:KC * 3 * H].rearrange("p (k n) -> p k n", k=KC)
        wo_s = hs[:, KC * 3 * H:KC * 4 * H].rearrange("p (k n) -> p k n", k=KC)
        m4 = hs[0:B, KC * 4 * H:KC * 4 * H + 4 * H]
        m4t = hs[0:B, KC * 6 * H:KC * 6 * H + 4 * H]
        g32 = ffn[:, 0:2 * I].rearrange("p (r n) -> p r n", r=2)
        hid = ffn[:, 2 * I:4 * I].rearrange("p (r n) -> p r n", r=2)
        hT = ffn[:, 4 * I:8 * I].bitcast(F16).rearrange("p (s f n) -> p s f n", s=2, f=FC)
        xT = ffn[:, 8 * I:9 * I].bitcast(F16).rearrange("p (r n) -> p r n", r=2)
        yo = ffn[:, 9 * I:10 * I].rearrange("p (r n) -> p r n", r=2)
        gbr = [h2T[:, n // 2 % 2, n % 2, S * (n // 4):S * (n // 4 + 1)].bitcast(F32) for n in range(GR)]
        ry = [h2T[:, n // 2, n % 2, 2 * S:3 * S].bitcast(F32) for n in range(YR)]
        rhT = hT.rearrange("p s f n -> p (s f n)").rearrange("p (r s f n) -> p r s f n", r=4, s=2, f=FC)[:, 0:2]

        bank = [ctx.enter_context(nc.psum_tensor(f"bank{i}", [P, 512], F32)) for i in range(8)]
        S0, S1, T0, T1, T2, OTb, M0, M1 = bank
        SB, TB, MB = [S0, S1], [T0, T1, T2], [M0, M1]

        s_const = sem("s_const")
        s_c = sem("s_c")
        s_wm = sem("s_wm")
        s_wq = sem("s_wq")
        s_wo = sem("s_wo")
        s_bias = sem("s_bias")
        s_x = [sem(f"s_xin{b}") for b in range(B)]
        s_sc = sem("s_sc")
        s_mp = sem("s_mp")
        s_m4 = sem("s_m4")
        s_md = sem("s_md")
        s_bc = [sem(f"s_bc{r}") for r in range(2)]
        s_gbb = sem("s_gbb")
        s_wh = sem("s_wh")
        s_wl = sem("s_wl")
        s_mv = sem("s_mv")
        s_rstd = sem("s_rstd")
        s_xn = sem("s_xn")
        s_xt = sem("s_xt")
        s_h1h = sem("s_h1h")
        s_h32 = sem("s_h32")
        s_h1l = sem("s_h1l")
        s_qkv = sem("s_qkv")
        s_qh = sem("s_qh")
        s_q32 = sem("s_q32")
        s_ql = sem("s_ql")
        s_v = sem("s_v")
        s_xb = sem("s_xb")
        s_qkw = [sem(f"s_qkw{r}") for r in range(2)]
        s_stk = [sem(f"s_stk{r}") for r in range(2)]
        s_s1 = sem("s_s1")
        s_mx = sem("s_mx")
        s_mt = sem("s_mt")
        s_neg = sem("s_neg")
        s_ngw = sem("s_ngw")
        s_ng = [sem(f"s_ng{r}") for r in range(2)]
        s_st = sem("s_st")
        s_exp = sem("s_exp")
        s_msk = sem("s_msk")
        s_pv = sem("s_pv")
        s_ote = sem("s_ote")
        s_rt = sem("s_rt")
        s_nrm = sem("s_nrm")
        s_at = sem("s_at")
        s_ath = sem("s_ath")
        s_atl = sem("s_atl")
        s_o = sem("s_o")
        s_x2 = sem("s_x2")
        s_mv2 = sem("s_mv2")
        s_rstd2 = sem("s_rstd2")
        s_hm = sem("s_hm")
        s_h2 = sem("s_h2")
        s_rh = sem("s_rh")
        s_rl = sem("s_rl")
        s_ht = sem("s_ht")
        s_hta = sem("s_hta")
        s_htd = sem("s_htd")
        s_r = sem("s_r")
        s_lg = sem("s_lg")
        s_dv = sem("s_dv")
        s_po = sem("s_po")
        s_eld = [sem(f"s_eld{r}") for r in range(3)]
        s_eh = sem("s_eh")
        s_el = sem("s_el")
        s_g = sem("s_g")
        s_u = sem("s_u")
        s_silu = sem("s_silu")
        s_hid = sem("s_hid")
        s_hh = sem("s_hh")
        s_hl = sem("s_hl")
        s_y = sem("s_y")
        s_ye = sem("s_ye")
        s_x3 = sem("s_x3")
        s_out = sem("s_out")
        s_fill = sem("s_fill")
        s_oh = sem("s_oh")
        s_rank = sem("s_rank")
        s_pos = sem("s_pos")
        s_te = sem("s_te")
        s_top = sem("s_top")
        s_sg = sem("s_sg")
        s_srow = sem("s_srow")
        s_sct = sem("s_sct")
        s_ld = [sem(f"s_ld{r}") for r in range(NT)]
        s_gbr = [sem(f"s_gbr{r}") for r in range(GR)]
        s_rxt = sem("s_rxt")
        s_rxe = sem("s_rxe")
        s_rg = sem("s_rg")
        s_ru = sem("s_ru")
        s_rsilu = sem("s_rsilu")
        s_rhid = sem("s_rhid")
        s_rht = sem("s_rht")
        s_rhh = sem("s_rhh")
        s_rhl = sem("s_rhl")
        s_ry = sem("s_ry")
        s_rye = sem("s_rye")
        s_add = sem("s_add")

        QU, KU = query_units(), key_units()

        def last_p(b):
            return min(b + 1, B - 1)

        unit_list = [(E, u) for u in range(3)] + [(e, u) for e in reversed(range(E)) for u in range(3)]
        NU = len(unit_list)

        def early_splits(b, gr):
            if b < B - 2:
                return ()
            n = 6 * (b - B + 2) + 3 * gr // 2
            return range(n, 6 * (b - B + 2) + 3 * (gr + 1) // 2)

        gu_v = gup.rearrange("e (k p) n -> e k p n", p=P)
        dn_v = down.rearrange("e (f p) n -> e p f n", p=P)

        block = ctx.enter_context(nc.Block())

        @block.sync
        def _(sp):
            sp.dma_start(cs[:, 0], cT.rearrange("(k p) b -> p k b", p=P)).then_inc(s_c, 16)
            sp.dma_start(x_sb[:, 0:TT, :], x[0].rearrange("(t p) n -> p t n", p=P)).then_inc(s_x[0], 16)
            sp.dma_start(wm, wmod.rearrange("(k p) n -> p k n", p=P)).then_inc(s_wm, 16)
            sp.dma_start(wq_s, wqkvT.rearrange("(k p) n -> p k n", p=P)).then_inc(s_wq, 16)
            sp.dma_start(bqk[:, :], bqkc).then_inc(s_bias, 16)
            sp.dma_start(bvb, bqkv[2 * H:3 * H].partition_broadcast(P)).then_inc(s_bias, 16)
            sp.dma_start(boutb, bout.partition_broadcast(P)).then_inc(s_bias, 16)
            sp.dma_start(wo_s, woutT.rearrange("(k p) n -> p k n", p=P)).then_inc(s_wo, 16)
            sp.dma_start(rw_s[:, :, :], rwT.rearrange("(k p) n -> p k n", p=P)).then_inc(s_wo, 16)
            for b in range(1, B):
                sp.dma_start(x_sb[:, TT * b:TT * (b + 1), :],
                             x[b].rearrange("(t p) n -> p t n", p=P)).then_inc(s_x[b], 16)
            sp.wait_ge(s_const, 2)
            sp.dma_start(xs_d.rearrange("(n p) w -> p n w", p=P),
                         fill.bitcast(U32).unsqueeze(1).to_broadcast([P, RT, ROW // 2])).then_inc(s_fill, 16)

            def stacks(b):
                r = b % 2
                sp.wait_ge(s_ql, 4 * (b + 1))
                if b == 0:
                    sp.wait_ge(s_const, 3)
                if b >= 2:
                    sp.wait_ge(s_pv, 16 * (b - 1))
                sp.dma_start(qk_d[r].rearrange("a (c p) n -> p (a c) n", p=P),
                             qk16.rearrange("p a c n -> p (a c) n")).then_inc(s_qkw[r], 16)
                sp.wait_ge(s_qkw[r], 16 * (b // 2 + 1))
                for par in range(2):
                    for a, parts in enumerate(((0, 0, 1), (2, 3, 2))):
                        for j, part in enumerate(parts):
                            src = qk_d[r, part].rearrange("(h two d) n -> two d h n", two=2, d=HD)
                            q0 = 64 * par + HD * j
                            dst = ks[r] if a else qs[r][:, :, par]
                            sp.dma_start(dst[q0:q0 + HD], src[par]).then_inc(s_stk[r], 16)

            def mod_rows(b):
                r = b % 2
                if b >= 2:
                    sp.wait_ge(s_h2, TT * (b - 1))
                sp.dma_start(bc[:, r, :], mod_d[b, 0:3 * H].partition_broadcast(P)).then_inc(s_bc[r], 16)

            def maxima(b):
                r = b % 2
                sp.wait_ge(s_neg, b + 1)
                sp.dma_start(ng_d[r], negm[:, :, :]).then_inc(s_ngw, 16)
                sp.wait_ge(s_ngw, 16 * (b + 1))
                src = ng_d[r].rearrange("(t two h) s q -> two s t h q", t=TT, two=2)
                for par in range(2):
                    for t in range(TT):
                        sp.dma_start(qs[r][P - 2:P, :, par, P * t:P * (t + 1)],
                                     src[par, :, t]).then_inc(s_ng[r], 16)

            def expert_load(n):
                e, u = unit_list[n]
                if n == 0:
                    sp.wait_ge(s_mp, 1)
                if n >= 3:
                    sp.wait_ge(s_el, n - 2)
                dst = stage[:, n % 3, :]
                s = s_eld[n % 3]
                if e == E:
                    if u < 2:
                        sp.dma_start(dst[:, 0:I], sgw[u * P:(u + 1) * P, :]).then_inc(s, 16)
                        sp.dma_start(dst[:, I:2 * I], suw[u * P:(u + 1) * P, :]).then_inc(s, 16)
                    else:
                        sp.dma_start(dst.rearrange("p (f n) -> p f n", f=FC),
                                     sdw.rearrange("(f p) n -> p f n", p=P)).then_inc(s, 32)
                elif u < 2:
                    sp.dma_start(dst, gu_v[e, u]).then_inc(s, 32)
                else:
                    sp.dma_start(dst.rearrange("p (f n) -> p f n", f=FC), dn_v[e]).then_inc(s, 32)

            sp.wait_ge(s_m4, 1)
            sp.dma_start(mod_d[:, :], m4[:, :]).then_inc(s_md, 16)
            sp.dma_start(gb_d[:, :], m4[:, 3 * H:4 * H]).then_inc(s_md, 16)
            sp.wait_ge(s_md, 32)
            mod_rows(0)
            mod_rows(1)
            stacks(0)
            for n in range(3):
                expert_load(n)
            stacks(1)
            maxima(0)
            for b in range(B):
                if b + 1 < B:
                    maxima(b + 1)
                if b + 2 < B:
                    stacks(b + 2)
                    mod_rows(b + 2)
                if b + 2 == B - 1:
                    for n in range(3, 6):
                        expert_load(n)
                    sp.wait_ge(s_xb, B)
                    sp.dma_start(gbb[:, :, :], mod_d[:, 3 * H:4 * H].partition_broadcast(P)).then_inc(s_gbb, 16)
            loaded = 6
            for b in range(B):
                while loaded < min(NU, 12 + 5 * (b + 1) + 3):
                    expert_load(loaded)
                    loaded += 1
                sp.wait_ge(s_x3, TT * (b + 1))
                sp.dma_start(out[b].rearrange("(t p) n -> p t n", p=P),
                             x_sb[:, TT * b:TT * (b + 1), :]).then_inc(s_out, 16)
            for r in range(RT):
                if r == 0:
                    sp.wait_ge(s_sct, 16 * NT)
                if r >= NT:
                    q = r - NT
                    sp.wait_ge(s_rhid, q + 1)
                    sp.wait_ge(s_rxt, q + 1)
                    sp.wait_ge(s_add, 16 * (q + 1))
                sp.dma_start(row[:, r % NT, :].bitcast(U32), xs_d[P * r:P * (r + 1), :]).then_inc(s_ld[r % NT], 16)

        @block.gpsimd
        def _(po):
            g = nc.gpsimd
            n_po = [0]

            def link(ins):
                n_po[0] += 1
                ins.then_inc(s_po, 1)
                po.wait_ge(s_po, n_po[0])

            link(g.memset(fill, 0.0))
            g.memset(fill[:, 514:516].bitcast(I32), OOB).then_inc(s_const, 1)
            link(g.memset(ident[:, :], 0.0))
            link(g.affine_select(out=ident[:, :], in_=ident[:, :], compare_op=ALU.not_equal, fill=1.0,
                                 base=0, pattern=[[-1, P]], channel_multiplier=1))
            g.tensor_copy(ident16[:, :], ident[:, :])
            g.memset(neghalf[:, :], -0.5).then_inc(s_const, 1)
            link(g.tensor_copy(identb[:, :], ident[:, :]))
            link(g.memset(maskb[:, :], 0.0))
            link(g.affine_select(out=maskb[:, :], in_=maskb[:, :], compare_op=ALU.is_ge, fill=NEG,
                                 base=0, pattern=[[-1, P]], channel_multiplier=1))
            for r in range(2):
                link(g.memset(qs[r].rearrange("p h two n -> p (h two n)").bitcast(F32), 0.0))
                for p0 in (32, 96):
                    link(g.memset(ks[r][p0:p0 + 32], 1.0))
            link(g.memset(v1[0], 1.0))
            g.memset(v1[1], 1.0).then_inc(s_const, 1)
            g.memset(ones16[:, :], 1.0)
            g.memset(onesE[:, :], 1.0)
            link(g.memset(tri16[:, :], 1.0))
            g.affine_select(out=tri16[:, :], in_=tri16[:, :], compare_op=ALU.is_ge, fill=0.0,
                            base=-1, pattern=[[1, P]], channel_multiplier=-1)
            g.iota(iw_i[:, :], pattern=[[-1, E]], base=E, channel_multiplier=0)
            g.iota(ij_i[:, :], pattern=[[P, NT]], base=0, channel_multiplier=0)
            link(g.iota(it_i[:, :], pattern=[[1, RT]], base=0, channel_multiplier=0))
            g.tensor_copy(iw[:, :], iw_i[:, :])
            g.tensor_copy(ij[:, :], ij_i[:, :])
            g.tensor_copy(it[:, :], it_i[:, :])
            g.iota(row32[:, :, 257].bitcast(I32), pattern=[[P, NT]], base=0, channel_multiplier=1)
            g.iota(row32[:, :, 258].bitcast(I32), pattern=[[1, B], [0, TT]], base=0, channel_multiplier=0)
            g.memset(row32[:, :, 259], 0.0).then_inc(s_const, 1)

            def rstd(ve, mv, rs, b, ready, done):
                c = slice(TT * b, TT * (b + 1))
                po.wait_ge(ready, b + 1)
                link(g.tensor_scalar(ve[:, c], mv[:, c, 1], EPS, 0.0, ALU.add, ALU.add))
                g.tensor_tensor(rs[:, c], ve[:, c], neghalf[:, :], ALU.pow).then_inc(done, 1)

            def project(b):
                rstd(ve1, mv1, rs1, b, s_mv, s_rstd)
                for k in range(KC):
                    po.wait_ge(s_h32, KC * b + k + 1)
                    if b and k == 0:
                        po.wait_ge(s_qkv, 6 * b)
                    g.tensor_tensor(h1[:, 1, k], h32[:, k], h1[:, 0, k], ALU.subtract).then_inc(s_h1l, 1)
                for u in range(4):
                    po.wait_ge(s_q32, 4 * b + u + 1)
                    if b and u == 0:
                        po.wait_ge(s_qkw[(b - 1) % 2], 16 * ((b - 1) // 2 + 1))
                    g.tensor_tensor(qk16[:, 2 * (u % 2) + 1, u // 2], q32[:, u % 2],
                                    qk16[:, 2 * (u % 2), u // 2], ALU.subtract).then_inc(s_ql, 1)

            def bias_x(b):
                po.wait_ge(s_bc[b % 2], 16 * (b // 2 + 1))
                po.wait_ge(s_xn, TT * (b + 1))
                if b == 0:
                    po.wait_ge(s_bias, 48)
                link(g.tensor_tensor(bga, boutb, bc[:, b % 2, 0:H], ALU.mult))
                for t in range(TT):
                    i = g.tensor_tensor(x_sb[:, TT * b + t], x_sb[:, TT * b + t], bga, ALU.add)
                link(i)
                g.tensor_copy(ve1[0:1, 0:1], ve1[0:1, 0:1]).then_inc(s_xb, 1)

            def masks(b, gr):
                for j in range(TT):
                    po.wait_ge(s_exp, 44 * b + UNITS * gr + CUM[j])
                    d = PT[j][:, :, 0:P]
                    g.affine_select(out=d, in_=d, compare_op=ALU.is_ge, fill=0.0, base=0,
                                    pattern=[[0, 4], [1, P]], channel_multiplier=-1).then_inc(s_msk, 1)

            def norm2(b):
                rstd(ve2, mv2, rs2, b, s_mv2, s_rstd2)
                for t in range(TT):
                    n = TT * b + t
                    po.wait_ge(s_hm, n + 1)
                    link(g.tensor_tensor(h2f[:, t], h2f[:, t], bc[:, b % 2, H:2 * H], ALU.add))
                    i = g.tensor_copy(row[:, n, 0:H], h2f[:, t])
                    i.then_inc(s_h2, 1)
                    po.wait_ge(s_h2, n + 1)
                    g.tensor_tensor(row[:, n, H:2 * H], h2f[:, t], row[:, n, 0:H],
                                    ALU.subtract).then_inc(s_rl, 1)

            for b in range(2):
                project(b)
                bias_x(b)
            for b in range(B):
                for gr in range(NG):
                    masks(b, gr)
                if b + 2 < B:
                    project(b + 2)
                norm2(b)
                if b + 2 < B:
                    bias_x(b + 2)
            done = 0
            for b in range(B):
                for t in range(TT):
                    n = TT * b + t
                    po.wait_ge(s_ye, n + 1)
                    g.tensor_tensor(x_sb[:, n], x_sb[:, n], yo[:, n % 2], ALU.add).then_inc(s_x3, 1)
                if b == 2:
                    po.wait_ge(s_pos, 1)
                    po.wait_ge(s_srow, 1)
                    po.wait_ge(s_fill, 16)
                    for n in range(NT):
                        g.indirect_dma_start(xs_d, bass.IndirectOffsetOnAxis(ap=pos_i[:, n:n + 1].bitcast(U32), axis=0),
                                             row[:, n, :].bitcast(U32), None).then_inc(s_sct, 16)

            def gate_rows(r):
                po.wait_ge(s_ld[r % NT], 16 * (r // NT + 1))
                if r == 0:
                    po.wait_ge(s_u, FC * B)
                if r >= GR:
                    po.wait_ge(s_rye, r - GR + 1)
                g.indirect_dma_start(gbr[r % GR], None, gb_d,
                                     bass.IndirectOffsetOnAxis(ap=row32[:, r % NT, 258:259].bitcast(U32), axis=0)
                                     ).then_inc(s_gbr[r % GR], 16)

            for r in range(4):
                gate_rows(r)
            po.wait_ge(s_out, 16 * B)
            for r in range(RT):
                po.wait_ge(s_rye, r + 1)
                g.indirect_dma_start(out.rearrange("b s n -> (b s) n"),
                                     bass.IndirectOffsetOnAxis(ap=row32[:, r % NT, 257:258].bitcast(U32), axis=0),
                                     ry[r % YR], None, bounds_check=B * S - 1, oob_is_err=False,
                                     compute_op=ALU.add).then_inc(s_add, 16)
                if r + 4 < RT:
                    gate_rows(r + 4)
                po.wait_ge(s_add, 16 * (r + 1))

        @block.scalar
        def _(ac):
            a = nc.scalar
            ac.wait_ge(s_c, 16)
            a.activation(cs[:, 1], cs[:, 0], ACT.Silu).then_inc(s_sc, 1)
            ac.wait_ge(s_wq, 16)
            a.activation(wq16[:, 0], wq_s, ACT.Copy, scale=WS).then_inc(s_wh, 1)
            ac.wait_ge(s_wo, 32)
            a.activation(wo16[:, 0], wo_s, ACT.Copy, scale=WS).then_inc(s_wh, 1)
            a.activation(rw16[:, 0], rw_s[:, :, :], ACT.Copy, scale=WS).then_inc(s_wh, 1)

            def project(b):
                for k in range(KC):
                    if k == 0:
                        ac.wait_ge(s_xt, b + 1)
                        if b == 0:
                            ac.wait_ge(s_m4, 1)
                        if b:
                            ac.wait_ge(s_qkv, 6 * b)
                    a.activation(h1[:, 0, k], MB[k][:, :], ACT.Identity, bias=sac[:, k, b:b + 1],
                                 scale=cac[:, k, b:b + 1]).then_inc(s_h1h, 1)
                for u in range(4):
                    ac.wait_ge(s_qkv, 6 * b + u + 1)
                    if b and u == 0:
                        ac.wait_ge(s_qkw[(b - 1) % 2], 16 * ((b - 1) // 2 + 1))
                    isk = u % 2
                    a.activation(qk16[:, 2 * isk, u // 2], SB[u % 2][:, :], ACT.Identity,
                                 bias=bqk[:, 2 * isk + u // 2:2 * isk + u // 2 + 1],
                                 scale=1.0 / WS if isk else 0.25 / WS).then_inc(s_qh, 1)

            def exps(b, gr):
                G = NG * b + gr
                for n, (j, i, m) in enumerate(KU):
                    N = 44 * b + UNITS * gr + n
                    w = S - P * j
                    ac.wait_ge(s_st, N + 1)
                    if i == 0 and G:
                        ac.wait_ge(s_pv, 4 * (G - 1) + j + 1)
                    a.activation(PT[j][:, i:i + m, :],
                                 TB[N % 3][:, 0:m * w].rearrange("p (i n) -> p i n", i=m),
                                 ACT.Exp).then_inc(s_exp, 1)
                    if n == 4 and gr:
                        outs(G - 1)

            def outs(G):
                ac.wait_ge(s_pv, 4 * G + 4)
                if G >= 2:
                    ac.wait_ge(s_rt, G - 1)
                a.activation(OTs[:, G % 2], OTb[:, :], ACT.Copy).then_inc(s_ote, 1)

            def attn_high(b):
                for k in range(KC):
                    ac.wait_ge(s_at, b + 1)
                    if b:
                        ac.wait_ge(s_o, TT * b)
                    a.activation(aT[:, 0, k], TB[k][:, :], ACT.Copy).then_inc(s_ath, 1)

            def h2_high(b):
                ac.wait_ge(s_ht, b + 1)
                a.activation(h2T[:, 0, :, S * b:S * (b + 1)],
                             T0[:, :].bitcast(F16).rearrange("p (k n) -> p k n", k=KC),
                             ACT.Copy).then_inc(s_hta, 1)

            def split_high(n):
                e, u = unit_list[n]
                ac.wait_ge(s_eld[n % 3], 32 * (n // 3 + 1))
                if n == 0:
                    ac.wait_ge(s_v, NT)
                    ac.wait_ge(s_qkw[1], 16 * 2)
                elif n == 6:
                    ac.wait_ge(s_pv, 16 * (B - 1))
                elif n == 12:
                    ac.wait_ge(s_pv, 16 * B)
                elif n == 18:
                    ac.wait_ge(s_o, NT)
                elif n == 24:
                    ac.wait_ge(s_rl, NT)
                c = place(e) + STEP * u
                a.activation(W[:, c:c + STEP], stage[:, n % 3, :],
                             ACT.Copy, scale=WS).then_inc(s_eh, 1)

            project(0)
            project(1)
            for b in range(B):
                for gr in range(NG):
                    exps(b, gr)
                    for n in early_splits(b, gr):
                        split_high(n)
                outs(NG * b + NG - 1)
                if b:
                    h2_high(b - 1)
                attn_high(b)
                if b + 2 < B:
                    project(b + 2)

            def hidden_high(n):
                ac.wait_ge(s_hid, n + 1)
                if n >= FC and n % FC == 0:
                    ac.wait_ge(s_y, TT * (n // FC))
                a.activation(hT[:, 0, n % FC], hid[:, n % 2], ACT.Copy).then_inc(s_hh, 1)

            split = 12
            for n in range(NT):
                ac.wait_ge(s_g, n + 1)
                if n >= 2:
                    ac.wait_ge(s_hid, n - 1)
                a.activation(g32[:, n % 2], [S0, M0][n % 2][:, :], ACT.Silu,
                             scale=1.0 / WS).then_inc(s_silu, 1)
                if n:
                    hidden_high(n - 1)
                if split < NU:
                    split_high(split)
                    split += 1
                if n == 3:
                    h2_high(B - 1)
                if n == 8:
                    ac.wait_ge(s_top, 1)
                    a.activation(srow[:, :], top[:, :], ACT.Sigmoid).then_inc(s_sg, 1)
            hidden_high(NT - 1)

            def routed_high(r):
                ac.wait_ge(s_rht, r + 1)
                if r >= 2:
                    ac.wait_ge(s_ry, r - 1)
                a.activation(rhT[:, r % 2, 0].rearrange("p f n -> p (f n)"), T1[:, :],
                             ACT.Copy).then_inc(s_rhh, 1)

            for r in range(RT + 1):
                if r:
                    routed_high(r - 1)
                if r < RT:
                    ac.wait_ge(s_rg, r + 1)
                    if r >= 2:
                        ac.wait_ge(s_rhid, r - 1)
                    a.activation(g32[:, r % 2], [S0, M0][r % 2][:, :], ACT.Silu,
                                 scale=row32[:, r % NT, 256:257]).then_inc(s_rsilu, 1)

        @block.vector
        def _(ve):
            v = nc.vector
            n_dv = [0]

            def link(ins):
                n_dv[0] += 1
                ins.then_inc(s_dv, 1)
                ve.wait_ge(s_dv, n_dv[0])

            def stats1(b):
                ve.wait_ge(s_x[b], 16)
                for t in range(TT):
                    i = v.bn_stats(st1[:, TT * b + t], x_sb[:, TT * b + t])
                link(i)
                for t in range(TT):
                    i = v.bn_aggr(mv1[:, TT * b + t], st1[:, TT * b + t])
                i.then_inc(s_mv, 1)

            def norm1(b):
                ve.wait_ge(s_rstd, b + 1)
                if b == 0:
                    ve.wait_ge(s_mv, 1)
                if b:
                    ve.wait_ge(s_xt, b)
                for t in range(TT):
                    n = TT * b + t
                    v.tensor_scalar(xn[:, t], x_sb[:, n], mv1[:, n, 0:1], rs1[:, n:n + 1],
                                    ALU.subtract, ALU.mult).then_inc(s_xn, 1)

            def project(b):
                stats1(b)
                norm1(b)
                if b == 0:
                    modulation()
                    low_parts()
                for k in range(KC):
                    ve.wait_ge(s_h1h, KC * b + k + 1)
                    if b and k == 0:
                        ve.wait_ge(s_ql, 4 * b)
                    v.tensor_scalar(h32[:, k], MB[k][:, :], cac[:, k, b:b + 1], sac[:, k, b:b + 1],
                                    ALU.mult, ALU.add).then_inc(s_h32, 1)
                for u in range(4):
                    ve.wait_ge(s_qh, 4 * b + u + 1)
                    if 4 * b + u >= 2:
                        ve.wait_ge(s_ql, 4 * b + u - 1)
                    isk = u % 2
                    v.tensor_scalar(q32[:, u % 2], SB[u % 2][:, :], 1.0 / WS if isk else 0.25 / WS,
                                    bqk[:, 2 * isk + u // 2:2 * isk + u // 2 + 1],
                                    ALU.mult, ALU.add).then_inc(s_q32, 1)
                for t in range(TT):
                    if t % 2 == 0:
                        ve.wait_ge(s_qkv, 6 * b + 5 + t // 2)
                    if t == 0 and b >= 2:
                        ve.wait_ge(s_pv, 16 * (b - 1))
                    dst = v1[b % 2][:, NH * 17 * t:NH * 17 * (t + 1)].rearrange("p (h d) -> p h d", d=17)
                    src = MB[t // 2][:, H * (t % 2):H * (t % 2 + 1)].rearrange("p (h d) -> p h d", d=HD)
                    v.scalar_tensor_tensor(dst[:, :, 0:HD], src, 1.0 / WS,
                                           bvb.rearrange("p (h d) -> p h d", d=HD),
                                           ALU.mult, ALU.add).then_inc(s_v, 1)

            def modulation():
                ve.wait_ge(s_mp, 1)
                v.tensor_copy(sac[:, :, :], T2[:, 0:8].rearrange("p (k b) -> p k b", k=KC))
                v.tensor_scalar(cac[:, :, :], T2[:, 8:16].rearrange("p (k b) -> p k b", k=KC),
                                1.0, None, ALU.add)
                v.tensor_copy(m4[:, H:2 * H], T0[0:B, H:2 * H])
                v.tensor_scalar(m4[:, 2 * H:3 * H], T1[0:B, 0:H], 1.0, None, ALU.add)
                for src, at_ in ((T0[0:B, 0:H], 0), (T1[0:B, H:2 * H], 3 * H)):
                    link(v.tensor_scalar(m4t[:, 0:H], src, 0.0, 2.0, ALU.is_ge, ALU.mult))
                    link(v.tensor_scalar(m4t[:, H:2 * H], src, -1.0, None, ALU.mult))
                    link(v.tensor_tensor(m4t[:, 2 * H:3 * H], src, m4t[:, H:2 * H], ALU.max))
                    link(v.tensor_scalar(m4t[:, 3 * H:4 * H], m4t[:, 2 * H:3 * H], 0.25, None, ALU.max))
                    link(v.scalar_tensor_tensor(m4[:, at_:at_ + H], m4t[:, 0:H], -1.0,
                                                m4t[:, 3 * H:4 * H], ALU.add, ALU.mult))
                ve.wait_ge(s_bias, 48)
                v.tensor_scalar(bqk[:, 0:2], bqk[:, 0:2], 0.25, None, ALU.mult).then_inc(s_m4, 1)
                ve.wait_ge(s_m4, 1)

            def low_parts():
                ve.wait_ge(s_wh, 1)
                v.scalar_tensor_tensor(wq16[:, 1], wq_s, WS, wq16[:, 0], ALU.mult,
                                       ALU.subtract).then_inc(s_wl, 1)
                ve.wait_ge(s_wh, 3)
                v.scalar_tensor_tensor(wo16[:, 1], wo_s, WS, wo16[:, 0], ALU.mult, ALU.subtract)
                v.scalar_tensor_tensor(rw16[:, 1], rw_s[:, :, :], WS, rw16[:, 0], ALU.mult,
                                       ALU.subtract).then_inc(s_wl, 1)

            def maxima(b, gr):
                for n, (t, i, m) in enumerate(QU):
                    N = 44 * b + UNITS * gr + n
                    w = P * (t + 1)
                    ve.wait_ge(s_s1, N + 1)
                    if gr == 0 and n == 0 and b >= 2:
                        ve.wait_ge(s_mt, b - 1)
                    par, hp0 = group_heads(gr)
                    c = NH * t + 8 * par + hp0 + i
                    v.tensor_reduce(mx[:, b % 2, c:c + m],
                                    SB[N % 2][:, 0:m * w].rearrange("p (i n) -> p i n", i=m),
                                    AX.X, ALU.max).then_inc(s_mx, 1)

            def negate(b):
                ve.wait_ge(s_mt, b + 1)
                if b:
                    ve.wait_ge(s_ngw, 16 * b)
                link(v.tensor_scalar(negm[:, 0], T2[0:64, 0:P], -1.0, None, ALU.mult))
                v.scalar_tensor_tensor(negm[:, 1], T2[0:64, 0:P], -1.0, negm[:, 0], ALU.mult,
                                       ALU.subtract).then_inc(s_neg, 1)

            def normalise(G):
                b, gr = G // NG, G % NG
                ve.wait_ge(s_rt, G + 1)
                if b and gr == 0:
                    ve.wait_ge(s_at, b)
                src = MB[G % 2][:, :].rearrange("p (t i d) -> p t i d", t=TT, i=4)
                r = rec[:, G % 2, :].rearrange("p (t i) -> p t i", t=TT)
                link(v.reciprocal(r, src[:, :, :, HD]))
                par, hp0 = group_heads(gr)
                dst = an.rearrange("p t (h two d) -> p two t h d", two=2, d=HD)[:, par, :, hp0:hp0 + 4]
                v.tensor_tensor(dst, src[:, :, :, 0:HD], r.unsqueeze(3).to_broadcast([P, TT, 4, HD]),
                                ALU.mult).then_inc(s_nrm, 1)

            def attn_low(b):
                for k in range(KC):
                    ve.wait_ge(s_ath, KC * b + k + 1)
                    if b and k == 0:
                        ve.wait_ge(s_o, TT * b)
                    v.tensor_tensor(aT[:, 1, k], TB[k][:, :], aT[:, 0, k], ALU.subtract).then_inc(s_atl, 1)

            def residual(b):
                ob = [T0, T1, S0, S1]
                for t in range(TT):
                    n = TT * b + t
                    ve.wait_ge(s_o, n + 1)
                    if t == 0:
                        ve.wait_ge(s_xb, b + 1)
                        if b:
                            ve.wait_ge(s_rl, TT * b)
                    link(v.scalar_tensor_tensor(o1[:, t], ob[t][:, 0:H], 1.0 / WS, bc[:, b % 2, 0:H],
                                                ALU.mult, ALU.mult))
                    v.tensor_tensor(x_sb[:, n], x_sb[:, n], o1[:, t], ALU.add).then_inc(s_x2, 1)
                ve.wait_ge(s_x2, TT * (b + 1))
                for t in range(TT):
                    i = v.bn_stats(st2[:, TT * b + t], x_sb[:, TT * b + t])
                link(i)
                for t in range(TT):
                    i = v.bn_aggr(mv2[:, TT * b + t], st2[:, TT * b + t])
                i.then_inc(s_mv2, 1)
                ve.wait_ge(s_mv2, b + 1)
                ve.wait_ge(s_rstd2, b + 1)
                for t in range(TT):
                    n = TT * b + t
                    link(v.tensor_scalar(h2f[:, t], x_sb[:, n], mv2[:, n, 0:1], rs2[:, n:n + 1],
                                         ALU.subtract, ALU.mult))
                    v.tensor_tensor(h2f[:, t], h2f[:, t], bc[:, b % 2, 2 * H:3 * H],
                                    ALU.mult).then_inc(s_hm, 1)

            def h2_low(b):
                ve.wait_ge(s_ht, b + 1)
                v.tensor_copy(h2T[:, 1, :, S * b:S * (b + 1)],
                              T1[:, :].bitcast(F16).rearrange("p (k n) -> p k n", k=KC)).then_inc(s_htd, 1)

            def logits(b):
                ve.wait_ge(s_r, b + 1)
                v.tensor_scalar(lg[:, TT * b:TT * (b + 1), :],
                                T2[:, 0:TT * E].rearrange("p (t e) -> p t e", t=TT), 1.0 / WS, None,
                                ALU.mult).then_inc(s_lg, 1)

            def split_low(n):
                e, u = unit_list[n]
                ve.wait_ge(s_eh, n + 1)
                c = place(e) + STEP * u
                v.scalar_tensor_tensor(W[:, c + WE:c + WE + STEP], stage[:, n % 3, :], WS,
                                       W[:, c:c + STEP], ALU.mult, ALU.subtract).then_inc(s_el, 1)

            project(0)
            project(1)
            for gr in range(NG):
                maxima(0, gr)
            negate(0)
            for b in range(B):
                for gr in range(NG):
                    if b + 1 < B:
                        maxima(b + 1, gr)
                    if gr:
                        normalise(NG * b + gr - 1)
                    for n in early_splits(b, gr):
                        split_low(n)
                if b:
                    h2_low(b - 1)
                    logits(b - 1)
                normalise(NG * b + NG - 1)
                attn_low(b)
                if b + 1 < B:
                    negate(b + 1)
                if b + 2 < B:
                    project(b + 2)
                residual(b)

            def hidden(n):
                ve.wait_ge(s_silu, n + 1)
                ve.wait_ge(s_u, n + 1)
                if n >= 2:
                    ve.wait_ge(s_hh, n - 1)
                    ve.wait_ge(s_hl, n - 1)
                v.scalar_tensor_tensor(hid[:, n % 2], [S1, M1][n % 2][:, :], 1.0 / WS, g32[:, n % 2],
                                       ALU.mult, ALU.mult).then_inc(s_hid, 1)

            def hidden_low(n):
                ve.wait_ge(s_hh, n + 1)
                ve.wait_ge(s_hid, n + 1)
                if n >= FC and n % FC == 0:
                    ve.wait_ge(s_y, TT * (n // FC))
                v.tensor_tensor(hT[:, 1, n % FC], hid[:, n % 2], hT[:, 0, n % FC], ALU.subtract).then_inc(s_hl, 1)

            def shared_out(b):
                for t in range(TT):
                    n = TT * b + t
                    ve.wait_ge(s_y, n + 1)
                    if n >= 2:
                        ve.wait_ge(s_x3, n - 1)
                    if n == 0:
                        ve.wait_ge(s_gbb, 16)
                    v.scalar_tensor_tensor(yo[:, n % 2], [T0, T1, T2, OTb][t][:, 0:H], 1.0 / WS,
                                           gbb[:, b], ALU.mult, ALU.mult).then_inc(s_ye, 1)

            def route():
                ve.wait_ge(s_lg, B)
                ve.wait_ge(s_const, 4)
                v.tensor_reduce(top[:, :], lg[:, :, :], AX.X, ALU.max).then_inc(s_top, 1)
                ve.wait_ge(s_top, 1)
                link(v.tensor_tensor(oh[:, :, :], lg[:, :, :], top[:, :].unsqueeze(2).to_broadcast([P, NT, E]),
                                     ALU.is_equal))
                link(v.tensor_tensor(ohw[:, :, :], oh[:, :, :], iw[:, :].unsqueeze(1).to_broadcast([P, NT, E]),
                                     ALU.mult))
                link(v.tensor_reduce(wtop[:, :], ohw[:, :, :], AX.X, ALU.max))
                link(v.tensor_tensor(oh[:, :, :], ohw[:, :, :], wtop[:, :].unsqueeze(2).to_broadcast([P, NT, E]),
                                     ALU.is_equal))
                v.tensor_copy(oh16[:, :, :], oh[:, :, :]).then_inc(s_oh, 1)

            def slots():
                ve.wait_ge(s_rank, 1)
                count = OTb[:, 0:E]
                rank = T2[:, 0:NT * E].rearrange("p (t e) -> p t e", t=NT)
                link(v.tensor_tensor(cmpc[:, :, :], count.unsqueeze(2).to_broadcast([P, E, NT]),
                                     ij[:, :].unsqueeze(1).to_broadcast([P, E, NT]), ALU.is_gt))
                link(v.tensor_reduce(ntile[:, :], cmpc[:, :, :], AX.X, ALU.add))
                link(v.tensor_tensor_scan(ends[:, :], onesE[:, :], ntile[:, :], 0.0, ALU.mult, ALU.add))
                link(v.tensor_tensor(base[:, :], ends[:, :], ntile[:, :], ALU.subtract))
                link(v.tensor_scalar(base[:, :], base[:, :], float(P), None, ALU.mult))
                link(v.tensor_tensor(posf[:, :, :], rank, base[:, :].unsqueeze(1).to_broadcast([P, NT, E]),
                                     ALU.add))
                link(v.tensor_tensor(posf[:, :, :], posf[:, :, :], oh[:, :, :], ALU.mult))
                link(v.tensor_reduce(posr[:, :], posf[:, :, :], AX.X, ALU.add))
                v.tensor_copy(pos_i[:, :], posr[:, :]).then_inc(s_pos, 1)
                link(v.tensor_tensor(tec[:, :, :], it[:, :].unsqueeze(2).to_broadcast([P, RT, E]),
                                     ends[:, :].unsqueeze(1).to_broadcast([P, RT, E]), ALU.is_ge))
                link(v.tensor_reduce(tef[:, :], tec[:, :, :], AX.X, ALU.add))
                link(v.tensor_scalar(tef[:, :], tef[:, :], -float(WX), float(E * WX), ALU.mult, ALU.add))
                v.tensor_copy(te_i[:, :], tef[:, :]).then_inc(s_te, 1)
                ve.wait_ge(s_sg, 1)
                v.tensor_scalar(row32[:, :, 256], srow[:, :], 1.0 / WS, None, ALU.mult).then_inc(s_srow, 1)

            split = 12
            for n in range(NT):
                b = n // FC
                hidden(n)
                if b and n % FC == 1:
                    shared_out(b - 1)
                if n:
                    hidden_low(n - 1)
                if split < NU:
                    split_low(split)
                    split += 1
                if n == 3:
                    h2_low(B - 1)
                    logits(B - 1)
                    route()
                if n == 9:
                    slots()
            hidden_low(NT - 1)
            shared_out(B - 1)

            def rows_in(r):
                ve.wait_ge(s_rxt, r + 1)
                if r >= 2:
                    ve.wait_ge(s_ru, r - 1)
                v.tensor_copy(xT[:, r % 2, 0:512], T0[:, 0:256].bitcast(F16)).then_inc(s_rxe, 1)

            def routed_low(r):
                ve.wait_ge(s_rhh, r + 1)
                v.tensor_tensor(rhT[:, r % 2, 1].rearrange("p f n -> p (f n)"), T1[:, :],
                                rhT[:, r % 2, 0].rearrange("p f n -> p (f n)"), ALU.subtract).then_inc(s_rhl, 1)

            def routed_out(r):
                ve.wait_ge(s_ry, r + 1)
                ve.wait_ge(s_gbr[r % GR], 16 * (r // GR + 1))
                if r >= YR:
                    ve.wait_ge(s_add, 16 * (r - YR + 1))
                v.scalar_tensor_tensor(ry[r % YR], [T2, OTb][r % 2][:, 0:H], 1.0 / WS, gbr[r % GR],
                                       ALU.mult, ALU.mult).then_inc(s_rye, 1)

            rows_in(0)
            for r in range(RT + 1):
                if r:
                    routed_low(r - 1)
                if r + 1 < RT:
                    rows_in(r + 1)
                if r >= 2:
                    routed_out(r - 2)
                if r < RT:
                    ve.wait_ge(s_ru, r + 1)
                    ve.wait_ge(s_rsilu, r + 1)
                    if r >= 2:
                        ve.wait_ge(s_rht, r - 1)
                    v.scalar_tensor_tensor(hid[:, r % 2], [S1, M1][r % 2][:, :], row32[:, r % NT, 256:257],
                                           g32[:, r % 2], ALU.mult, ALU.mult).then_inc(s_rhid, 1)
            routed_out(RT - 1)

        @block.tensor
        def _(pe):
            t_ = nc.tensor

            def split_mm(outp, pairs, **kw):
                prods = [p for (ah, al, bh, bl) in pairs for p in ((ah, bh), (ah, bl), (al, bh))]
                for n, (l, r) in enumerate(prods):
                    i = t_.matmul(outp, l, r, start=(n == 0), stop=(n == len(prods) - 1), **kw)
                return i

            def modulation():
                pe.wait_ge(s_sc, 1)
                pe.wait_ge(s_wm, 16)
                for c in range(4):
                    for k in range(KC):
                        t_.matmul(T2[:, 4 * c:4 * c + 4], wm[:, k, P * c:P * (c + 1)], cs[:, 1, k],
                                  start=(k == 0), stop=(k == KC - 1))
                for c, bk in enumerate((T0, T1)):
                    for k in range(KC):
                        i = t_.matmul(bk[0:B, :], cs[:, 1, k], wm[:, k, 512 * (c + 1):512 * (c + 2)],
                                      start=(k == 0), stop=(k == KC - 1))
                i.then_inc(s_mp, 1)

            def project(b):
                pe.wait_ge(s_xn, TT * (b + 1))
                if b == 0:
                    pe.wait_ge(s_const, 2)
                if b:
                    pe.wait_ge(s_v, TT * b)
                if b >= 2:
                    pe.wait_ge(s_nrm, NG * (b - 1))
                for k in range(KC):
                    for t in range(TT):
                        i = t_.transpose(MB[k][:, P * t:P * (t + 1)], xn[:, t, P * k:P * (k + 1)], ident[:, :])
                i.then_inc(s_xt, 1)
                if b == 0:
                    modulation()
                    pe.wait_ge(s_wl, 1)
                pe.wait_ge(s_h1l, KC * (b + 1))
                for u in range(4):
                    n = 4 * b + u
                    if n >= 2:
                        pe.wait_ge(s_q32, n - 1)
                    if u == 0 and b >= 2:
                        pe.wait_ge(s_mx, 44 * b)
                    c = H * (u % 2) + P * (u // 2)
                    split_mm(SB[u % 2][:, :],
                             [(wq16[:, 0, k, c:c + P], wq16[:, 1, k, c:c + P], h1[:, 0, k], h1[:, 1, k])
                              for k in range(KC)]).then_inc(s_qkv, 1)
                pe.wait_ge(s_h32, KC * (b + 1))
                for t in range(TT):
                    sl = slice(P * t, P * (t + 1))
                    i = split_mm(MB[t // 2][:, H * (t % 2):H * (t % 2 + 1)],
                                 [(h1[:, 0, k, sl], h1[:, 1, k, sl], wq16[:, 0, k, 2 * H:3 * H],
                                   wq16[:, 1, k, 2 * H:3 * H]) for k in range(KC)])
                    if t % 2:
                        i.then_inc(s_qkv, 1)

            def scores(b, gr, n):
                N = 44 * b + UNITS * gr + n
                t, i0, m = QU[n]
                r = b % 2
                par, hp0 = group_heads(gr)
                if gr == 0 and n == 0:
                    pe.wait_ge(s_stk[r], 16 * 12 * (b // 2 + 1))
                    pe.wait_ge(s_q32, 4 * (last_p(max(b - 1, 0)) + 1))
                    if b == 0:
                        pe.wait_ge(s_const, 3)
                    if b >= 2:
                        pe.wait_ge(s_x2, TT * (b - 1))
                if N >= 2:
                    pe.wait_ge(s_mx, N - 1)
                w = P * (t + 1)
                bk = SB[N % 2]
                for i in range(m):
                    hp = hp0 + i0 + i
                    t_.matmul(bk[:, w * i:w * (i + 1)], qs[r][0:P - 2, hp, par, P * t:w],
                              ks[r][0:P - 2, hp, 0:w], start=(i == 0), stop=False, skip_group_check=True)
                t_.matmul(bk[:, 0:m * w].rearrange("p (i n) -> p i n", i=m)[:, :, w - P:w], identb[:, :],
                          maskb[:, :].unsqueeze(1).to_broadcast([P, m, P]), start=False, stop=True,
                          skip_group_check=True).then_inc(s_s1, 1)

            def max_turn(b):
                pe.wait_ge(s_mx, 44 * (b + 1))
                if b:
                    pe.wait_ge(s_exp, 44 * b)
                if b >= 2:
                    pe.wait_ge(s_lg, b - 1)
                t_.transpose(T2[0:64, 0:P], mx[:, b % 2], ident[:, :]).then_inc(s_mt, 1)

            def scores_t(b, gr, n):
                N = 44 * b + UNITS * gr + n
                j, i0, m = KU[n]
                r = b % 2
                par, hp0 = group_heads(gr)
                if gr == 0 and n == 0:
                    pe.wait_ge(s_ng[r], 16 * 2 * TT * (b // 2 + 1))
                    pe.wait_ge(s_neg, b + 1)
                    if b:
                        pe.wait_ge(s_x2, TT * b)
                if N >= 3:
                    pe.wait_ge(s_exp, N - 2)
                w = S - P * j
                for i in range(m):
                    hp = hp0 + i0 + i
                    q = t_.matmul(TB[N % 3][:, w * i:w * (i + 1)], ks[r][:, hp, P * j:P * (j + 1)],
                                  qs[r][:, hp, par, P * j:S], start=True, stop=True)
                q.then_inc(s_st, 1)

            def values(G, j):
                b, gr = G // NG, G % NG
                if gr == 0 and j == 0:
                    pe.wait_ge(s_v, TT * (b + 1))
                if j == 0 and G:
                    pe.wait_ge(s_ote, G)
                pe.wait_ge(s_msk, 4 * G + j + 1)
                par, hp0 = group_heads(gr)
                for i in range(4):
                    h = 2 * (hp0 + i) + par
                    c = 17 * (NH * j + h)
                    q = t_.matmul(OTb[32 * i:32 * i + 32, P * j:S], v1[b % 2][:, c:c + 32], PT[j][:, i],
                                  start=(j == 0), stop=(j == TT - 1), tile_position=(0, 32 * i),
                                  skip_group_check=True)
                q.then_inc(s_pv, 1)

            def turn_out(G):
                pe.wait_ge(s_ote, G + 1)
                if G >= 2:
                    pe.wait_ge(s_nrm, G - 1)
                if G % NG == 0:
                    pe.wait_ge(s_v, TT * (last_p(G // NG) + 1))
                for t in range(TT):
                    q = t_.transpose(MB[G % 2][:, P * t:P * (t + 1)], OTs[:, G % 2, P * t:P * (t + 1)], ident[:, :])
                q.then_inc(s_rt, 1)

            def attend(b):
                for gr in range(NG):
                    G = NG * b + gr
                    for n in range(UNITS):
                        scores_t(b, gr, n)
                        if b + 1 < B:
                            scores(b + 1, gr, n)
                        if n == 1 and gr:
                            values(G - 1, 2)
                        if n == 3 and gr:
                            values(G - 1, 3)
                        if n == 6 and gr:
                            turn_out(G - 1)
                        if n == 8:
                            values(G, 0)
                        if n == 10:
                            values(G, 1)
                values(NG * b + NG - 1, 2)
                values(NG * b + NG - 1, 3)

            def attn_turn(b):
                turn_out(NG * b + NG - 1)
                pe.wait_ge(s_nrm, NG * (b + 1))
                pe.wait_ge(s_exp, 44 * (b + 1))
                if b:
                    pe.wait_ge(s_htd, b)
                    pe.wait_ge(s_hta, b)
                for k in range(KC):
                    for t in range(TT):
                        q = t_.transpose(TB[k][:, P * t:P * (t + 1)], an[:, t, P * k:P * (k + 1)], ident[:, :])
                q.then_inc(s_at, 1)

            def output(b):
                pe.wait_ge(s_atl, KC * (b + 1))
                if b == 0:
                    pe.wait_ge(s_wl, 2)
                for t, bk in enumerate((T0, T1, S0, S1)):
                    if t == 2:
                        pe.wait_ge(s_q32, 4 * (min(b + 2, B - 1) + 1))
                        pe.wait_ge(s_mx, 44 * (min(b + 1, B - 1) + 1))
                    sl = slice(P * t, P * (t + 1))
                    split_mm(bk[:, 0:H], [(aT[:, 0, k, sl], aT[:, 1, k, sl], wo16[:, 0, k], wo16[:, 1, k])
                                          for k in range(KC)]).then_inc(s_o, 1)

            def h2_turn(b):
                pe.wait_ge(s_rl, TT * (b + 1))
                pe.wait_ge(s_exp, 44 * min(b + 2, B))
                pe.wait_ge(s_x2, TT * (b + 1))
                for part, bk in enumerate((T0, T1)):
                    o = bk[:, :].bitcast(F16)
                    for k in range(KC):
                        for t in range(TT):
                            q = t_.transpose(o[:, S * k + P * t:S * k + P * (t + 1)],
                                             row[:, TT * b + t, H * part + P * k:H * part + P * (k + 1)],
                                             ident16[:, :])
                q.then_inc(s_ht, 1)

            def router(b):
                pe.wait_ge(s_hta, b + 1)
                pe.wait_ge(s_htd, b + 1)
                for t in range(TT):
                    sl = slice(S * b + P * t, S * b + P * (t + 1))
                    q = split_mm(T2[:, E * t:E * (t + 1)],
                                 [(h2T[:, 0, k, sl], h2T[:, 1, k, sl], rw16[:, 0, k], rw16[:, 1, k])
                                  for k in range(KC)])
                q.then_inc(s_r, 1)

            project(0)
            project(1)
            for gr in range(NG):
                for n in range(UNITS):
                    scores(0, gr, n)
            max_turn(0)
            for b in range(B):
                attend(b)
                if b:
                    h2_turn(b - 1)
                    router(b - 1)
                attn_turn(b)
                if b + 1 < B:
                    max_turn(b + 1)
                if b + 2 < B:
                    project(b + 2)
                output(b)

            def we(e, part, k_or_f, lo, n, is_down=False):
                c = place(e) + part * WE + (KC * 2 * I + H * k_or_f if is_down else 2 * I * k_or_f) + lo
                return W[:, c:c + n]

            def shared_up(n):
                b, f = n // FC, n % FC
                tok = slice(S * b, S * (b + 1))
                gk, uk = (S0, S1) if n % 2 == 0 else (M0, M1)
                if n == 0:
                    pe.wait_ge(s_el, 3)
                    pe.wait_ge(s_x2, TT * B)
                if n == 1:
                    pe.wait_ge(s_nrm, NG * B)
                if n >= 2:
                    pe.wait_ge(s_hid, n - 1)
                for half, bk, s in ((0, gk, s_g), (I, uk, s_u)):
                    split_mm(bk[:, :], [(we(E, 0, k, half + P * f, P), we(E, 1, k, half + P * f, P),
                                         h2T[:, 0, k, tok], h2T[:, 1, k, tok])
                                        for k in range(KC)]).then_inc(s, 1)

            def shared_down(b):
                pe.wait_ge(s_hl, FC * (b + 1))
                for t, bk in enumerate((T0, T1, T2, OTb)):
                    if b:
                        pe.wait_ge(s_ye, TT * (b - 1) + t + 1)
                    elif t == 0:
                        pe.wait_ge(s_lg, B)
                        pe.wait_ge(s_htd, B)
                        pe.wait_ge(s_hta, B)
                    sl = slice(P * t, P * (t + 1))
                    split_mm(bk[:, 0:H], [(hT[:, 0, f, sl], hT[:, 1, f, sl], we(E, 0, f, 0, H, True),
                                           we(E, 1, f, 0, H, True)) for f in range(FC)]).then_inc(s_y, 1)

            def ranks():
                pe.wait_ge(s_oh, 1)
                pe.wait_ge(s_ye, TT * 2)
                rank = T2[:, 0:NT * E]
                t_.matmul(rank, tri16[:, :], oh16[:, :, :].rearrange("p t e -> p (t e)"), start=True,
                          stop=False, skip_group_check=True)
                for t in range(NT - 1):
                    m = NT - 1 - t
                    t_.matmul(rank[:, E * (t + 1):].rearrange("p (t e) -> p t e", t=m), ones16[:, :],
                              oh16[:, t:t + 1, :].to_broadcast([P, m, E]), start=False, stop=(t == NT - 2),
                              skip_group_check=True)
                for t in range(NT):
                    q = t_.matmul(OTb[:, 0:E], ones16[:, :], oh16[:, t], start=(t == 0), stop=(t == NT - 1))
                q.then_inc(s_rank, 1)

            for n in range(NT):
                b = n // FC
                shared_up(n)
                if n == 3:
                    h2_turn(B - 1)
                    router(B - 1)
                if b and n % FC == 1:
                    if b - 1 == 2:
                        pe.wait_ge(s_pos, 1)
                    shared_down(b - 1)
                if n == 10:
                    ranks()
            shared_down(B - 1)

            def rows_turn(r):
                pe.wait_ge(s_ld[r % NT], 16 * (r // NT + 1))
                if r:
                    pe.wait_ge(s_rxe, r)
                else:
                    pe.wait_ge(s_ye, NT)
                o = T0[:, 0:256].bitcast(F16)
                for c in range(4):
                    q = t_.transpose(o[:, P * c:P * (c + 1)], row[:, r % NT, P * c:P * (c + 1)], ident16[:, :])
                q.then_inc(s_rxt, 1)

            def up_half(r, off, half, bk, s):
                pairs = []
                for k in range(KC):
                    c = 2 * I * k + half
                    pairs.append((xT[:, r % 2, P * k:P * (k + 1)], xT[:, r % 2, 256 + P * k:256 + P * (k + 1)],
                                  W[:, bass.ds(off + c, I)], W[:, bass.ds(off + (c + WE), I)]))
                split_mm(bk[:, :], pairs).then_inc(s, 1)

            def hidden_turn(r):
                pe.wait_ge(s_rhid, r + 1)
                if r:
                    pe.wait_ge(s_rhl, r)
                for f in range(FC):
                    q = t_.transpose(T1[:, P * f:P * (f + 1)], hid[:, r % 2, P * f:P * (f + 1)], ident[:, :])
                q.then_inc(s_rht, 1)

            def down_rows(r, off):
                pe.wait_ge(s_rhl, r + 1)
                if r >= 2:
                    pe.wait_ge(s_rye, r - 1)
                pairs = []
                for f in range(FC):
                    c = KC * 2 * I + H * f
                    pairs.append((rhT[:, r % 2, 0, f], rhT[:, r % 2, 1, f],
                                  W[:, bass.ds(off + c, H)], W[:, bass.ds(off + (c + WE), H)]))
                split_mm([T2, OTb][r % 2][:, 0:H], pairs).then_inc(s_ry, 1)

            rows_turn(0)
            pe.wait_ge(s_te, 1)
            pe.wait_ge(s_el, NU)
            offs = {}
            for r in range(RT + 1):
                if r:
                    hidden_turn(r - 1)
                if r < RT:
                    offs[r] = t_.value_load(te_i[0:1, r:r + 1], min_val=0, max_val=E * WX)
                    pe.wait_ge(s_rxe, r + 1)
                    if r >= 2:
                        pe.wait_ge(s_rhid, r - 1)
                    elif r == 0:
                        pe.wait_ge(s_hid, NT)
                    gk, uk = (S0, S1) if r % 2 == 0 else (M0, M1)
                    up_half(r, offs[r], 0, gk, s_rg)
                    if r + 1 < RT:
                        rows_turn(r + 1)
                    up_half(r, offs[r], I, uk, s_ru)
                if r:
                    down_rows(r - 1, offs[r - 1])


_INS = ["x", "wqkvT", "bqkv", "bqkc", "woutT", "bout", "rwT", "gup", "down", "sgw", "suw", "sdw", "cT", "wmod"]


def kernel(L0_attn_x, L0_attn_Wqkv, L0_attn_bqkv, L0_attn_Wout, L0_attn_bout, L0_ffn_router_w,
           L0_ffn_gate_up_proj, L0_ffn_down_proj, L0_ffn_shared_gate_w, L0_ffn_shared_up_w,
           L0_ffn_shared_down_w, L0_c, L0_wmod):
    import concourse.bacc as bacc
    from concourse.bass_utils import run_bass_kernel_spmd

    given = dict(x=L0_attn_x, wqkvT=np.asarray(L0_attn_Wqkv).T, bqkv=L0_attn_bqkv,
                 bqkc=np.asarray(L0_attn_bqkv)[:2 * H].reshape(4, P).T,
                 woutT=np.asarray(L0_attn_Wout).T, bout=L0_attn_bout,
                 rwT=np.asarray(L0_ffn_router_w).T, gup=L0_ffn_gate_up_proj, down=L0_ffn_down_proj,
                 sgw=L0_ffn_shared_gate_w, suw=L0_ffn_shared_up_w, sdw=L0_ffn_shared_down_w,
                 cT=np.asarray(L0_c).T, wmod=L0_wmod)
    nc = bacc.Bacc("TRN2", target_bir_lowering=False, num_devices=1)
    arrays, args = {}, []
    for name in _INS:
        a = np.ascontiguousarray(given[name])
        arrays["in_" + name] = a
        args.append(nc.dram_tensor("in_" + name, a.shape, mybir.dt.from_np(a.dtype), kind="ExternalInput").ap())
    args.append(nc.dram_tensor("out_0", (B, S, H), F32, kind="ExternalOutput").ap())
    build(nc, *args)
    r = run_bass_kernel_spmd(nc, [arrays], core_ids=[0])
    return r.results[0]["out_0"]
```

```python
import numpy as np
import concourse.bass as bass
from concourse import mybir
from contextlib import ExitStack

F32, F16, BF16, I32 = mybir.dt.float32, mybir.dt.float16, mybir.dt.bfloat16, mybir.dt.int32
U32 = mybir.dt.uint32
ALU = mybir.AluOpType
ACT = mybir.ActivationFunctionType
AX = mybir.AxisListType

P = 128
B, S, H = 4, 512, 256
NH, HD = 16, 16
E, I = 8, 512
TT = S // P
NT = B * TT
KC = H // P
FC = I // P
RT = NT + E - 1
WS = 64.0
EPS = 1e-5
WE = KC * 2 * I + FC * H
WX = 2 * WE
ROW = 520
OOB = 1 << 20
NEG = -1e30
UNITS = 11
BU = 4 * UNITS
CUM = [4, 8, 10, 11]
STEP = 1024
GR = 4
YR = 4
NEAR = 3
GAP = 10240
SPLIT_AT = 5
DEEP = 1
POOL_UNITS = (9, 11, 13, 15)
NG = 4


def group_heads(g):
    return g % 2, 4 * (g // 2)


def place(e):
    return (E - e) * WX + (GAP if E - e >= NEAR else 0)


def query_units():
    return [(0, 0, 4), (1, 0, 2), (1, 2, 2)] + [(t, i, 1) for t in (2, 3) for i in range(4)]


def key_units():
    return [(0, i, 1) for i in range(4)] + [(1, i, 1) for i in range(4)] + [(2, 0, 2), (2, 2, 2), (3, 0, 4)]


SIDE = [(1, "max", 0, 1), (4, "v", 1, 0), (5, "stats1", 2, 0), (6, "v", 1, 1),
        (9, "attn", -1, 0), (10, "norm1", 2, 0), (11, "attn", -1, 1),
        (14, "turn", 2, 0), (16, "turn", 2, 1), (19, "out", -1, 0), (21, "out", -1, 1),
        (22, "stats2", -1, 0), (23, "qk", 2, 0), (25, "scale2", -1, 0), (25, "qk", 2, 1), (26, "max", 1, 0),
        (27, "scale2", -1, 1), (28, "parts2", -1, 0), (29, "scale2", -1, 2), (29, "qk", 2, 2),
        (30, "parts2", -1, 1), (31, "scale2", -1, 3), (31, "qk", 2, 3), (33, "parts2", -1, 2),
        (35, "parts2", -1, 3), (20, "bias", 0, 0), (38, "h2", -1, 0), (40, "h2", -1, 1),
        (42, "route", -1, 0)]


LAST = [(3, "up", 0, 0), (7, "hidden", 0, 0), (8, "up", 0, 1), (12, "hidden", 0, 1), (13, "up", 0, 2),
        (17, "hidden", 0, 2), (18, "up", 0, 3), (24, "hidden", 0, 3), (28, "down", 0, 0),
        (31, "down", 0, 1)]


def side_jobs(b, n):
    early = 6 if b < 0 else 0
    jobs = [(job, b + d, part) for at, job, d, part in SIDE
            if at - (min(early, at - 2) if d == 2 else 0) == n and 0 <= b + d < B]
    if b == B - 1:
        jobs += [(job, c, part) for at, job, c, part in LAST if at == n]
    return jobs


def build(nc, x, wqkvT, bqkv, bqkc, woutT, bout, rwT, gup, down, sgw, suw, sdw, cT, wmod, out):
    ctx = ExitStack()
    with ctx:
        def sb(name, shape, dt=F32):
            return ctx.enter_context(nc.sbuf_tensor(name, shape, dt))

        def sem(name):
            return ctx.enter_context(nc.semaphore(name))

        qk_d = nc.dram_tensor("qk_d", [2, 2, NH, 3, HD, S], F16).ap()
        ng_d = nc.dram_tensor("ng_d", [2, 2, 2, 32, P], F16).ap()
        mod_d = nc.dram_tensor("mod_d", [B, 4 * H], F32).ap()
        gb_d = nc.dram_tensor("gb_d", [B, H], F32).ap()
        xs_d = nc.dram_tensor("xs_d", [RT * P, ROW // 2], U32).ap()

        W = sb("W", [P, (E + 1) * WX + GAP], F16)
        x_sb = sb("x_sb", [P, NT, H])
        row = sb("row", [P, NT, ROW], F16)
        row32 = row[:, :, :].bitcast(F32)
        h2T = sb("h2T", [P, 2, KC, B * S], F16)
        stage = sb("stage", [P, 3, STEP])
        ffn = W[:, NEAR * WX:NEAR * WX + GAP].bitcast(F32)
        probs = W[:, (E + 1) * WX:(E + 1) * WX + GAP].bitcast(F32)
        gbb = sb("gbb", [P, B, H])
        boutb = sb("boutb", [P, H])[:, :]
        bga = sb("bga", [P, H])[:, :]
        ident = sb("ident", [P, P])
        ident16 = sb("ident16", [P, P], F16)
        identb = sb("identb", [P, P], BF16)
        maskb = sb("maskb", [P, P], BF16)
        tri16 = sb("tri16", [P, P], F16)
        ones16 = sb("ones16", [P, P], F16)
        neghalf = sb("neghalf", [P, TT])
        iw_i = sb("iw_i", [P, E], I32)
        ij_i = sb("ij_i", [P, NT], I32)
        it_i = sb("it_i", [P, RT], I32)
        iw = sb("iw", [P, E])
        ij = sb("ij", [P, NT])
        it = sb("it", [P, RT])
        cs = sb("cs", [P, 2, KC, B])
        sac = sb("sac", [P, KC, B])
        cac = sb("cac", [P, KC, B])
        bqk = sb("bqk", [P, 4])
        st1 = sb("st1", [P, NT, 6])
        mv1 = sb("mv1", [P, NT, 2])
        ve1 = sb("ve1", [P, NT])
        rs1 = sb("rs1", [P, NT])
        st2 = sb("st2", [P, NT, 6])
        mv2 = sb("mv2", [P, NT, 2])
        ve2 = sb("ve2", [P, NT])
        rs2 = sb("rs2", [P, NT])
        rw_s = sb("rw_s", [P, KC, E])
        rw16 = sb("rw16", [P, 2, KC, E], F16)
        lg = sb("lg", [P, NT, E])
        mx = sb("mx", [P, 2, 2, 32])
        mx_v = mx[:, :, :, :].rearrange("p r f (two i t) -> p r f two i t", two=2, i=4)
        negm = sb("negm", [32, 2, P], F16)
        rec = sb("rec", [P, 2, NH])
        top = sb("top", [P, NT])
        oh = sb("oh", [P, NT, E])
        ohw = sb("ohw", [P, NT, E])
        wtop = sb("wtop", [P, NT])
        oh16 = sb("oh16", [P, NT, E], F16)
        cmpc = sb("cmpc", [P, E, NT])
        ntile = sb("ntile", [P, E])
        onesE = sb("onesE", [P, E])
        ends = sb("ends", [P, E])
        base = sb("base", [P, E])
        posf = sb("posf", [P, NT, E])
        posr = sb("posr", [P, NT])
        pos_i = sb("pos_i", [P, NT], I32)
        tec = sb("tec", [P, RT, E])
        tef = sb("tef", [P, RT])
        te_i = sb("te_i", [P, RT], I32)
        teg = sb("teg", [P, RT])
        srow = sb("srow", [P, NT])
        fillb = sb("fillb", [P, ROW], F16)
        fill = fillb[:, :]

        at = [0]

        def early(cols, dt=F32):
            n = cols * (2 if dt == F32 else 1)
            v = W[:, at[0]:at[0] + n]
            at[0] += n
            return v.bitcast(F32) if dt == F32 else v

        wq16 = early(2 * KC * 3 * H, F16).rearrange("p (s k n) -> p s k n", s=2, k=KC)
        xn = early(TT * H).rearrange("p (t n) -> p t n", t=TT)
        h1 = early(2 * KC * S, F16).rearrange("p (s k n) -> p s k n", s=2, k=KC)
        h32 = early(KC * S).rearrange("p (k n) -> p k n", k=KC)
        q32 = h32
        bvb = early(H)
        qk16 = early(4 * 2 * S, F16).rearrange("p (a c n) -> p a c n", a=4, c=2)
        qs, ks, v1 = [], [], []
        for _ in range(2):
            qs.append(early(NH * S, F16).rearrange("p (h two n) -> p h two n", two=2, n=S))
            ks.append(early(NH // 2 * S, F16).rearrange("p (h n) -> p h n", n=S))
            v1.append(early(TT * NH * 17 + 16))
        wo16 = early(2 * KC * H, F16).rearrange("p (s k n) -> p s k n", s=2, k=KC)
        OTs = early(2 * S).rearrange("p (r n) -> p r n", r=2)
        an = early(TT * H).rearrange("p (t n) -> p t n", t=TT)
        aT = early(2 * KC * S, F16).rearrange("p (s k n) -> p s k n", s=2, k=KC)
        bc = early(2 * 3 * H).rearrange("p (r n) -> p r n", r=2)
        o1 = early(TT * H).rearrange("p (t n) -> p t n", t=TT)
        h2f = o1
        assert at[0] <= (E + 1) * WX
        pt_at = [0, 4 * 512, 4 * 896, 4 * 1152]
        PT = [probs[:, pt_at[j]:pt_at[j] + 4 * (S - P * j)].rearrange("p (i n) -> p i n", i=4)
              for j in range(TT)]
        wm = stage[:, :, :].rearrange("p a b -> p (a b)").rearrange("p (k n) -> p k n", k=KC)
        hs = h2T[:, :, :, :].rearrange("p a b c -> p (a b c)").bitcast(F32)
        wq_s = hs[:, 0:KC * 3 * H].rearrange("p (k n) -> p k n", k=KC)
        wo_s = hs[:, KC * 3 * H:KC * 4 * H].rearrange("p (k n) -> p k n", k=KC)
        m4 = hs[0:B, KC * 4 * H:KC * 4 * H + 4 * H]
        mraw = hs[0:B, 0:4 * H]
        m4t = hs[0:B, KC * 6 * H:KC * 6 * H + 2 * H]
        g32 = ffn[:, 0:2 * I].rearrange("p (r n) -> p r n", r=2)
        hid = ffn[:, 2 * I:4 * I].rearrange("p (r n) -> p r n", r=2)
        hT = ffn[:, 4 * I:8 * I].bitcast(F16).rearrange("p (s f n) -> p s f n", s=2, f=FC)
        yo = ffn[:, 8 * I:9 * I].rearrange("p (r n) -> p r n", r=2)
        xT = [h2T[:, 0, n, 3 * S:4 * S] for n in range(2)]
        gbr = [h2T[:, n // 2, n % 2, S:2 * S].bitcast(F32) for n in range(GR)]
        ry = [h2T[:, n // 2, n % 2, 2 * S:3 * S].bitcast(F32) for n in range(YR)]
        rhT = hT.rearrange("p s f n -> p (s f n)").rearrange("p (r s f n) -> p r s f n", r=4, s=2, f=FC)[:, 0:2]

        bank = [ctx.enter_context(nc.psum_tensor(f"bank{i}", [P, 512], F32)) for i in range(8)]
        S0, S1, T0, T1, T2, OTb, M0, M1 = bank
        SB = [S0, S1, T2]

        def t_bank(N):
            return [T0, T1][N % 2] if N < BU * (B - 1) else [T0, T1, T2][N % 3]

        s_const = sem("s_const")
        s_c = sem("s_c")
        s_wm = sem("s_wm")
        s_wmr = sem("s_wmr")
        s_wq = sem("s_wq")
        s_wo = sem("s_wo")
        s_bias = sem("s_bias")
        s_x = [sem(f"s_xin{b}") for b in range(B)]
        s_sc = sem("s_sc")
        s_mc = sem("s_mc")
        s_col = sem("s_col")
        s_zero = sem("s_zero")
        s_mp = sem("s_mp")
        s_mr = sem("s_mr")
        s_m4 = sem("s_m4")
        s_md = sem("s_md")
        s_bc = [sem(f"s_bc{r}") for r in range(2)]
        s_gbb = sem("s_gbb")
        s_wh = sem("s_wh")
        s_wl = sem("s_wl")
        s_mv = sem("s_mv")
        s_rstd = sem("s_rstd")
        s_xn = sem("s_xn")
        s_xt = sem("s_xt")
        s_h1h = sem("s_h1h")
        s_h32 = sem("s_h32")
        s_h1l = sem("s_h1l")
        s_qkv = sem("s_qkv")
        s_qh = sem("s_qh")
        s_q32 = sem("s_q32")
        s_ql = sem("s_ql")
        s_v = sem("s_v")
        s_xb = sem("s_xb")
        s_qkw = [[sem(f"s_qkw{r}_{f}") for f in range(2)] for r in range(2)]
        s_stk = [[sem(f"s_stk{r}_{f}") for f in range(2)] for r in range(2)]
        s_s1 = sem("s_s1")
        s_mx = sem("s_mx")
        s_mt = sem("s_mt")
        s_neg = sem("s_neg")
        s_ngw = sem("s_ngw")
        s_ng = [[sem(f"s_ng{r}_{f}") for f in range(2)] for r in range(2)]
        s_st = sem("s_st")
        s_exp = sem("s_exp")
        s_msk = sem("s_msk")
        s_pv = sem("s_pv")
        s_ote = sem("s_ote")
        s_rt = sem("s_rt")
        s_nrm = sem("s_nrm")
        s_at = sem("s_at")
        s_ath = sem("s_ath")
        s_atl = sem("s_atl")
        s_o = sem("s_o")
        s_x2 = sem("s_x2")
        s_mv2 = sem("s_mv2")
        s_rstd2 = sem("s_rstd2")
        s_hm = sem("s_hm")
        s_h2 = sem("s_h2")
        s_h2v = sem("s_h2v")
        s_rh = sem("s_rh")
        s_rl = sem("s_rl")
        s_ht = sem("s_ht")
        s_hta = sem("s_hta")
        s_htd = sem("s_htd")
        s_r = sem("s_r")
        s_lg = sem("s_lg")
        s_dv = sem("s_dv")
        s_po = sem("s_po")
        s_eld = [sem(f"s_eld{r}") for r in range(4)]
        s_eh = sem("s_eh")
        s_el = sem("s_el")
        s_elp = sem("s_elp")
        s_g = sem("s_g")
        s_u = sem("s_u")
        s_silu = sem("s_silu")
        s_hid = sem("s_hid")
        s_hh = sem("s_hh")
        s_hl = sem("s_hl")
        s_y = sem("s_y")
        s_ye = sem("s_ye")
        s_x3 = sem("s_x3")
        s_out = sem("s_out")
        s_fill = sem("s_fill")
        s_oh = sem("s_oh")
        s_rank = sem("s_rank")
        s_pos = sem("s_pos")
        s_te = sem("s_te")
        s_top = sem("s_top")
        s_sg = sem("s_sg")
        s_srow = sem("s_srow")
        s_sct = sem("s_sct")
        s_ld = [sem(f"s_ld{r}") for r in range(NT)]
        s_gbr = [sem(f"s_gbr{r}") for r in range(GR)]
        s_rxt = sem("s_rxt")
        s_rxe = sem("s_rxe")
        s_rg = sem("s_rg")
        s_ru = sem("s_ru")
        s_rsilu = sem("s_rsilu")
        s_rhid = sem("s_rhid")
        s_rht = sem("s_rht")
        s_rhh = sem("s_rhh")
        s_rhl = sem("s_rhl")
        s_ry = sem("s_ry")
        s_rye = sem("s_rye")
        s_add = sem("s_add")

        QU, KU = query_units(), key_units()

        def side_bank(job, c, k):
            tail = {"attn": [T0, T1], "out": [T2, OTb], "h2": [T0, T1], "route": [T2]}
            head = {"turn": [M1, M0], "qk": [M1, M0, S0, S1]}
            if c == 0 and job in head:
                return head[job][k]
            return tail[job][k] if c == B - 1 and job in tail else M1

        def released(job, c, k):
            return {"down": (s_ye, TT * c + 2 * (k + 1)),
                    "max": (s_neg, 2 * c + k + 1), "v": (s_v, TT * c + 2 * (k + 1)),
                    "attn": (s_atl, KC * c + k + 1), "turn": (s_h32, KC * c + k + 1),
                    "out": (s_x2, TT * c + 2 * (k + 1)), "qk": (s_q32, 4 * c + k + 1),
                    "h2": ((s_hta, s_htd)[k % 2], c + 1), "route": (s_lg, c + 1)}[job]

        unit_list = [(E - i, u) for i in (0, 1, 2, 3, 4, 8, 5, 6, 7) for u in range(3)]

        def split_done(n):
            by_pool = n in POOL_UNITS
            return (s_elp if by_pool else s_el,
                    sum((m in POOL_UNITS) == by_pool for m in range(n + 1)))

        def slot(n):
            return n % 3 if n < 12 else (n - 12) % 4

        def staged(n):
            if slot(n) < 3:
                return stage[:, slot(n), :].rearrange("p (s n) -> p s n", s=4)
            return h2T[:, :, :, 0:S].bitcast(F32).rearrange("p a k n -> p (a k) n")

        def loaded_count(n):
            return 32 * sum(slot(m) == slot(n) for m in range(n + 1))

        def weights(n, part):
            e, u = unit_list[n]
            c = place(e) + STEP * u + part * WE
            return W[:, c:c + STEP].rearrange("p (s n) -> p s n", s=4)

        def up_banks(n):
            return (S0, S1) if n < FC * DEEP or n % 2 == 0 else (M0, M1)
        NU = len(unit_list)

        def early_splits(b, gr):
            if b == B - 2:
                return range(gr, gr + 1) if gr < 3 else range(0)
            if b == B - 1:
                return range(3 + 2 * gr, 5 + 2 * gr) if gr < 3 else range(0)
            return range(0)

        def ffn_splits(n):
            return (2, 1, 1, 1, 1, 1, 2, 2, 2, 2, 2, 1)[n - FC * DEEP]

        gu_v = gup.rearrange("e (k p) n -> e k p n", p=P)
        dn_v = down.rearrange("e (f p) n -> e p f n", p=P)

        block = ctx.enter_context(nc.Block())

        @block.sync
        def _(sp):
            sp.dma_start(x_sb[:, 0:TT, :], x[0].rearrange("(t p) n -> p t n", p=P)).then_inc(s_x[0], 16)
            sp.dma_start(cs[:, 0], cT.rearrange("(k p) b -> p k b", p=P)).then_inc(s_c, 16)
            wmod_v = wmod.rearrange("(k p) n -> p k n", p=P)
            sp.dma_start(wm[:, :, 0:2 * H], wmod_v[:, :, 0:2 * H]).then_inc(s_wm, 16)
            sp.dma_start(wq_s, wqkvT.rearrange("(k p) n -> p k n", p=P)).then_inc(s_wq, 16)
            sp.dma_start(bqk[:, :], bqkc).then_inc(s_bias, 16)
            sp.dma_start(bvb, bqkv[2 * H:3 * H].partition_broadcast(P)).then_inc(s_bias, 16)
            sp.dma_start(boutb, bout.partition_broadcast(P)).then_inc(s_bias, 16)
            sp.dma_start(wm[:, :, 2 * H:6 * H], wmod_v[:, :, 2 * H:6 * H]).then_inc(s_wmr, 16)
            sp.dma_start(wo_s, woutT.rearrange("(k p) n -> p k n", p=P)).then_inc(s_wo, 16)
            sp.dma_start(rw_s[:, :, :], rwT.rearrange("(k p) n -> p k n", p=P)).then_inc(s_wo, 16)
            for b in range(1, B):
                sp.dma_start(x_sb[:, TT * b:TT * (b + 1), :],
                             x[b].rearrange("(t p) n -> p t n", p=P)).then_inc(s_x[b], 16)

            def qk_out(b, f):
                r = b % 2
                for a, j, part in ((0, 0, 0), (0, 2, 0), (1, 0, 2), (1, 1, 2), (0, 1, 1), (1, 2, 3)):
                    if (a, j) == (0, 0):
                        sp.wait_ge(s_qh, 4 * b + 2 * (f + 1))
                    if (a, j) == (0, 1):
                        sp.wait_ge(s_ql, 4 * b + 2 * (f + 1))
                    sp.dma_start(qk_d[r, a, 8 * f:8 * f + 8, j], qk16[:, part, f]).then_inc(s_qkw[r][f], 16)

            def stacks(b, f):
                r = b % 2
                sp.wait_ge(s_qkw[r][f], 16 * 6 * (b // 2 + 1))
                if b == 0 and f == 0:
                    sp.wait_ge(s_zero, 1)
                if b == 1 and f == 0:
                    sp.wait_ge(s_const, 4)
                    sp.wait_ge(s_zero, 2)
                if b >= 2:
                    sp.wait_ge(s_st, BU * (b - 2) + BU // 2 * (f + 1))
                hp = slice(4 * f, 4 * f + 4)
                for par in range(2):
                    for a, dst in ((0, qs[r][:, :, par]), (1, ks[r])):
                        src = qk_d[r, a].rearrange("(h two) j d n -> two (j d) h n", two=2)[par]
                        sp.dma_start(dst[64 * par:64 * par + 3 * HD, hp], src[:, hp]).then_inc(s_stk[r][f], 16)

            def mod_rows(b):
                r = b % 2
                if b >= 2:
                    sp.wait_ge(s_rl, TT * (b - 1))
                sp.dma_start(bc[:, r, :], mod_d[b, 0:3 * H].partition_broadcast(P)).then_inc(s_bc[r], 16)

            def maxima_out(b, f):
                sp.wait_ge(s_neg, 2 * b + f + 1)
                sp.dma_start(ng_d[b % 2, f].rearrange("s p q -> p s q"), negm[:, :, :]).then_inc(s_ngw, 16)

            def maxima(b, f):
                r = b % 2
                sp.wait_ge(s_ngw, 16 * (2 * b + f + 1))
                src = ng_d[r, f].rearrange("s (two i t) q -> two s i (t q)", two=2, i=4)
                for par in range(2):
                    sp.dma_start(qs[r][P - 2:P, 4 * f:4 * f + 4, par], src[par]).then_inc(s_ng[r][f], 16)

            def expert_load(n):
                e, u = unit_list[n]
                if n == 0:
                    sp.wait_ge(s_mp, 1)
                before = [m for m in range(n) if slot(m) == slot(n)]
                if before:
                    sp.wait_ge(*split_done(before[-1]))
                elif n >= 12:
                    sp.wait_ge(s_u, FC)
                dst, s = staged(n), s_eld[slot(n)]
                if e == E and u < 2:
                    dst = dst.rearrange("p s n -> p (s n)")
                    sp.dma_start(dst[:, 0:I], sgw[u * P:(u + 1) * P, :]).then_inc(s, 16)
                    sp.dma_start(dst[:, I:2 * I], suw[u * P:(u + 1) * P, :]).then_inc(s, 16)
                elif e == E:
                    sp.dma_start(dst, sdw.rearrange("(f p) n -> p f n", p=P)).then_inc(s, 32)
                elif u < 2:
                    sp.dma_start(dst, gu_v[e, u].rearrange("p (s n) -> p s n", s=4)).then_inc(s, 32)
                else:
                    sp.dma_start(dst, dn_v[e]).then_inc(s, 32)

            qk_out(0, 0)
            stacks(0, 0)
            qk_out(0, 1)
            stacks(0, 1)
            loaded = 0
            for b in range(-1, B):
                if b >= 0:
                    maxima_out(b, 1)
                    maxima(b, 1)
                if 0 <= b < B - 1:
                    if b == 0:
                        sp.wait_ge(s_const, 5)
                    tiles = slice(8 * b, min(RT, 8 * (b + 1)))
                    sp.dma_start(xs_d.rearrange("(n p) w -> p n w", p=P)[:, tiles],
                                 fill.bitcast(U32).unsqueeze(1).to_broadcast([P, tiles.stop - tiles.start, ROW // 2])
                                 ).then_inc(s_fill, 16)
                while loaded < {-1: 0, 0: 3, 1: 3, 2: 6, 3: 12}[b]:
                    expert_load(loaded)
                    loaded += 1
                if b < 0:
                    qk_out(1, 0)
                    stacks(1, 0)
                if b + 1 < B:
                    maxima_out(b + 1, 0)
                    maxima(b + 1, 0)
                if 2 <= b + 2 < B:
                    qk_out(b + 2, 0)
                    stacks(b + 2, 0)
                if b + 2 < B:
                    qk_out(b + 2, 1)
                if 0 < b + 1 < B:
                    mod_rows(b + 1)
                if b + 2 < B:
                    stacks(b + 2, 1)
                if b < 0:
                    sp.wait_ge(s_m4, 1)
                    sp.dma_start(mod_d[:, :], m4[:, :]).then_inc(s_md, 16)
                    sp.dma_start(gb_d[:, :], m4[:, 3 * H:4 * H]).then_inc(s_md, 16)
                    sp.wait_ge(s_md, 32)
                    mod_rows(0)
                    sp.dma_start(gbb[:, :, :], mod_d[:, 3 * H:4 * H].partition_broadcast(P)).then_inc(s_gbb, 16)

            def result(b):
                sp.wait_ge(s_x3, TT * (b + 1))
                sp.dma_start(out[b].rearrange("(t p) n -> p t n", p=P),
                             x_sb[:, TT * b:TT * (b + 1), :]).then_inc(s_out, 16)

            for b in range(DEEP):
                result(b)
            for n in range(loaded, NU):
                expert_load(n)
            sp.wait_ge(s_sct, 16 * NT)
            for r in range(NT):
                sp.dma_start(row[:, r, :].bitcast(U32), xs_d[P * r:P * (r + 1), :]).then_inc(s_ld[r], 16)
            for b in range(DEEP, B):
                result(b)
            for r in range(NT, RT):
                q = r - NT
                sp.wait_ge(s_rhid, q + 1)
                sp.wait_ge(s_rxt, q + 1)
                sp.wait_ge(s_add, 16 * (q + 1))
                sp.dma_start(row[:, q, :].bitcast(U32), xs_d[P * r:P * (r + 1), :]).then_inc(s_ld[q], 16)

        @block.gpsimd
        def _(po):
            g = nc.gpsimd
            n_po = [0]

            def link(ins):
                n_po[0] += 1
                ins.then_inc(s_po, 1)
                po.wait_ge(s_po, n_po[0])

            link(g.memset(ident[:, :], 0.0))
            link(g.affine_select(out=ident[:, :], in_=ident[:, :], compare_op=ALU.not_equal, fill=1.0,
                                 base=0, pattern=[[-1, P]], channel_multiplier=1))
            g.tensor_copy(ident16[:, :], ident[:, :])
            g.memset(neghalf[:, :], -0.5).then_inc(s_const, 1)
            po.wait_ge(s_const, 1)

            def constants():
                link(g.tensor_copy(identb[:, :], ident[:, :]))
                link(g.memset(maskb[:, :], 0.0))
                g.affine_select(out=maskb[:, :], in_=maskb[:, :], compare_op=ALU.is_ge, fill=NEG,
                                base=0, pattern=[[-1, P]], channel_multiplier=1).then_inc(s_const, 1)
                po.wait_ge(s_const, 2)
                link(g.memset(v1[0], 1.0))
                g.memset(v1[1], 1.0).then_inc(s_const, 1)
                po.wait_ge(s_const, 3)
                g.memset(qs[1].rearrange("p h two n -> p (h two n)").bitcast(F32), 0.0).then_inc(s_const, 1)
                po.wait_ge(s_const, 4)
                link(g.memset(fill, 0.0))
                g.memset(fill[:, 514:516].bitcast(I32), OOB).then_inc(s_const, 1)
                g.memset(ones16[:, :], 1.0)
                g.memset(onesE[:, :], 1.0)
                link(g.memset(tri16[:, :], 1.0))
                g.affine_select(out=tri16[:, :], in_=tri16[:, :], compare_op=ALU.is_ge, fill=0.0,
                                base=-1, pattern=[[1, P]], channel_multiplier=-1)
                g.iota(iw_i[:, :], pattern=[[-1, E]], base=E, channel_multiplier=0)
                g.iota(ij_i[:, :], pattern=[[P, NT]], base=0, channel_multiplier=0)
                link(g.iota(it_i[:, :], pattern=[[1, RT]], base=0, channel_multiplier=0))
                g.tensor_copy(iw[:, :], iw_i[:, :])
                g.tensor_copy(ij[:, :], ij_i[:, :])
                g.tensor_copy(it[:, :], it_i[:, :])
                g.iota(row32[:, :, 257].bitcast(I32), pattern=[[P, NT]], base=0, channel_multiplier=1)
                g.iota(row32[:, :, 258].bitcast(I32), pattern=[[1, B], [0, TT]], base=0, channel_multiplier=0)
                link(g.memset(row32[:, :, 259], 0.0))

            def rstd(ve, mv, rs, b, ready, done):
                c = slice(TT * b, TT * (b + 1))
                po.wait_ge(ready, b + 1)
                link(g.tensor_scalar(ve[:, c], mv[:, c, 1], EPS, 0.0, ALU.add, ALU.add))
                g.tensor_tensor(rs[:, c], ve[:, c], neghalf[:, :], ALU.pow).then_inc(done, 1)

            def modulation_rows(part):
                if part == 0:
                    po.wait_ge(s_mr, 2)
                    g.tensor_copy(m4[:, H:2 * H], mraw[:, H:2 * H])
                    g.tensor_scalar(m4[:, 2 * H:3 * H], mraw[:, 2 * H:3 * H], 1.0, 0.0, ALU.add, ALU.add)
                gate = slice(3 * H * part, 3 * H * part + H)
                sign, size = m4t[:, 0:H], m4t[:, H:2 * H]
                link(g.tensor_scalar(sign, mraw[:, gate], 0.0, 2.0, ALU.is_ge, ALU.mult))
                link(g.tensor_scalar(sign, sign, -1.0, 0.0, ALU.add, ALU.add))
                link(g.tensor_tensor(size, mraw[:, gate], sign, ALU.mult))
                link(g.tensor_scalar(size, size, 0.25, 0.0, ALU.max, ALU.add))
                i = g.tensor_tensor(m4[:, gate], sign, size, ALU.mult)
                if part == 0:
                    link(i)
                else:
                    i.then_inc(s_m4, 1)
                    po.wait_ge(s_m4, 1)

            def h_low(b, k):
                po.wait_ge(s_h32, KC * b + k + 1)
                if b and k == 0:
                    po.wait_ge(s_qkv, 6 * b)
                g.tensor_tensor(h1[:, 1, k], h32[:, k], h1[:, 0, k], ALU.subtract).then_inc(s_h1l, 1)

            def qk_low(b, u):
                po.wait_ge(s_q32, 4 * b + u + 1)
                if b and u % 2 == 0:
                    po.wait_ge(s_qkw[(b - 1) % 2][u // 2], 16 * 6 * ((b - 1) // 2 + 1))
                g.tensor_tensor(qk16[:, 2 * (u % 2) + 1, u // 2], q32[:, u % 2],
                                qk16[:, 2 * (u % 2), u // 2], ALU.subtract).then_inc(s_ql, 1)

            def bias_x(b):
                po.wait_ge(s_bc[b % 2], 16 * (b // 2 + 1))
                po.wait_ge(s_xn, TT * (b + 1))
                if b == 0:
                    po.wait_ge(s_bias, 48)
                link(g.tensor_tensor(bga, boutb, bc[:, b % 2, 0:H], ALU.mult))
                for t in range(TT):
                    i = g.tensor_tensor(x_sb[:, TT * b + t], x_sb[:, TT * b + t], bga, ALU.add)
                link(i)
                g.tensor_copy(ve1[0:1, 0:1], ve1[0:1, 0:1]).then_inc(s_xb, 1)

            def mask(G, j):
                po.wait_ge(s_exp, UNITS * G + CUM[j])
                d = PT[j][:, :, 0:P]
                g.affine_select(out=d, in_=d, compare_op=ALU.is_ge, fill=0.0, base=0,
                                pattern=[[0, 4], [1, P]], channel_multiplier=-1).then_inc(s_msk, 1)

            def modulate2(b, t):
                po.wait_ge(s_hm, TT * b + t + 1 - (2 if b == B - 1 else 0))
                link(g.tensor_tensor(h2f[:, t], h2f[:, t], bc[:, b % 2, 2 * H:3 * H], ALU.mult))
                g.tensor_tensor(h2f[:, t], h2f[:, t], bc[:, b % 2, H:2 * H], ALU.add).then_inc(s_h2, 1)

            def split_low(n):
                po.wait_ge(s_eh, n + 1)
                link(g.tensor_scalar(staged(n), staged(n), WS, 0.0, ALU.mult, ALU.add))
                g.tensor_tensor(weights(n, 1), staged(n), weights(n, 0), ALU.subtract).then_inc(s_elp, 1)

            rstd(ve1, mv1, rs1, 0, s_mv, s_rstd)
            h_low(0, 0)
            h_low(0, 1)
            for u in range(4):
                qk_low(0, u)
            constants()
            for b in range(-1, B):
                for n in range(BU):
                    if b < 0 and n in (14, 26):
                        modulation_rows(n == 26)
                    if b >= 0 and n % UNITS + 1 in CUM:
                        mask(NG * b + n // UNITS, CUM.index(n % UNITS + 1))
                    if n % UNITS == (SPLIT_AT if b == B - 1 else 8):
                        for u in early_splits(b, n // UNITS):
                            if u in POOL_UNITS:
                                split_low(u)
                    for job, c, k in side_jobs(b, n):
                        if job == "stats1":
                            rstd(ve1, mv1, rs1, c, s_mv, s_rstd)
                        elif job == "turn":
                            h_low(c, k)
                        elif job == "qk":
                            qk_low(c, k)
                        elif job == "stats2":
                            rstd(ve2, mv2, rs2, c, s_mv2, s_rstd2)
                        elif job == "scale2":
                            modulate2(c, k)
                        elif job == "bias":
                            bias_x(c)
            split_low(9)
            rstd(ve2, mv2, rs2, B - 1, s_mv2, s_rstd2)
            for t in (2, 3):
                modulate2(B - 1, t)
            for n in (11, 13, 15):
                split_low(n)
            po.wait_ge(s_pos, 1)
            po.wait_ge(s_srow, 1)
            po.wait_ge(s_fill, 16 * (B - 1))
            for n in range(NT):
                g.indirect_dma_start(xs_d, bass.IndirectOffsetOnAxis(ap=pos_i[:, n:n + 1].bitcast(U32), axis=0),
                                     row[:, n, :].bitcast(U32), None).then_inc(s_sct, 16)

            def gate_rows(r):
                po.wait_ge(s_ld[r % NT], 16 * (r // NT + 1))
                if r == 0:
                    po.wait_ge(s_u, FC * B)
                if r >= GR:
                    po.wait_ge(s_rye, r - GR + 1)
                g.indirect_dma_start(gbr[r % GR], None, gb_d,
                                     bass.IndirectOffsetOnAxis(ap=row32[:, r % NT, 258:259].bitcast(U32), axis=0)
                                     ).then_inc(s_gbr[r % GR], 16)

            for r in range(4):
                gate_rows(r)
            po.wait_ge(s_out, 16 * B)
            for r in range(RT):
                po.wait_ge(s_rye, r + 1)
                g.indirect_dma_start(out.rearrange("b s n -> (b s) n"),
                                     bass.IndirectOffsetOnAxis(ap=row32[:, r % NT, 257:258].bitcast(U32), axis=0),
                                     ry[r % YR], None, bounds_check=B * S - 1, oob_is_err=False,
                                     compute_op=ALU.add).then_inc(s_add, 16)
                if r + 4 < RT:
                    gate_rows(r + 4)
                po.wait_ge(s_add, 16 * (r + 1))

        @block.scalar
        def _(ac):
            a = nc.scalar
            ac.wait_ge(s_c, 16)
            a.activation(cs[:, 1], cs[:, 0], ACT.Silu).then_inc(s_sc, 1)
            ac.wait_ge(s_wq, 16)
            a.activation(wq16[:, 0], wq_s, ACT.Copy, scale=WS).then_inc(s_wh, 1)

            def other_high():
                ac.wait_ge(s_wo, 32)
                a.activation(wo16[:, 0], wo_s, ACT.Copy, scale=WS).then_inc(s_wh, 1)
                a.activation(rw16[:, 0], rw_s[:, :, :], ACT.Copy, scale=WS).then_inc(s_wh, 1)

            def h_parts(b, k):
                ac.wait_ge(s_xt, KC * b + k + 1)
                if b == 0 and k == 0:
                    ac.wait_ge(s_col, 1)
                if b and k == 0:
                    ac.wait_ge(s_qkv, 6 * b)
                    ac.wait_ge(s_ql, 4 * b)
                for dst, s in ((h1[:, 0, k], s_h1h), (h32[:, k], s_h32)):
                    a.activation(dst, side_bank("turn", b, k)[:, :], ACT.Identity, bias=sac[:, k, b:b + 1],
                                 scale=cac[:, k, b:b + 1]).then_inc(s, 1)

            def qk_parts(b, u):
                ac.wait_ge(s_qkv, 6 * b + u + 1)
                if b and u % 2 == 0:
                    ac.wait_ge(s_qkw[(b - 1) % 2][u // 2], 16 * 6 * ((b - 1) // 2 + 1))
                if u >= 2:
                    ac.wait_ge(s_ql, 4 * b + u - 1)
                else:
                    ac.wait_ge(s_h1l, KC * (b + 1))
                isk = u % 2
                for dst, s in ((qk16[:, 2 * isk, u // 2], s_qh), (q32[:, u % 2], s_q32)):
                    a.activation(dst, side_bank("qk", b, u)[:, :], ACT.Identity,
                                 bias=bqk[:, 2 * isk + u // 2:2 * isk + u // 2 + 1],
                                 scale=1.0 / WS if isk else 0.25 / WS).then_inc(s, 1)

            def exps(N):
                G, n = N // UNITS, N % UNITS
                j, i, m = KU[n]
                w = S - P * j
                ac.wait_ge(s_st, N + 1)
                if i == 0 and G:
                    ac.wait_ge(s_pv, 4 * (G - 1) + j + 1)
                a.activation(PT[j][:, i:i + m, :],
                             t_bank(N)[:, 0:m * w].rearrange("p (i n) -> p i n", i=m),
                             ACT.Exp).then_inc(s_exp, 1)

            def outs(G):
                ac.wait_ge(s_pv, 4 * G + 4)
                if G >= 2:
                    ac.wait_ge(s_rt, G - 1)
                a.activation(OTs[:, G % 2], OTb[:, :], ACT.Copy).then_inc(s_ote, 1)

            def attn_high(b, k):
                ac.wait_ge(s_at, KC * b + k + 1)
                if b and k == 0:
                    ac.wait_ge(s_o, TT * b)
                a.activation(aT[:, 0, k], side_bank("attn", b, k)[:, :], ACT.Copy).then_inc(s_ath, 1)

            def rows_high(b, t):
                n = TT * b + t
                if b == B - 1 and t < 2:
                    ac.wait_ge(s_h2v, t + 1)
                elif b == B - 1:
                    ac.wait_ge(s_h2, n - 1)
                else:
                    ac.wait_ge(s_h2, n + 1)
                a.activation(row[:, n, 0:H], h2f[:, t], ACT.Copy).then_inc(s_rh, 1)

            def h2_high(b):
                ac.wait_ge(s_ht, 2 * b + 1)
                a.activation(h2T[:, 0, :, S * b:S * (b + 1)],
                             side_bank("h2", b, 0)[:, :].bitcast(F16).rearrange("p (k n) -> p k n", k=KC),
                             ACT.Copy).then_inc(s_hta, 1)

            def split_high(n):
                ac.wait_ge(s_eld[slot(n)], loaded_count(n))
                if n == 0:
                    ac.wait_ge(s_v, NT)
                    ac.wait_ge(s_qkw[1][0], 16 * 12)
                    ac.wait_ge(s_qkw[1][1], 16 * 12)
                elif n == 6:
                    ac.wait_ge(s_pv, 16 * (B - 1))
                elif n == 9:
                    ac.wait_ge(s_pv, 16 * B)
                elif n == 18:
                    ac.wait_ge(s_o, NT)
                elif n == 21:
                    ac.wait_ge(s_rl, NT)
                a.activation(weights(n, 0), staged(n), ACT.Copy, scale=WS).then_inc(s_eh, 1)

            def silu(n):
                ac.wait_ge(s_g, n + 1)
                if n == 0:
                    ac.wait_ge(s_pv, 16 * (B - 1))
                if n >= 2:
                    ac.wait_ge(s_hid, n - 1)
                deep = n < FC * DEEP
                a.activation(g32[:, n % 2], up_banks(n)[0][:, :], ACT.Tanh if deep else ACT.Silu,
                             scale=0.5 / WS if deep else 1.0 / WS).then_inc(s_silu, 1)

            def hidden_high(n):
                ac.wait_ge(s_hid, n + 1)
                if n >= FC and n % FC == 0:
                    ac.wait_ge(s_y, TT * (n // FC))
                a.activation(hT[:, 0, n % FC], hid[:, n % 2], ACT.Copy).then_inc(s_hh, 1)

            h_parts(0, 0)
            h_parts(0, 1)
            for u in range(4):
                qk_parts(0, u)
            ac.wait_ge(s_mp, 1)
            ac.wait_ge(s_wl, 1)
            for c, bk in enumerate((T0, T1)):
                a.activation(mraw[:, 512 * c:512 * (c + 1)], bk[0:B, :], ACT.Copy).then_inc(s_mr, 1)
            other_high()
            for b in range(-1, B):
                for n in range(BU):
                    G = NG * b + n // UNITS
                    if b >= 0:
                        exps(BU * b + n)
                    if n % UNITS == 4 and G > 0:
                        outs(G - 1)
                    for job, c, k in side_jobs(b, n):
                        if job == "turn":
                            h_parts(c, k)
                        elif job == "qk":
                            qk_parts(c, k)
                        elif job == "attn":
                            attn_high(c, k)
                        elif job == "parts2":
                            rows_high(c, k)
                        elif job == "h2" and k == 0:
                            h2_high(c)
                        elif job == "up":
                            silu(FC * c + k)
                        elif job == "hidden":
                            hidden_high(FC * c + k)
                    if n % UNITS == (SPLIT_AT if b == B - 1 else 8):
                        for u in early_splits(b, n // UNITS):
                            split_high(u)
            outs(NG * B - 1)

            split = 9
            for n in range(FC * DEEP, NT):
                silu(n)
                if n == 9:
                    ac.wait_ge(s_top, 1)
                    a.activation(srow[:, :], top[:, :], ACT.Sigmoid).then_inc(s_sg, 1)
                if n > FC * DEEP:
                    hidden_high(n - 1)
                if n == 4:
                    attn_high(B - 1, 0)
                    attn_high(B - 1, 1)
                if n == 6:
                    for t in range(TT):
                        rows_high(B - 1, t)
                if n == 8:
                    h2_high(B - 1)
                for _ in range(ffn_splits(n)):
                    split_high(split)
                    split += 1
            hidden_high(NT - 1)

            def routed_high(r):
                ac.wait_ge(s_rht, r + 1)
                if r >= 2:
                    ac.wait_ge(s_ry, r - 1)
                a.activation(rhT[:, r % 2, 0].rearrange("p f n -> p (f n)"), T1[:, :],
                             ACT.Copy).then_inc(s_rhh, 1)

            for r in range(RT + 1):
                if r:
                    routed_high(r - 1)
                if r < RT:
                    ac.wait_ge(s_rg, r + 1)
                    if r >= 2:
                        ac.wait_ge(s_rhid, r - 1)
                    a.activation(g32[:, r % 2], [S0, M0][r % 2][:, :], ACT.Silu,
                                 scale=row32[:, r % NT, 256:257]).then_inc(s_rsilu, 1)

        @block.vector
        def _(ve):
            v = nc.vector
            n_dv = [0]

            def link(ins):
                n_dv[0] += 1
                ins.then_inc(s_dv, 1)
                ve.wait_ge(s_dv, n_dv[0])

            def stats1(b):
                ve.wait_ge(s_x[b], 16)
                for t in range(TT):
                    i = v.bn_stats(st1[:, TT * b + t], x_sb[:, TT * b + t])
                link(i)
                for t in range(TT):
                    i = v.bn_aggr(mv1[:, TT * b + t], st1[:, TT * b + t])
                i.then_inc(s_mv, 1)

            def norm1(b):
                ve.wait_ge(s_rstd, b + 1)
                ve.wait_ge(s_mv, b + 1)
                if b:
                    ve.wait_ge(s_xt, KC * b)
                for t in range(TT):
                    n = TT * b + t
                    v.tensor_scalar(xn[:, t], x_sb[:, n], mv1[:, n, 0:1], rs1[:, n:n + 1],
                                    ALU.subtract, ALU.mult).then_inc(s_xn, 1)

            def v_out(b, k):
                ve.wait_ge(s_qkv, 6 * b + 5 + k)
                if k == 0 and b == 0:
                    ve.wait_ge(s_const, 3)
                if k == 0 and b >= 2:
                    ve.wait_ge(s_pv, 16 * (b - 1))
                for t in (2 * k, 2 * k + 1):
                    dst = v1[b % 2][:, NH * 17 * t:NH * 17 * (t + 1)].rearrange("p (h d) -> p h d", d=17)
                    src = M1[:, H * (t % 2):H * (t % 2 + 1)].rearrange("p (h d) -> p h d", d=HD)
                    v.scalar_tensor_tensor(dst[:, :, 0:HD], src, 1.0 / WS,
                                           bvb.rearrange("p (h d) -> p h d", d=HD),
                                           ALU.mult, ALU.add).then_inc(s_v, 1)

            def modulation_columns():
                ve.wait_ge(s_mc, 1)
                ve.wait_ge(s_bias, 48)
                v.tensor_copy(sac[:, :, :], T2[:, 0:8].rearrange("p (k b) -> p k b", k=KC))
                v.tensor_scalar(cac[:, :, :], T2[:, 8:16].rearrange("p (k b) -> p k b", k=KC),
                                1.0, None, ALU.add)
                v.tensor_scalar(bqk[:, 0:2], bqk[:, 0:2], 0.25, None, ALU.mult).then_inc(s_col, 1)

            def low_qkv():
                ve.wait_ge(s_wh, 1)
                v.scalar_tensor_tensor(wq16[:, 1], wq_s, WS, wq16[:, 0], ALU.mult,
                                       ALU.subtract).then_inc(s_wl, 1)

            def low_others():
                ve.wait_ge(s_wh, 3)
                v.scalar_tensor_tensor(wo16[:, 1], wo_s, WS, wo16[:, 0], ALU.mult, ALU.subtract)
                v.scalar_tensor_tensor(rw16[:, 1], rw_s[:, :, :], WS, rw16[:, 0], ALU.mult,
                                       ALU.subtract).then_inc(s_wl, 1)

            def maxima(N):
                b, gr = N // BU, N % BU // UNITS
                t, i, m = QU[N % UNITS]
                w = P * (t + 1)
                par, hp0 = group_heads(gr)
                ve.wait_ge(s_s1, N + 1)
                if N % BU == 0 and b >= 2:
                    ve.wait_ge(s_mt, 2 * (b - 1))
                v.tensor_reduce(mx_v[:, b % 2, hp0 // 4, par, i:i + m, t],
                                SB[N % 3][:, 0:m * w].rearrange("p (i n) -> p i n", i=m),
                                AX.X, ALU.max).then_inc(s_mx, 1)

            def negate(b, f):
                ve.wait_ge(s_mt, 2 * b + f + 1)
                if b or f:
                    ve.wait_ge(s_ngw, 16 * (2 * b + f))
                link(v.tensor_scalar(negm[:, 0], M1[0:32, 0:P], -1.0, None, ALU.mult))
                v.scalar_tensor_tensor(negm[:, 1], M1[0:32, 0:P], -1.0, negm[:, 0], ALU.mult,
                                       ALU.subtract).then_inc(s_neg, 1)

            def normalise(G):
                b, gr = G // NG, G % NG
                ve.wait_ge(s_rt, G + 1)
                if b and gr == 0:
                    ve.wait_ge(s_at, KC * b)
                src = M0[:, :].rearrange("p (t i d) -> p t i d", t=TT, i=4)
                r = rec[:, G % 2, :].rearrange("p (t i) -> p t i", t=TT)
                link(v.reciprocal(r, src[:, :, :, HD]))
                par, hp0 = group_heads(gr)
                dst = an.rearrange("p t (h two d) -> p two t h d", two=2, d=HD)[:, par, :, hp0:hp0 + 4]
                v.tensor_tensor(dst, src[:, :, :, 0:HD], r.unsqueeze(3).to_broadcast([P, TT, 4, HD]),
                                ALU.mult).then_inc(s_nrm, 1)

            def attn_low(b, k):
                ve.wait_ge(s_ath, KC * b + k + 1)
                if b and k == 0:
                    ve.wait_ge(s_o, TT * b)
                v.tensor_tensor(aT[:, 1, k], side_bank("attn", b, k)[:, :], aT[:, 0, k],
                                ALU.subtract).then_inc(s_atl, 1)

            def residual(b, k):
                for t in (2 * k, 2 * k + 1):
                    n = TT * b + t
                    if t % 2 == 0:
                        ve.wait_ge(s_o, n + 2)
                    if t == 0:
                        ve.wait_ge(s_xb, b + 1)
                        if b:
                            ve.wait_ge(s_rl, TT * b)
                    link(v.scalar_tensor_tensor(o1[:, t], side_bank("out", b, k)[:, H * (t % 2):H * (t % 2 + 1)],
                                                1.0 / WS, bc[:, b % 2, 0:H], ALU.mult, ALU.mult))
                    v.tensor_tensor(x_sb[:, n], x_sb[:, n], o1[:, t], ALU.add).then_inc(s_x2, 1)

            def stats2(b):
                ve.wait_ge(s_x2, TT * (b + 1))
                for t in range(TT):
                    i = v.bn_stats(st2[:, TT * b + t], x_sb[:, TT * b + t])
                link(i)
                for t in range(TT):
                    i = v.bn_aggr(mv2[:, TT * b + t], st2[:, TT * b + t])
                i.then_inc(s_mv2, 1)

            def scale2(b, t):
                n = TT * b + t
                ve.wait_ge(s_mv2, b + 1)
                ve.wait_ge(s_rstd2, b + 1)
                v.tensor_scalar(h2f[:, t], x_sb[:, n], mv2[:, n, 0:1], rs2[:, n:n + 1],
                                ALU.subtract, ALU.mult).then_inc(s_hm, 1)

            def modulate2(b, t):
                ve.wait_ge(s_hm, TT * (b + 1))
                link(v.tensor_tensor(h2f[:, t], h2f[:, t], bc[:, b % 2, 2 * H:3 * H], ALU.mult))
                v.tensor_tensor(h2f[:, t], h2f[:, t], bc[:, b % 2, H:2 * H], ALU.add).then_inc(s_h2v, 1)

            def rows_low(b, t):
                n = TT * b + t
                ve.wait_ge(s_rh, n + 1)
                v.tensor_tensor(row[:, n, H:2 * H], h2f[:, t], row[:, n, 0:H], ALU.subtract).then_inc(s_rl, 1)

            def h2_low(b):
                ve.wait_ge(s_ht, 2 * b + 2)
                v.tensor_copy(h2T[:, 1, :, S * b:S * (b + 1)],
                              side_bank("h2", b, 1)[:, :].bitcast(F16).rearrange("p (k n) -> p k n", k=KC)
                              ).then_inc(s_htd, 1)

            def logits(b):
                ve.wait_ge(s_r, b + 1)
                v.tensor_scalar(lg[:, TT * b:TT * (b + 1), :],
                                side_bank("route", b, 0)[:, 0:TT * E].rearrange("p (t e) -> p t e", t=TT),
                                1.0 / WS, None, ALU.mult).then_inc(s_lg, 1)

            def split_low(n):
                if n in POOL_UNITS:
                    return
                ve.wait_ge(s_eh, n + 1)
                v.scalar_tensor_tensor(weights(n, 1), staged(n), WS, weights(n, 0), ALU.mult,
                                       ALU.subtract).then_inc(s_el, 1)

            def hidden(n):
                ve.wait_ge(s_silu, n + 1)
                ve.wait_ge(s_u, n + 1)
                if n >= 2:
                    ve.wait_ge(s_hh, n - 1)
                    ve.wait_ge(s_hl, n - 1)
                scale = 1.0 / WS
                if n < FC * DEEP:
                    scale = 0.5 / WS ** 2
                    link(v.scalar_tensor_tensor(g32[:, n % 2], g32[:, n % 2], 1.0, up_banks(n)[0][:, :],
                                                ALU.add, ALU.mult))
                v.scalar_tensor_tensor(hid[:, n % 2], up_banks(n)[1][:, :], scale, g32[:, n % 2],
                                       ALU.mult, ALU.mult).then_inc(s_hid, 1)

            def hidden_low(n):
                ve.wait_ge(s_hh, n + 1)
                ve.wait_ge(s_hid, n + 1)
                if n >= FC and n % FC == 0:
                    ve.wait_ge(s_y, TT * (n // FC))
                v.tensor_tensor(hT[:, 1, n % FC], hid[:, n % 2], hT[:, 0, n % FC], ALU.subtract).then_inc(s_hl, 1)

            def add_shared(n):
                ve.wait_ge(s_ye, n + 1)
                v.tensor_tensor(x_sb[:, n], x_sb[:, n], yo[:, n % 2], ALU.add).then_inc(s_x3, 1)

            def shared_out(b, half):
                for t in (2 * half, 2 * half + 1):
                    n = TT * b + t
                    if b < DEEP:
                        y = M1[:, H * (t % 2):H * (t % 2 + 1)]
                        ve.wait_ge(s_y, TT * b + 2 * half + 2)
                    else:
                        y = [T0, T1, T2, OTb][t][:, 0:H]
                        ve.wait_ge(s_y, n + 1)
                    if n == 0:
                        ve.wait_ge(s_gbb, 16)
                    if n >= 2:
                        ve.wait_ge(s_x3, n - 1)
                    v.scalar_tensor_tensor(yo[:, n % 2], y, 1.0 / WS, gbb[:, b],
                                           ALU.mult, ALU.mult).then_inc(s_ye, 1)
                for t in (2 * half, 2 * half + 1):
                    add_shared(TT * b + t)

            stats1(0)
            norm1(0)
            modulation_columns()
            low_qkv()
            v.memset(qs[0].rearrange("p h two n -> p (h two n)").bitcast(F32), 0.0)
            for r in range(2):
                for p0 in (32, 96):
                    i = v.memset(ks[r][p0:p0 + 32], 1.0)
                i.then_inc(s_zero, 1)
            for b in range(-1, B):
                for n in range(BU):
                    G = NG * b + n // UNITS
                    if b + 1 < B:
                        maxima(BU * (b + 1) + n)
                    if n % UNITS == 7 and G > 0:
                        normalise(G - 1)
                    if b < 0 and n == 22:
                        low_others()
                    for job, c, k in side_jobs(b, n):
                        if job == "max":
                            negate(c, k)
                        elif job == "v":
                            v_out(c, k)
                        elif job == "stats1":
                            stats1(c)
                        elif job == "norm1":
                            norm1(c)
                        elif job == "attn":
                            attn_low(c, k)
                        elif job == "out":
                            residual(c, k)
                        elif job == "stats2":
                            stats2(c)
                        elif job == "scale2":
                            scale2(c, k)
                        elif job == "parts2":
                            rows_low(c, k)
                        elif job == "h2" and k == 1:
                            h2_low(c)
                        elif job == "route":
                            logits(c)
                        elif job == "up":
                            hidden(FC * c + k)
                        elif job == "hidden":
                            hidden_low(FC * c + k)
                        elif job == "down":
                            shared_out(c, k)
                    if n % UNITS == (SPLIT_AT if b == B - 1 else 8):
                        for u in early_splits(b, n // UNITS):
                            split_low(u)
            normalise(NG * B - 1)

            def route():
                ve.wait_ge(s_lg, B)
                ve.wait_ge(s_const, 5)
                v.tensor_reduce(top[:, :], lg[:, :, :], AX.X, ALU.max).then_inc(s_top, 1)
                ve.wait_ge(s_top, 1)
                link(v.tensor_tensor(oh[:, :, :], lg[:, :, :], top[:, :].unsqueeze(2).to_broadcast([P, NT, E]),
                                     ALU.is_equal))
                link(v.tensor_tensor(ohw[:, :, :], oh[:, :, :], iw[:, :].unsqueeze(1).to_broadcast([P, NT, E]),
                                     ALU.mult))
                link(v.tensor_reduce(wtop[:, :], ohw[:, :, :], AX.X, ALU.max))
                link(v.tensor_tensor(oh[:, :, :], ohw[:, :, :], wtop[:, :].unsqueeze(2).to_broadcast([P, NT, E]),
                                     ALU.is_equal))
                v.tensor_copy(oh16[:, :, :], oh[:, :, :]).then_inc(s_oh, 1)

            def slots():
                ve.wait_ge(s_rank, 1)
                count = OTb[:, 0:E]
                rank = T2[:, 0:NT * E].rearrange("p (t e) -> p t e", t=NT)
                link(v.tensor_tensor(cmpc[:, :, :], count.unsqueeze(2).to_broadcast([P, E, NT]),
                                     ij[:, :].unsqueeze(1).to_broadcast([P, E, NT]), ALU.is_gt))
                link(v.tensor_reduce(ntile[:, :], cmpc[:, :, :], AX.X, ALU.add))
                link(v.tensor_tensor_scan(ends[:, :], onesE[:, :], ntile[:, :], 0.0, ALU.mult, ALU.add))
                link(v.tensor_tensor(base[:, :], ends[:, :], ntile[:, :], ALU.subtract))
                link(v.tensor_scalar(base[:, :], base[:, :], float(P), None, ALU.mult))
                link(v.tensor_tensor(posf[:, :, :], rank, base[:, :].unsqueeze(1).to_broadcast([P, NT, E]),
                                     ALU.add))
                link(v.tensor_tensor(posf[:, :, :], posf[:, :, :], oh[:, :, :], ALU.mult))
                link(v.tensor_reduce(posr[:, :], posf[:, :, :], AX.X, ALU.add))
                v.tensor_copy(pos_i[:, :], posr[:, :]).then_inc(s_pos, 1)
                link(v.tensor_tensor(tec[:, :, :], it[:, :].unsqueeze(2).to_broadcast([P, RT, E]),
                                     ends[:, :].unsqueeze(1).to_broadcast([P, RT, E]), ALU.is_ge))
                link(v.tensor_reduce(tef[:, :], tec[:, :, :], AX.X, ALU.add))
                link(v.tensor_scalar(teg[:, :], tef[:, :], E - NEAR + 0.5, float(GAP), ALU.is_lt, ALU.mult))
                link(v.tensor_scalar(tef[:, :], tef[:, :], -float(WX), float(E * WX), ALU.mult, ALU.add))
                v.tensor_tensor(te_i[:, :], tef[:, :], teg[:, :], ALU.add).then_inc(s_te, 1)
                ve.wait_ge(s_sg, 1)
                v.tensor_scalar(row32[:, :, 256], srow[:, :], 1.0 / WS, None, ALU.mult).then_inc(s_srow, 1)

            split = 9
            for n in range(FC * DEEP, NT):
                hidden(n)
                if n == 4:
                    attn_low(B - 1, 0)
                    attn_low(B - 1, 1)
                if n == 5:
                    residual(B - 1, 0)
                    residual(B - 1, 1)
                    stats2(B - 1)
                if n == 6:
                    for t in (2, 3, 0, 1):
                        scale2(B - 1, t)
                    for t in (0, 1):
                        modulate2(B - 1, t)
                if n == 9:
                    logits(B - 1)
                    route()
                    shared_out(1, 0)
                    slots()
                if n == 10:
                    shared_out(1, 1)
                if n == 13:
                    shared_out(2, 0)
                    shared_out(2, 1)
                if n > FC * DEEP:
                    hidden_low(n - 1)
                if n == 6:
                    for t in range(TT):
                        rows_low(B - 1, t)
                if n == 8:
                    h2_low(B - 1)
                for _ in range(ffn_splits(n)):
                    split_low(split)
                    split += 1
            hidden_low(NT - 1)

            def rows_in(r):
                ve.wait_ge(s_rxt, r + 1)
                if r >= 2:
                    ve.wait_ge(s_ru, r - 1)
                v.tensor_copy(xT[r % 2], T0[:, 0:256].bitcast(F16)).then_inc(s_rxe, 1)

            def routed_low(r):
                ve.wait_ge(s_rhh, r + 1)
                v.tensor_tensor(rhT[:, r % 2, 1].rearrange("p f n -> p (f n)"), T1[:, :],
                                rhT[:, r % 2, 0].rearrange("p f n -> p (f n)"), ALU.subtract).then_inc(s_rhl, 1)

            def routed_out(r):
                ve.wait_ge(s_ry, r + 1)
                ve.wait_ge(s_gbr[r % GR], 16 * (r // GR + 1))
                if r >= YR:
                    ve.wait_ge(s_add, 16 * (r - YR + 1))
                v.scalar_tensor_tensor(ry[r % YR], [T2, OTb][r % 2][:, 0:H], 1.0 / WS, gbr[r % GR],
                                       ALU.mult, ALU.mult).then_inc(s_rye, 1)

            rows_in(0)
            shared_out(B - 1, 0)
            shared_out(B - 1, 1)
            for r in range(RT + 1):
                if r:
                    routed_low(r - 1)
                if r + 1 < RT:
                    rows_in(r + 1)
                if r >= 2:
                    routed_out(r - 2)
                if r < RT:
                    ve.wait_ge(s_ru, r + 1)
                    ve.wait_ge(s_rsilu, r + 1)
                    if r >= 2:
                        ve.wait_ge(s_rht, r - 1)
                    v.scalar_tensor_tensor(hid[:, r % 2], [S1, M1][r % 2][:, :], row32[:, r % NT, 256:257],
                                           g32[:, r % 2], ALU.mult, ALU.mult).then_inc(s_rhid, 1)
            routed_out(RT - 1)

        @block.tensor
        def _(pe):
            t_ = nc.tensor

            def split_mm(outp, pairs, **kw):
                prods = [p for (ah, al, bh, bl) in pairs for p in ((ah, bh), (ah, bl), (al, bh))]
                for n, (l, r) in enumerate(prods):
                    i = t_.matmul(outp, l, r, start=(n == 0), stop=(n == len(prods) - 1), **kw)
                return i

            def modulation_columns():
                pe.wait_ge(s_sc, 1)
                pe.wait_ge(s_wm, 16)
                for c in range(4):
                    for k in range(KC):
                        i = t_.matmul(T2[:, 4 * c:4 * c + 4], wm[:, k, P * c:P * (c + 1)], cs[:, 1, k],
                                      start=(k == 0), stop=(k == KC - 1))
                i.then_inc(s_mc, 1)

            def modulation_rows():
                pe.wait_ge(s_wmr, 16)
                for c, bk in enumerate((T0, T1)):
                    for k in range(KC):
                        i = t_.matmul(bk[0:B, :], cs[:, 1, k], wm[:, k, 512 * (c + 1):512 * (c + 2)],
                                      start=(k == 0), stop=(k == KC - 1))
                i.then_inc(s_mp, 1)

            last_job = []

            def take_bank(job, c, k):
                if last_job:
                    pe.wait_ge(*released(*last_job[-1]))
                last_job.append((job, c, k))

            def turn(b, k):
                pe.wait_ge(s_xn, TT * (b + 1))
                for t in range(TT):
                    i = t_.transpose(side_bank("turn", b, k)[:, P * t:P * (t + 1)], xn[:, t, P * k:P * (k + 1)], ident[:, :])
                i.then_inc(s_xt, 1)

            def project_qk(b, u):
                pe.wait_ge(s_wl, 1)
                pe.wait_ge(s_h1l, KC * (b + 1))
                c = H * (u % 2) + P * (u // 2)
                split_mm(side_bank("qk", b, u)[:, :], [(wq16[:, 0, k, c:c + P], wq16[:, 1, k, c:c + P], h1[:, 0, k], h1[:, 1, k])
                                    for k in range(KC)]).then_inc(s_qkv, 1)

            def project_v(b, half):
                for t in (2 * half, 2 * half + 1):
                    sl = slice(P * t, P * (t + 1))
                    i = split_mm(M1[:, H * (t % 2):H * (t % 2 + 1)],
                                 [(h1[:, 0, k, sl], h1[:, 1, k, sl], wq16[:, 0, k, 2 * H:3 * H],
                                   wq16[:, 1, k, 2 * H:3 * H]) for k in range(KC)])
                i.then_inc(s_qkv, 1)

            def scores(N):
                b, gr = N // BU, N % BU // UNITS
                t, i0, m = QU[N % UNITS]
                r = b % 2
                par, hp0 = group_heads(gr)
                if N % (BU // 2) == 0:
                    pe.wait_ge(s_stk[r][gr // 2], 16 * 4 * (b // 2 + 1))
                if N == 0:
                    pe.wait_ge(s_const, 2)
                    pe.wait_ge(s_q32, 4)
                if N == 2:
                    pe.wait_ge(s_col, 1)
                if N >= 3:
                    pe.wait_ge(s_mx, N - 2)
                w = P * (t + 1)
                bk = SB[N % 3]
                for i in range(m):
                    hp = hp0 + i0 + i
                    t_.matmul(bk[:, w * i:w * (i + 1)], qs[r][0:P - 2, hp, par, P * t:w],
                              ks[r][0:P - 2, hp, 0:w], start=(i == 0), stop=False, skip_group_check=True)
                t_.matmul(bk[:, 0:m * w].rearrange("p (i n) -> p i n", i=m)[:, :, w - P:w], identb[:, :],
                          maskb[:, :].unsqueeze(1).to_broadcast([P, m, P]), start=False, stop=True,
                          skip_group_check=True).then_inc(s_s1, 1)

            def max_turn(b, f):
                pe.wait_ge(s_mx, BU * b + BU // 2 * (f + 1))
                t_.transpose(M1[0:32, 0:P], mx[:, b % 2, f], ident[:, :]).then_inc(s_mt, 1)

            def scores_t(N):
                b, gr = N // BU, N % BU // UNITS
                j, i0, m = KU[N % UNITS]
                r = b % 2
                par, hp0 = group_heads(gr)
                if N % (BU // 2) == 0:
                    pe.wait_ge(s_ng[r][gr // 2], 16 * 2 * (b // 2 + 1))
                if N == 0:
                    pe.wait_ge(s_mr, 2)
                before = [n for n in range(max(N - 3, 0), N) if t_bank(n) is t_bank(N)]
                if before:
                    pe.wait_ge(s_exp, before[-1] + 1)
                if t_bank(N) is T2:
                    pe.wait_ge(s_mx, BU * B)
                w = S - P * j
                for i in range(m):
                    hp = hp0 + i0 + i
                    q = t_.matmul(t_bank(N)[:, w * i:w * (i + 1)], ks[r][:, hp, P * j:P * (j + 1)],
                                  qs[r][:, hp, par, P * j:S], start=True, stop=True)
                q.then_inc(s_st, 1)

            def values(G, j):
                b, gr = G // NG, G % NG
                if gr == 0 and j == 0:
                    pe.wait_ge(s_v, TT * (b + 1))
                if j == 0 and G:
                    pe.wait_ge(s_ote, G)
                pe.wait_ge(s_msk, 4 * G + j + 1)
                par, hp0 = group_heads(gr)
                for i in range(4):
                    h = 2 * (hp0 + i) + par
                    c = 17 * (NH * j + h)
                    q = t_.matmul(OTb[32 * i:32 * i + 32, P * j:S], v1[b % 2][:, c:c + 32], PT[j][:, i],
                                  start=(j == 0), stop=(j == TT - 1), tile_position=(0, 32 * i),
                                  skip_group_check=True)
                q.then_inc(s_pv, 1)

            def turn_out(G):
                pe.wait_ge(s_ote, G + 1)
                if G:
                    pe.wait_ge(s_nrm, G)
                for t in range(TT):
                    q = t_.transpose(M0[:, P * t:P * (t + 1)], OTs[:, G % 2, P * t:P * (t + 1)], ident[:, :])
                q.then_inc(s_rt, 1)

            def attn_turn(b, k):
                pe.wait_ge(s_nrm, NG * (b + 1))
                if b == B - 1:
                    pe.wait_ge(s_exp, BU * B)
                for t in range(TT):
                    q = t_.transpose(side_bank("attn", b, k)[:, P * t:P * (t + 1)],
                                     an[:, t, P * k:P * (k + 1)], ident[:, :])
                q.then_inc(s_at, 1)

            def output(b, half):
                pe.wait_ge(s_atl, KC * (b + 1))
                if b == 0:
                    pe.wait_ge(s_wl, 2)
                for t in (2 * half, 2 * half + 1):
                    sl = slice(P * t, P * (t + 1))
                    split_mm(side_bank("out", b, half)[:, H * (t % 2):H * (t % 2 + 1)],
                             [(aT[:, 0, k, sl], aT[:, 1, k, sl], wo16[:, 0, k], wo16[:, 1, k])
                              for k in range(KC)]).then_inc(s_o, 1)

            def h2_turn(b, part):
                pe.wait_ge(s_rl, TT * (b + 1))
                o = side_bank("h2", b, part)[:, :].bitcast(F16)
                for k in range(KC):
                    for t in range(TT):
                        q = t_.transpose(o[:, S * k + P * t:S * k + P * (t + 1)],
                                         row[:, TT * b + t, H * part + P * k:H * part + P * (k + 1)],
                                         ident16[:, :])
                q.then_inc(s_ht, 1)

            def router(b):
                pe.wait_ge(s_hta, b + 1)
                pe.wait_ge(s_htd, b + 1)
                for t in range(TT):
                    sl = slice(S * b + P * t, S * b + P * (t + 1))
                    q = split_mm(side_bank("route", b, 0)[:, E * t:E * (t + 1)],
                                 [(h2T[:, 0, k, sl], h2T[:, 1, k, sl], rw16[:, 0, k], rw16[:, 1, k])
                                  for k in range(KC)])
                q.then_inc(s_r, 1)

            def we(e, part, k_or_f, lo, n, is_down=False):
                c = place(e) + part * WE + (KC * 2 * I + H * k_or_f if is_down else 2 * I * k_or_f) + lo
                return W[:, c:c + n]

            def shared_up(n):
                b, f = n // FC, n % FC
                tok = slice(S * b, S * (b + 1))
                gk, uk = up_banks(n)
                if n == 0:
                    pe.wait_ge(*split_done(2))
                    pe.wait_ge(s_mx, BU * B)
                elif n <= FC * DEEP:
                    pe.wait_ge(s_hid, n)
                else:
                    pe.wait_ge(s_hid, n - 1)
                if n == FC * DEEP + 1:
                    pe.wait_ge(s_nrm, NG * B)
                    pe.wait_ge(*released(*last_job[-1]))
                for half, bk, s in ((0, gk, s_g), (I, uk, s_u)):
                    split_mm(bk[:, :], [(we(E, 0, k, half + P * f, P), we(E, 1, k, half + P * f, P),
                                         h2T[:, 0, k, tok], h2T[:, 1, k, tok])
                                        for k in range(KC)]).then_inc(s, 1)

            def shared_down(b, half):
                pe.wait_ge(s_hl, FC * (b + 1))
                for t in (2 * half, 2 * half + 1):
                    if b < DEEP:
                        y = M1[:, H * (t % 2):H * (t % 2 + 1)]
                    else:
                        y = [T0, T1, T2, OTb][t][:, 0:H]
                    if b > DEEP:
                        pe.wait_ge(s_ye, TT * (b - 1) + t + 1)
                    if b == DEEP and t == 0:
                        pe.wait_ge(s_htd, B)
                        pe.wait_ge(s_hta, B)
                    if b == DEEP and t == 2:
                        pe.wait_ge(s_pos, 1)
                    if b == B - 1 and t == 0:
                        pe.wait_ge(s_rxe, 1)
                    sl = slice(P * t, P * (t + 1))
                    split_mm(y, [(hT[:, 0, f, sl], hT[:, 1, f, sl], we(E, 0, f, 0, H, True),
                                  we(E, 1, f, 0, H, True)) for f in range(FC)]).then_inc(s_y, 1)

            pe.wait_ge(s_const, 1)
            modulation_columns()
            for k in range(KC):
                turn(0, k)
            pe.wait_ge(s_h32, KC)
            for u in range(4):
                project_qk(0, u)
            last_job.append(("qk", 0, 0))
            modulation_rows()
            for b in range(-1, B):
                for n in range(BU):
                    G = NG * b + n // UNITS
                    if b >= 0:
                        scores_t(BU * b + n)
                    if b + 1 < B:
                        scores(BU * (b + 1) + n)
                    if n % UNITS == 1 and G > 0:
                        values(G - 1, 2)
                    if n % UNITS == 3 and G > 0:
                        values(G - 1, 3)
                    if n % UNITS == 6 and G > 0:
                        turn_out(G - 1)
                    if n % UNITS == 8 and b >= 0:
                        values(G, 0)
                    if n % UNITS == 10 and b >= 0:
                        values(G, 1)
                    for job, c, k in side_jobs(b, n):
                        if job in ("max", "v", "attn", "turn", "out", "qk", "h2", "route", "down"):
                            take_bank(job, c, k)
                        if job == "max":
                            max_turn(c, k)
                        elif job == "v":
                            project_v(c, k)
                        elif job == "attn":
                            attn_turn(c, k)
                        elif job == "turn":
                            turn(c, k)
                        elif job == "out":
                            output(c, k)
                        elif job == "qk":
                            project_qk(c, k)
                        elif job == "h2":
                            h2_turn(c, k)
                        elif job == "route":
                            router(c)
                        elif job == "up":
                            shared_up(FC * c + k)
                        elif job == "down":
                            shared_down(c, k)
            values(NG * B - 1, 2)
            values(NG * B - 1, 3)
            turn_out(NG * B - 1)

            def ranks():
                pe.wait_ge(s_oh, 1)
                pe.wait_ge(s_lg, B)
                rank = T2[:, 0:NT * E]
                t_.matmul(rank, tri16[:, :], oh16[:, :, :].rearrange("p t e -> p (t e)"), start=True,
                          stop=False, skip_group_check=True)
                for t in range(NT - 1):
                    m = NT - 1 - t
                    t_.matmul(rank[:, E * (t + 1):].rearrange("p (t e) -> p t e", t=m), ones16[:, :],
                              oh16[:, t:t + 1, :].to_broadcast([P, m, E]), start=False, stop=(t == NT - 2),
                              skip_group_check=True)
                for t in range(NT):
                    q = t_.matmul(OTb[:, 0:E], ones16[:, :], oh16[:, t], start=(t == 0), stop=(t == NT - 1))
                q.then_inc(s_rank, 1)

            for n in range(FC * DEEP, NT):
                shared_up(n)
                if n == 4:
                    attn_turn(B - 1, 0)
                    attn_turn(B - 1, 1)
                if n == 5:
                    output(B - 1, 0)
                    output(B - 1, 1)
                if n == 8:
                    pe.wait_ge(s_x2, TT * B)
                    h2_turn(B - 1, 0)
                    h2_turn(B - 1, 1)
                if n == 9:
                    router(B - 1)
                    shared_down(1, 0)
                    ranks()
                if n == 10:
                    shared_down(1, 1)
                if n == 13:
                    shared_down(2, 0)
                    shared_down(2, 1)

            def rows_turn(r):
                pe.wait_ge(s_ld[r % NT], 16 * (r // NT + 1))
                if r:
                    pe.wait_ge(s_rxe, r)
                if r < 2:
                    pe.wait_ge(s_ye, (TT * (B - 2) if r == 0 else TT * (B - 1)) + 1)
                o = T0[:, 0:256].bitcast(F16)
                for c in range(4):
                    q = t_.transpose(o[:, P * c:P * (c + 1)], row[:, r % NT, P * c:P * (c + 1)], ident16[:, :])
                q.then_inc(s_rxt, 1)

            def up_half(r, off, half, bk, s):
                pairs = []
                for k in range(KC):
                    c = 2 * I * k + half
                    pairs.append((xT[r % 2][:, P * k:P * (k + 1)], xT[r % 2][:, H + P * k:H + P * (k + 1)],
                                  W[:, bass.ds(off + c, I)], W[:, bass.ds(off + (c + WE), I)]))
                split_mm(bk[:, :], pairs).then_inc(s, 1)

            def hidden_turn(r):
                pe.wait_ge(s_rhid, r + 1)
                if r:
                    pe.wait_ge(s_rhl, r)
                else:
                    pe.wait_ge(s_ye, NT)
                for f in range(FC):
                    q = t_.transpose(T1[:, P * f:P * (f + 1)], hid[:, r % 2, P * f:P * (f + 1)], ident[:, :])
                q.then_inc(s_rht, 1)

            def down_rows(r, off):
                pe.wait_ge(s_rhl, r + 1)
                if r >= 2:
                    pe.wait_ge(s_rye, r - 1)
                pairs = []
                for f in range(FC):
                    c = KC * 2 * I + H * f
                    pairs.append((rhT[:, r % 2, 0, f], rhT[:, r % 2, 1, f],
                                  W[:, bass.ds(off + c, H)], W[:, bass.ds(off + (c + WE), H)]))
                split_mm([T2, OTb][r % 2][:, 0:H], pairs).then_inc(s_ry, 1)

            rows_turn(0)
            pe.wait_ge(s_te, 1)
            pe.wait_ge(s_el, NU - len(POOL_UNITS))
            pe.wait_ge(s_elp, len(POOL_UNITS))
            offs = {}
            for r in range(RT + 1):
                if r:
                    hidden_turn(r - 1)
                if r < RT:
                    offs[r] = t_.value_load(te_i[0:1, r:r + 1], min_val=0, max_val=E * WX + GAP)
                    pe.wait_ge(s_rxe, r + 1)
                    if r >= 2:
                        pe.wait_ge(s_rhid, r - 1)
                    elif r == 0:
                        pe.wait_ge(s_hid, NT)
                    gk, uk = (S0, S1) if r % 2 == 0 else (M0, M1)
                    up_half(r, offs[r], 0, gk, s_rg)
                    if r == 0:
                        shared_down(B - 1, 0)
                        shared_down(B - 1, 1)
                    if r + 1 < RT:
                        rows_turn(r + 1)
                    up_half(r, offs[r], I, uk, s_ru)
                if r:
                    down_rows(r - 1, offs[r - 1])


_INS = ["x", "wqkvT", "bqkv", "bqkc", "woutT", "bout", "rwT", "gup", "down", "sgw", "suw", "sdw", "cT", "wmod"]


def kernel(L0_attn_x, L0_attn_Wqkv, L0_attn_bqkv, L0_attn_Wout, L0_attn_bout, L0_ffn_router_w,
           L0_ffn_gate_up_proj, L0_ffn_down_proj, L0_ffn_shared_gate_w, L0_ffn_shared_up_w,
           L0_ffn_shared_down_w, L0_c, L0_wmod):
    import concourse.bacc as bacc
    from concourse.bass_utils import run_bass_kernel_spmd

    given = dict(x=L0_attn_x, wqkvT=np.asarray(L0_attn_Wqkv).T, bqkv=L0_attn_bqkv,
                 bqkc=np.asarray(L0_attn_bqkv)[:2 * H].reshape(4, P).T,
                 woutT=np.asarray(L0_attn_Wout).T, bout=L0_attn_bout,
                 rwT=np.asarray(L0_ffn_router_w).T, gup=L0_ffn_gate_up_proj, down=L0_ffn_down_proj,
                 sgw=L0_ffn_shared_gate_w, suw=L0_ffn_shared_up_w, sdw=L0_ffn_shared_down_w,
                 cT=np.asarray(L0_c).T, wmod=L0_wmod)
    nc = bacc.Bacc("TRN2", target_bir_lowering=False, num_devices=1)
    arrays, args = {}, []
    for name in _INS:
        a = np.ascontiguousarray(given[name])
        arrays["in_" + name] = a
        args.append(nc.dram_tensor("in_" + name, a.shape, mybir.dt.from_np(a.dtype), kind="ExternalInput").ap())
    args.append(nc.dram_tensor("out_0", (B, S, H), F32, kind="ExternalOutput").ap())
    build(nc, *args)
    r = run_bass_kernel_spmd(nc, [arrays], core_ids=[0])
    return r.results[0]["out_0"]
```
